# Optimizing a Trainium2 kernel written in Bass

```python
import numpy as np
import jax
import jax.numpy as jnp

def _softmax(x, axis=-1):
    return jax.nn.softmax(x, axis=axis)

def _gelu(x):
    return jax.nn.gelu(x, approximate=True)

def _silu(x):
    return jax.nn.silu(x)

def _sigmoid(x):
    return jax.nn.sigmoid(x)

def _layernorm(x, axis=-1, eps=1e-05):
    m = jnp.mean(x, axis=axis, keepdims=True)
    v = jnp.var(x, axis=axis, keepdims=True)
    return (x - m) / jnp.sqrt(v + eps)

def _scatter_add(tgt, idx, src, axis=0):
    return tgt.at[idx].add(src)

def _segment_sum(src, seg, n):
    return jax.ops.segment_sum(src, seg, n)
kernel_name = 'mk_prb_d2_jaxref_r8_d96c57'

def setup_inputs(seed: int=0):
    np.random.seed(seed)
    _w = jnp.asarray

    def _L0_attn_setup():
        import math
        import jax, jax.numpy as jnp
        import numpy as np
        D = 128
        NH = 16
        DH = D // NH

        def _rope(q, k, base=10000.0):
            half = q.shape[-1] // 2
            freqs = jnp.arange(half, dtype=q.dtype) / half
            theta = 1.0 / base ** freqs
            t = jnp.arange(q.shape[-2], dtype=q.dtype)
            ang = t[:, None] * theta[None, :]
            cos = jnp.cos(ang)[None, None, :, :]
            sin = jnp.sin(ang)[None, None, :, :]

            def rot(x):
                x1, x2 = (x[..., :half], x[..., half:])
                return jnp.concatenate([x1 * cos - x2 * sin, x1 * sin + x2 * cos], axis=-1)
            return (rot(q), rot(k))
        key = jax.random.key(seed)
        k1, k2, k3 = jax.random.split(key, 3)
        x = jax.random.normal(k1, (2, 256, D), dtype=jnp.float32)
        s = 1.0 / math.sqrt(D)
        W_qkv = jax.random.normal(k2, (D, 3 * D), dtype=jnp.float32) * s
        W_o = jax.random.normal(k3, (D, D), dtype=jnp.float32) * s
        return {'x': x, 'W_qkv': W_qkv, 'W_o': W_o}
    _L0_attn_in = _L0_attn_setup()

    def _L0_ffn_setup():
        import jax, jax.numpy as jnp
        import numpy as np
        DIM = 128
        DEPTH = 2
        HEADS = 8
        DIM_HEAD = 64
        WINDOW = 64
        INNER = HEADS * DIM_HEAD
        HID = int(DIM * 4 * 2 / 3)
        B, N = (2, 1024)
        QK_SCALE = 8.0

        def shift_token(t):
            t1, t2 = jnp.split(t, 2, axis=-1)
            t2 = jnp.pad(t2, ((0, 0), (1, 0), (0, 0)))[:, :-1]
            return jnp.concatenate([t1, t2], axis=-1)

        def l2norm(t):
            return t / jnp.clip(jnp.linalg.norm(t, axis=-1, keepdims=True), 1e-12)

        def rotate_half(x):
            x1, x2 = jnp.split(x, 2, axis=-1)
            return jnp.concatenate([-x2, x1], axis=-1)

        def rotary_xpos(q, k):
            n = q.shape[-2]
            half_idx = jnp.arange(0, DIM_HEAD, 2, dtype=jnp.float32)
            inv_freq = 1.0 / 10000.0 ** (half_idx / DIM_HEAD)
            t = jnp.arange(n, dtype=jnp.float32)
            freqs = t[:, None] * inv_freq[None, :]
            freqs = jnp.concatenate([freqs, freqs], axis=-1)
            base = (half_idx + 0.4 * DIM_HEAD) / (1.4 * DIM_HEAD)
            power = (t - n // 2) / float(WINDOW // 2)
            scale = base[None, :] ** power[:, None]
            scale = jnp.concatenate([scale, scale], axis=-1)
            cos, sin = (jnp.cos(freqs), jnp.sin(freqs))
            q = q * cos * scale + rotate_half(q) * sin * scale
            k = k * cos / scale + rotate_half(k) * sin / scale
            return (q, k)

        def local_attention(q, k, v):
            b, h, n, d = q.shape
            w = n // WINDOW
            bq = q.reshape(b, h, w, WINDOW, d) * QK_SCALE
            bk = k.reshape(b, h, w, WINDOW, d)
            bv = v.reshape(b, h, w, WINDOW, d)

            def look_around(t):
                p = jnp.pad(t, ((0, 0), (0, 0), (1, 0), (0, 0), (0, 0)))
                return jnp.concatenate([p[:, :, :w], p[:, :, 1:]], axis=3)
            bk, bv = (look_around(bk), look_around(bv))
            bt = jnp.arange(n).reshape(w, WINDOW)
            btp = jnp.pad(bt, ((1, 0), (0, 0)), constant_values=-1)
            btk = jnp.concatenate([btp[:w], btp[1:]], axis=1)
            sim = jnp.einsum('bhwid,bhwjd->bhwij', bq, bk)
            i = bt[:, :, None]
            j = btk[:, None, :]
            mask = (i < j) | (i > j + WINDOW) | (j == -1)
            sim = jnp.where(mask, -jnp.finfo(sim.dtype).max, sim)
            attn = jax.nn.softmax(sim, axis=-1)
            out = jnp.einsum('bhwij,bhwjd->bhwid', attn, bv)
            return out.reshape(b, h, n, d)

        def _layer(x, wqkv, qs, ksc, wo, lg, lb, w1, b1, w2, b2):
            b, n, _ = x.shape
            h = shift_token(x)
            qkv = h @ wqkv
            q, k, v = jnp.split(qkv, 3, axis=-1)
            to_heads = lambda t: t.reshape(b, n, HEADS, DIM_HEAD).transpose(0, 2, 1, 3)
            q, k, v = (to_heads(q), to_heads(k), to_heads(v))
            q = l2norm(q) * qs
            k = l2norm(k) * ksc
            q, k = rotary_xpos(q, k)
            o = local_attention(q, k, v)
            o = o.transpose(0, 2, 1, 3).reshape(b, n, INNER)
            x = x + o @ wo
            h = shift_token(x)
            mu = h.mean(-1, keepdims=True)
            var = h.var(-1, keepdims=True)
            h = (h - mu) / jnp.sqrt(var + 1e-05) * lg + lb
            h = h @ w1 + b1
            a, g = jnp.split(h, 2, axis=-1)
            h = a * jax.nn.gelu(g, approximate=False)
            x = x + h @ w2 + b2
            return x
        key = jax.random.key(seed)
        ks = jax.random.split(key, 6)
        return {'x': jax.random.normal(ks[0], (B, N, DIM), jnp.float32), 'wqkv': jax.random.normal(ks[1], (DEPTH, DIM, 3 * INNER), jnp.float32) * 0.02, 'q_scale': jnp.ones((DEPTH, DIM_HEAD), jnp.float32), 'k_scale': jnp.ones((DEPTH, DIM_HEAD), jnp.float32), 'wo': jax.random.normal(ks[2], (DEPTH, INNER, DIM), jnp.float32) * 0.02, 'ln_g': jnp.ones((DEPTH, DIM), jnp.float32), 'ln_b': jnp.zeros((DEPTH, DIM), jnp.float32), 'w1': jax.random.normal(ks[3], (DEPTH, DIM, 2 * HID), jnp.float32) * 0.02, 'b1': jnp.zeros((DEPTH, 2 * HID), jnp.float32), 'w2': jax.random.normal(ks[4], (DEPTH, HID, DIM), jnp.float32) * 0.02, 'b2': jnp.zeros((DEPTH, DIM), jnp.float32)}
    _L0_ffn_in = _L0_ffn_setup()

    def _L1_attn_setup():
        import jax, jax.numpy as jnp
        import numpy as np
        D_MODEL = 128
        N_HEADS = 16
        DH = D_MODEL // N_HEADS
        B, T = (4, 256)
        ROPE_BASE = 10000.0
        EPS = 1e-06

        def _rope(q, k, base=ROPE_BASE):
            half = q.shape[-1] // 2
            freqs = jnp.arange(half, dtype=q.dtype)
            inv_freq = base ** (-freqs / half)
            pos = jnp.arange(q.shape[2], dtype=q.dtype)
            ang = pos[:, None] * inv_freq[None, :]
            c = jnp.cos(ang)[None, None]
            s = jnp.sin(ang)[None, None]

            def rot(x):
                x1 = x[..., :half]
                x2 = x[..., half:2 * half]
                return jnp.concatenate([x1 * c - x2 * s, x1 * s + x2 * c], axis=-1)
            return (rot(q), rot(k))

        def _phi(x):
            return jax.nn.elu(x) + 1.0

        def _forward(x, Wq, Wk, Wv, Wo):
            Bx, Tx, D = x.shape
            H, dh = (N_HEADS, D // N_HEADS)
            q = (x @ Wq.T).reshape(Bx, Tx, H, dh).transpose(0, 2, 1, 3)
            k = (x @ Wk.T).reshape(Bx, Tx, H, dh).transpose(0, 2, 1, 3)
            v = (x @ Wv.T).reshape(Bx, Tx, H, dh).transpose(0, 2, 1, 3)
            q, k = _rope(q, k)
            q = _phi(q)
            k = _phi(k)
            qT = q.transpose(2, 0, 1, 3)
            kT = k.transpose(2, 0, 1, 3)
            vT = v.transpose(2, 0, 1, 3)

            def step(carry, qkv):
                K_sum, KV = carry
                q_t, k_t, v_t = qkv
                K_sum = K_sum + k_t
                KV = KV + k_t[..., :, None] * v_t[..., None, :]
                num = jnp.einsum('bhd,bhde->bhe', q_t, KV)
                den = jnp.maximum(jnp.einsum('bhd,bhd->bh', q_t, K_sum), EPS)
                return ((K_sum, KV), num / den[..., None])
            init = (jnp.zeros((Bx, H, dh), x.dtype), jnp.zeros((Bx, H, dh, dh), x.dtype))
            _, Y = jax.lax.scan(step, init, (qT, kT, vT))
            Y = Y.transpose(1, 0, 2, 3).reshape(Bx, Tx, D)
            return Y @ Wo.T
        key = jax.random.key(seed)
        kx, kq, kk, kv, ko = jax.random.split(key, 5)
        scale = 0.02
        return {'x': jax.random.normal(kx, (B, T, D_MODEL), jnp.float32), 'Wq': jax.random.normal(kq, (D_MODEL, D_MODEL), jnp.float32) * scale, 'Wk': jax.random.normal(kk, (D_MODEL, D_MODEL), jnp.float32) * scale, 'Wv': jax.random.normal(kv, (D_MODEL, D_MODEL), jnp.float32) * scale, 'Wo': jax.random.normal(ko, (D_MODEL, D_MODEL), jnp.float32) * scale}
    _L1_attn_in = _L1_attn_setup()

    def _L1_ffn_setup():
        import jax, jax.numpy as jnp
        import numpy as np
        NUM_EXPERTS = 8
        TOP_K = 2
        D = 128
        H = 4 * D
        B, S = (4, 256)
        key = jax.random.key(seed)
        ks = jax.random.split(key, 8)
        s = 0.02
        return {'x': jax.random.normal(ks[0], (B, S, D), dtype=jnp.float32), 'gate_w': jax.random.normal(ks[1], (NUM_EXPERTS, D), dtype=jnp.float32) * s, 'gate_b': jnp.zeros((NUM_EXPERTS,), dtype=jnp.float32), 'w1': jax.random.normal(ks[2], (NUM_EXPERTS, D, H), dtype=jnp.float32) * s, 'b1': jnp.zeros((NUM_EXPERTS, H), dtype=jnp.float32), 'w2': jax.random.normal(ks[3], (NUM_EXPERTS, H, D), dtype=jnp.float32) * s, 'b2': jnp.zeros((NUM_EXPERTS, D), dtype=jnp.float32)}
    _L1_ffn_in = _L1_ffn_setup()
    _d = {'L0_attn_x': _L0_attn_in['x'], 'L0_attn_W_qkv': _L0_attn_in['W_qkv'], 'L0_attn_W_o': _L0_attn_in['W_o'], 'L0_ffn_wqkv': _L0_ffn_in['wqkv'], 'L0_ffn_q_scale': _L0_ffn_in['q_scale'], 'L0_ffn_k_scale': _L0_ffn_in['k_scale'], 'L0_ffn_wo': _L0_ffn_in['wo'], 'L0_ffn_ln_g': _L0_ffn_in['ln_g'], 'L0_ffn_ln_b': _L0_ffn_in['ln_b'], 'L0_ffn_w1': _L0_ffn_in['w1'], 'L0_ffn_b1': _L0_ffn_in['b1'], 'L0_ffn_w2': _L0_ffn_in['w2'], 'L0_ffn_b2': _L0_ffn_in['b2'], 'L1_attn_Wq': _L1_attn_in['Wq'], 'L1_attn_Wk': _L1_attn_in['Wk'], 'L1_attn_Wv': _L1_attn_in['Wv'], 'L1_attn_Wo': _L1_attn_in['Wo'], 'L1_ffn_gate_w': _L1_ffn_in['gate_w'], 'L1_ffn_gate_b': _L1_ffn_in['gate_b'], 'L1_ffn_w1': _L1_ffn_in['w1'], 'L1_ffn_b1': _L1_ffn_in['b1'], 'L1_ffn_w2': _L1_ffn_in['w2'], 'L1_ffn_b2': _L1_ffn_in['b2']}
    _x0 = _d['L0_attn_x']
    _d['L0_attn_x'] = jax.random.normal(jax.random.fold_in(jax.random.key(seed), 1), (4, 1024, 128), dtype=_x0.dtype)
    del _x0
    return _d

def reference(L0_attn_x, L0_attn_W_qkv, L0_attn_W_o, L0_ffn_wqkv, L0_ffn_q_scale, L0_ffn_k_scale, L0_ffn_wo, L0_ffn_ln_g, L0_ffn_ln_b, L0_ffn_w1, L0_ffn_b1, L0_ffn_w2, L0_ffn_b2, L1_attn_Wq, L1_attn_Wk, L1_attn_Wv, L1_attn_Wo, L1_ffn_gate_w, L1_ffn_gate_b, L1_ffn_w1, L1_ffn_b1, L1_ffn_w2, L1_ffn_b2):

    def _L0_attn_ref(x, W_qkv, W_o):
        import math
        import jax, jax.numpy as jnp
        import numpy as np
        D = 128
        NH = 16
        DH = D // NH

        def _rope(q, k, base=10000.0):
            half = q.shape[-1] // 2
            freqs = jnp.arange(half, dtype=q.dtype) / half
            theta = 1.0 / base ** freqs
            t = jnp.arange(q.shape[-2], dtype=q.dtype)
            ang = t[:, None] * theta[None, :]
            cos = jnp.cos(ang)[None, None, :, :]
            sin = jnp.sin(ang)[None, None, :, :]

            def rot(x):
                x1, x2 = (x[..., :half], x[..., half:])
                return jnp.concatenate([x1 * cos - x2 * sin, x1 * sin + x2 * cos], axis=-1)
            return (rot(q), rot(k))
        B, T, d = x.shape
        qkv = x @ W_qkv
        q, k, v = jnp.split(qkv, 3, axis=-1)
        q = q.reshape(B, T, NH, DH).transpose(0, 2, 1, 3)
        k = k.reshape(B, T, NH, DH).transpose(0, 2, 1, 3)
        v = v.reshape(B, T, NH, DH).transpose(0, 2, 1, 3)
        q, k = _rope(q, k)
        att = jnp.einsum('bhtd,bhsd->bhts', q, k) / math.sqrt(DH)
        mask = jnp.triu(jnp.full((T, T), -jnp.inf, dtype=att.dtype), 1)
        att = att + mask
        w = jax.nn.softmax(att, axis=-1)
        y = jnp.einsum('bhts,bhsd->bhtd', w, v)
        y = y.transpose(0, 2, 1, 3).reshape(B, T, d)
        return y @ W_o

    def _L0_ffn_ref(x, wqkv, q_scale, k_scale, wo, ln_g, ln_b, w1, b1, w2, b2):
        import jax, jax.numpy as jnp
        import numpy as np
        DIM = 128
        DEPTH = 2
        HEADS = 8
        DIM_HEAD = 64
        WINDOW = 64
        INNER = HEADS * DIM_HEAD
        HID = int(DIM * 4 * 2 / 3)
        B, N = (2, 1024)
        QK_SCALE = 8.0

        def shift_token(t):
            t1, t2 = jnp.split(t, 2, axis=-1)
            t2 = jnp.pad(t2, ((0, 0), (1, 0), (0, 0)))[:, :-1]
            return jnp.concatenate([t1, t2], axis=-1)

        def l2norm(t):
            return t / jnp.clip(jnp.linalg.norm(t, axis=-1, keepdims=True), 1e-12)

        def rotate_half(x):
            x1, x2 = jnp.split(x, 2, axis=-1)
            return jnp.concatenate([-x2, x1], axis=-1)

        def rotary_xpos(q, k):
            n = q.shape[-2]
            half_idx = jnp.arange(0, DIM_HEAD, 2, dtype=jnp.float32)
            inv_freq = 1.0 / 10000.0 ** (half_idx / DIM_HEAD)
            t = jnp.arange(n, dtype=jnp.float32)
            freqs = t[:, None] * inv_freq[None, :]
            freqs = jnp.concatenate([freqs, freqs], axis=-1)
            base = (half_idx + 0.4 * DIM_HEAD) / (1.4 * DIM_HEAD)
            power = (t - n // 2) / float(WINDOW // 2)
            scale = base[None, :] ** power[:, None]
            scale = jnp.concatenate([scale, scale], axis=-1)
            cos, sin = (jnp.cos(freqs), jnp.sin(freqs))
            q = q * cos * scale + rotate_half(q) * sin * scale
            k = k * cos / scale + rotate_half(k) * sin / scale
            return (q, k)

        def local_attention(q, k, v):
            b, h, n, d = q.shape
            w = n // WINDOW
            bq = q.reshape(b, h, w, WINDOW, d) * QK_SCALE
            bk = k.reshape(b, h, w, WINDOW, d)
            bv = v.reshape(b, h, w, WINDOW, d)

            def look_around(t):
                p = jnp.pad(t, ((0, 0), (0, 0), (1, 0), (0, 0), (0, 0)))
                return jnp.concatenate([p[:, :, :w], p[:, :, 1:]], axis=3)
            bk, bv = (look_around(bk), look_around(bv))
            bt = jnp.arange(n).reshape(w, WINDOW)
            btp = jnp.pad(bt, ((1, 0), (0, 0)), constant_values=-1)
            btk = jnp.concatenate([btp[:w], btp[1:]], axis=1)
            sim = jnp.einsum('bhwid,bhwjd->bhwij', bq, bk)
            i = bt[:, :, None]
            j = btk[:, None, :]
            mask = (i < j) | (i > j + WINDOW) | (j == -1)
            sim = jnp.where(mask, -jnp.finfo(sim.dtype).max, sim)
            attn = jax.nn.softmax(sim, axis=-1)
            out = jnp.einsum('bhwij,bhwjd->bhwid', attn, bv)
            return out.reshape(b, h, n, d)

        def _layer(x, wqkv, qs, ksc, wo, lg, lb, w1, b1, w2, b2):
            b, n, _ = x.shape
            h = shift_token(x)
            qkv = h @ wqkv
            q, k, v = jnp.split(qkv, 3, axis=-1)
            to_heads = lambda t: t.reshape(b, n, HEADS, DIM_HEAD).transpose(0, 2, 1, 3)
            q, k, v = (to_heads(q), to_heads(k), to_heads(v))
            q = l2norm(q) * qs
            k = l2norm(k) * ksc
            q, k = rotary_xpos(q, k)
            o = local_attention(q, k, v)
            o = o.transpose(0, 2, 1, 3).reshape(b, n, INNER)
            x = x + o @ wo
            h = shift_token(x)
            mu = h.mean(-1, keepdims=True)
            var = h.var(-1, keepdims=True)
            h = (h - mu) / jnp.sqrt(var + 1e-05) * lg + lb
            h = h @ w1 + b1
            a, g = jnp.split(h, 2, axis=-1)
            h = a * jax.nn.gelu(g, approximate=False)
            x = x + h @ w2 + b2
            return x
        for l in range(DEPTH):
            x = _layer(x, wqkv[l], q_scale[l], k_scale[l], wo[l], ln_g[l], ln_b[l], w1[l], b1[l], w2[l], b2[l])
        return x

    def _L1_attn_ref(x, Wq, Wk, Wv, Wo):
        import jax, jax.numpy as jnp
        import numpy as np
        D_MODEL = 128
        N_HEADS = 16
        DH = D_MODEL // N_HEADS
        B, T = (4, 256)
        ROPE_BASE = 10000.0
        EPS = 1e-06

        def _rope(q, k, base=ROPE_BASE):
            half = q.shape[-1] // 2
            freqs = jnp.arange(half, dtype=q.dtype)
            inv_freq = base ** (-freqs / half)
            pos = jnp.arange(q.shape[2], dtype=q.dtype)
            ang = pos[:, None] * inv_freq[None, :]
            c = jnp.cos(ang)[None, None]
            s = jnp.sin(ang)[None, None]

            def rot(x):
                x1 = x[..., :half]
                x2 = x[..., half:2 * half]
                return jnp.concatenate([x1 * c - x2 * s, x1 * s + x2 * c], axis=-1)
            return (rot(q), rot(k))

        def _phi(x):
            return jax.nn.elu(x) + 1.0

        def _forward(x, Wq, Wk, Wv, Wo):
            Bx, Tx, D = x.shape
            H, dh = (N_HEADS, D // N_HEADS)
            q = (x @ Wq.T).reshape(Bx, Tx, H, dh).transpose(0, 2, 1, 3)
            k = (x @ Wk.T).reshape(Bx, Tx, H, dh).transpose(0, 2, 1, 3)
            v = (x @ Wv.T).reshape(Bx, Tx, H, dh).transpose(0, 2, 1, 3)
            q, k = _rope(q, k)
            q = _phi(q)
            k = _phi(k)
            qT = q.transpose(2, 0, 1, 3)
            kT = k.transpose(2, 0, 1, 3)
            vT = v.transpose(2, 0, 1, 3)

            def step(carry, qkv):
                K_sum, KV = carry
                q_t, k_t, v_t = qkv
                K_sum = K_sum + k_t
                KV = KV + k_t[..., :, None] * v_t[..., None, :]
                num = jnp.einsum('bhd,bhde->bhe', q_t, KV)
                den = jnp.maximum(jnp.einsum('bhd,bhd->bh', q_t, K_sum), EPS)
                return ((K_sum, KV), num / den[..., None])
            init = (jnp.zeros((Bx, H, dh), x.dtype), jnp.zeros((Bx, H, dh, dh), x.dtype))
            _, Y = jax.lax.scan(step, init, (qT, kT, vT))
            Y = Y.transpose(1, 0, 2, 3).reshape(Bx, Tx, D)
            return Y @ Wo.T
        return _forward(x, Wq, Wk, Wv, Wo)

    def _L1_ffn_ref(x, gate_w, gate_b, w1, b1, w2, b2):
        import jax, jax.numpy as jnp
        import numpy as np
        NUM_EXPERTS = 8
        TOP_K = 2
        D = 128
        H = 4 * D
        B, S = (4, 256)
        orig_shape = x.shape
        xf = x.reshape(-1, orig_shape[-1])
        gates = xf @ gate_w.T + gate_b
        weights, indices = jax.lax.top_k(gates, TOP_K)
        weights = jax.nn.softmax(weights, axis=-1)
        out = jnp.zeros_like(xf)
        for e in range(NUM_EXPERTS):
            w_e = jnp.sum(weights * (indices == e), axis=-1, keepdims=True)
            h = jax.nn.gelu(xf @ w1[e] + b1[e], approximate=False)
            out = out + w_e * (h @ w2[e] + b2[e])
        return out.reshape(orig_shape)
    x = L0_attn_x
    xn = _layernorm(x, axis=-1)
    x = x + _L0_attn_ref(xn, L0_attn_W_qkv, L0_attn_W_o) + _L0_ffn_ref(xn, L0_ffn_wqkv, L0_ffn_q_scale, L0_ffn_k_scale, L0_ffn_wo, L0_ffn_ln_g, L0_ffn_ln_b, L0_ffn_w1, L0_ffn_b1, L0_ffn_w2, L0_ffn_b2)
    xn = _layernorm(x, axis=-1)
    x = x + _L1_attn_ref(xn, L1_attn_Wq, L1_attn_Wk, L1_attn_Wv, L1_attn_Wo) + _L1_ffn_ref(xn, L1_ffn_gate_w, L1_ffn_gate_b, L1_ffn_w1, L1_ffn_b1, L1_ffn_w2, L1_ffn_b2)
    return x

_drawn_inputs = setup_inputs


def setup_inputs(seed=0):
    import zlib

    import numpy as np

    out = dict(_drawn_inputs(seed))
    spreads = {'L0_ffn_q_scale': (1.0, 0.6),
     'L0_ffn_k_scale': (1.0, 0.6),
     'L0_ffn_ln_g': (1.0, 0.6),
     'L0_ffn_ln_b': (0.0, 0.8),
     'L0_ffn_b1': (0.0, 0.8),
     'L0_ffn_b2': (0.0, 0.327),
     'L1_ffn_gate_b': (0.0, 0.975),
     'L1_ffn_b1': (0.0, 2.0),
     'L1_ffn_b2': (0.0, 2.0)}
    factors = {'L0_ffn_wqkv': 3.843,
     'L0_ffn_wo': 3.789,
     'L0_ffn_w1': 5.763,
     'L0_ffn_w2': 5.676,
     'L1_attn_Wq': 200.0,
     'L1_attn_Wk': 200.0,
     'L1_attn_Wv': 8.0,
     'L1_attn_Wo': 8.0,
     'L1_ffn_w1': 10.748,
     'L1_ffn_w2': 2.726,
     'L0_attn_W_qkv': 4.745,
     'L0_attn_W_o': 4.788}
    for name, (base, spread) in spreads.items():
        noise = np.random.default_rng([zlib.crc32(name.encode()), seed]).standard_normal(out[name].shape)
        drawn = base * np.exp(spread * noise) if base else spread * noise
        out[name] = jnp.asarray(drawn.astype(out[name].dtype))
    for name, factor in factors.items():
        out[name] = (out[name] * factor).astype(out[name].dtype)
    return out
```

```python
import math
from contextlib import ExitStack

import numpy as np
import concourse.bass as bass
from concourse import mybir

F32 = mybir.dt.float32
BF16 = mybir.dt.bfloat16
U32 = mybir.dt.uint32
ALU = mybir.AluOpType
ACT = mybir.ActivationFunctionType
AX = mybir.AxisListType

B, T, D = 4, 1024, 128
NT = T // 128
H, DH = 16, 8
HG, GH = 4, 4
SLOT = 32
DEPTH, LH, LD = 2, 8, 64
INNER = LH * LD
WIN = 64
HID = int(D * 4 * 2 / 3)
HID_CHUNKS = [(0, 128), (128, 128), (256, HID - 256)]
E, EH = 8, 512
BIG = 1e30
M_ROW = 64
Q_PART = [0, 0, 1, 1, 0, 2]
K_PART = [0, 1, 0, 1, 2, 0]


def constant_arrays():
    c = {}
    c["ident"] = np.eye(128, dtype=np.float32)
    p, j = np.arange(128)[:, None], np.arange(128)[None, :]
    tri = np.stack([np.where(j > p, -BIG, 0.0), np.where(p > j, -BIG, 0.0)], axis=1)
    c["causal"] = tri.astype(np.float32)
    c["keep"] = (j >= p).astype(np.float32)
    q = p % WIN
    allowed = (q <= j - 0) & (j <= q + WIN)
    window = np.where(allowed, 0.0, -BIG)
    first = np.where(allowed & ~((p < WIN) & (j < WIN)), 0.0, -BIG)
    c["window"] = np.stack([first, window], axis=1).astype(np.float32)
    c["head_of"] = (p // DH == np.arange(H)[None, :]).astype(np.float32)
    half = DH // 2
    theta = (np.float32(1.0) / np.float32(10000.0) ** (np.arange(half, dtype=np.float32) / np.float32(half)))
    ang = np.arange(T, dtype=np.float32)[:, None] * theta.astype(np.float32)[None, :]
    cos, sin = np.cos(ang.astype(np.float64)), np.sin(ang.astype(np.float64))
    d = np.arange(D) % DH
    c["rope"] = np.stack([cos.T[d % half], sin.T[d % half] * np.where(d < half, -1.0, 1.0)[:, None]], axis=1).astype(np.float32)
    idx = np.arange(0, LD, 2, dtype=np.float32)
    inv = (np.float32(1.0) / np.float32(10000.0) ** (idx / np.float32(LD))).astype(np.float32)
    t = np.arange(T, dtype=np.float32)
    fr = (t[:, None] * inv[None, :]).astype(np.float32)
    fr = np.concatenate([fr, fr], -1).astype(np.float64)
    base = ((idx + np.float32(0.4 * LD)) / np.float32(1.4 * LD)).astype(np.float32)
    power = ((t - T // 2) / np.float32(WIN // 2)).astype(np.float32)
    sc = base[None, :].astype(np.float64) ** power[:, None].astype(np.float64)
    sc = np.concatenate([sc, sc], -1)
    sign = np.where(np.arange(LD) < LD // 2, -1.0, 1.0)[None, :]
    tabs = np.stack([np.cos(fr) * sc * 8.0, np.sin(fr) * sc * sign * 8.0,
                     np.cos(fr) / sc, np.sin(fr) / sc * sign], axis=0)
    c["xpos"] = tabs.reshape(4, NT, 128, LD).transpose(2, 0, 1, 3).astype(np.float32).copy()
    return c


def build(nc, a, c, out):
    ctx = ExitStack()
    with ctx:
        taken = {}

        def sb(name, shape, dt=F32, where=ctx):
            taken[name] = taken.get(name, 0) + 1
            return where.enter_context(nc.sbuf_tensor(name if taken[name] == 1 else f"{name}_{taken[name]}", shape, dt))

        sems = {}

        def S(name):
            if name not in sems:
                sems[name] = ctx.enter_context(nc.semaphore(name))
            return sems[name]

        PS = ctx.enter_context(nc.psum_tensor("PS", [128, 8, 512], F32))

        parts_dram = nc.dram_tensor("parts_dram", (2, 128, 3, T), BF16, kind="Internal").ap()
        max_dram = nc.dram_tensor("max_dram", (HG, 3, GH * NT, 128), BF16, kind="Internal").ap()

        w_attn0 = sb("w_attn0", [128, 5, D])
        w_out0 = sb("w_out0", [128, D])
        w_attn1 = sb("w_attn1", [128, 5, D])
        w_out1 = sb("w_out1", [128, D])
        w_qkv = sb("w_qkv", [128, DEPTH, 3 * INNER])
        w_o = sb("w_o", [128, DEPTH, 4, D])
        w_up = sb("w_up", [128, DEPTH, 2 * HID])
        w_down = sb("w_down", [128, DEPTH, 3, D])
        b_up = sb("b_up", [128, DEPTH, 2, 3])
        b_down = sb("b_down", [128, DEPTH, D])
        ln_gb = sb("ln_gb", [128, DEPTH, 2])
        w_gate = sb("w_gate", [128, E])
        b_gate = sb("b_gate", [128, E])
        w_e1 = sb("w_e1", [128, E, EH])
        b_e1 = sb("b_e1", [128, E, 4])
        w_e2 = sb("w_e2", [128, E, 4, D])
        b_e2 = sb("b_e2", [NT * E, NT, D])
        ident = sb("ident", [128, 128])
        identb = sb("identb", [128, 128], BF16)
        causalb = sb("causalb", [128, 2, 128], BF16)
        keep = sb("keep", [128, 128])
        windowb = sb("windowb", [128, 2, 4, 128], BF16)
        head_of = sb("head_of", [128, H])
        rope = sb("rope", [128, 2, T])
        xpos = sb("xpos", [128, DEPTH, 4, NT, LD])
        eps_ln = sb("eps_ln", [128, 1])
        tie = sb("tie", [128, E, E])
        x_tok = sb("x_tok", [128, NT, D])
        xs_tok = sb("xs_tok", [128, NT, D])
        xT = sb("xT", [128, T])
        hT = sb("hT", [128, T])

        def chain(eng, sem):
            n = [0]

            def link(ins):
                n[0] += 1
                ins.then_inc(sem, 1)
                eng.wait_ge(sem, n[0])
            return link

        def end_phase():
            nc.all_engine_barrier()
            for s in sems.values():
                nc.gpsimd.sem_clear(s)
            nc.all_engine_barrier()

        with ExitStack() as tmp:
            windowf = sb("windowf", [128, 2, 128], F32, tmp)
            causalf = sb("causalf", [128, 2, 128], F32, tmp)
            xposf = sb("xposf", [128, 4, NT, LD], F32, tmp)
            scales = sb("scales", [128, DEPTH, 4, LD], F32, tmp)
            loads = [
                (w_attn0[:], a["w_attn0"]), (w_out0[:], a["w_out0"]), (w_attn1[:], a["w_attn1"]), (w_out1[:], a["w_out1"]),
                (w_qkv[:], a["w_qkv"]), (w_o[:], a["w_o"]), (w_up[:], a["w_up"]),
                (w_down[:], a["w_down"]), (b_up[:], a["b_up"]),
                (b_down[:], a["b_down"].partition_broadcast(128)), (ln_gb[:], a["ln_gb"]),
                (w_gate[:], a["w_gate"]), (b_gate[:], a["b_gate"].partition_broadcast(128)),
                (w_e1[:], a["w_e1"]), (b_e1[:], a["b_e1"]), (w_e2[:], a["w_e2"]), (b_e2[:], a["b_e2"]),
                (ident[:], c["ident"]), (causalf[:], c["causal"]), (keep[:], c["keep"]), (windowf[:], c["window"]),
                (head_of[:], c["head_of"]), (rope[:], c["rope"]), (xposf[:], c["xpos"]),
                (scales[:], a["scales"].partition_broadcast(128)),
            ]
            with nc.Block() as block:
                @block.sync
                def _(sp):
                    for dst, src in loads:
                        sp.dma_start(dst, src).then_inc(S("weights_in"), 16)
                    sp.wait_ge(S("weights_in"), 16 * len(loads))

                @block.gpsimd
                def _(pool):
                    pool.memset(tie[:], 1.0).then_inc(S("tie"), 1)
                    pool.wait_ge(S("tie"), 1)
                    pool.affine_select(out=tie[:], in_=tie[:], compare_op=ALU.is_gt, fill=0.0,
                                       base=0, pattern=[[1, E], [-1, E]], channel_multiplier=0).then_inc(S("tie"), 1)
                    pool.memset(eps_ln[:], 1e-5)

                @block.vector
                def _(dve):
                    dve.wait_ge(S("weights_in"), 16 * len(loads))
                    dve.tensor_copy(identb[:], ident[:])
                    dve.tensor_copy(causalb[:], causalf[:])
                    for r in range(4):
                        dve.tensor_copy(windowb[:, :, r, :], windowf[:])
                    for l in range(DEPTH):
                        for k in range(4):
                            dve.tensor_tensor(xpos[:, l, k], xposf[:, k], scales[:, l, k].unsqueeze(1).to_broadcast([128, NT, LD]), ALU.mult)
        end_phase()

        def layer_norm(block, x, dst, ready, tag):
            @block.vector
            def _(dve):
                link = chain(dve, S(tag + "_dve"))
                ready(dve)
                for i in range(NT):
                    last = dve.bn_stats(stats[:, i, :], x[:, i, :])
                link(last)
                for i in range(NT):
                    last = dve.bn_aggr(mean_var[:, i, :], stats[:, i, :])
                last.then_inc(S(tag + "_var"), 1)
                dve.wait_ge(S(tag + "_sd"), 1)
                link(dve.reciprocal(rstd[:], sd[:]))
                for i in range(NT):
                    dve.tensor_scalar(dst[:, i, :], x[:, i, :], mean_var[:, i, 0:1], rstd[:, i:i + 1],
                                      ALU.subtract, ALU.mult).then_inc(S(tag + "_normed"), 1)

            @block.scalar
            def _(act):
                act.wait_ge(S(tag + "_var"), 1)
                act.activation(sd[:], mean_var[:, :, 1], ACT.Sqrt, bias=eps_ln[:, 0:1]).then_inc(S(tag + "_sd"), 1)

        stats = sb("stats", [128, NT, 6])
        mean_var = sb("mean_var", [128, NT, 2])
        sd = sb("sd", [128, NT])
        rstd = sb("rstd", [128, NT])

        def shifted_evac(eng, copy, bank, half, sem):
            t0 = 512 * half
            copy(hT[0:64, t0:t0 + 512], PS[0:64, bank, :])
            n = 512 if half == 0 else 511
            return copy(hT[64:128, t0 + 1:t0 + 1 + n], PS[64:128, bank, 0:n])

        def act_copy(act):
            return lambda o, i: act.activation(o, i, ACT.Copy)

        def projections(block, w, xT, phi, Vst, r_q, r_k, scr, parts, Qs, Ks):
            @block.tensor
            def _(pe):
                for n in range(4):
                    for j in range(2):
                        last = pe.matmul(PS[:, 2 * n + j, :], w[:, n, :], xT[:, 512 * j:512 * j + 512], start=True, stop=True)
                    last.then_inc(S("proj"), 1)
                pe.wait_ge(S("proj_read"), 1)
                for i in range(NT):
                    last = pe.matmul(PS[:, i // 4, 128 * (i % 4):128 * (i % 4) + 128], xT[:, 128 * i:128 * i + 128], w[:, 4, :], start=True, stop=True)
                last.then_inc(S("proj_v"), 1)
                if phi:
                    pe.wait_ge(S("rotated"), 2)
                    pe.wait_ge(S("v_out"), 1)
                    for i in range(NT):
                        last = pe.transpose(PS[:, i // 4, 128 * (i % 4):128 * (i % 4) + 128], r_k[:, 128 * i:128 * i + 128], ident[:])
                    last.then_inc(S("k_turned"), 1)

            @block.vector
            def _(dve):
                link = chain(dve, S("proj_dve"))
                for n, r in enumerate((r_q, r_k)):
                    dve.wait_ge(S("proj"), 2 * n + 1)
                    dve.tensor_tensor(scr[:, 0], PS[:, 4 * n:4 * n + 2, :].rearrange("p a b -> p (a b)"), rope[:, 0], ALU.mult).then_inc(S("proj_read"), 1)
                    dve.wait_ge(S("proj"), 2 * n + 2)
                    dve.wait_ge(S("proj_read"), n + 1)
                    link(dve.tensor_tensor(scr[:, 1], PS[:, 4 * n + 2:4 * n + 4, :].rearrange("p a b -> p (a b)"), rope[:, 1], ALU.mult))
                    if phi:
                        link(dve.tensor_tensor(r[:], scr[:, 0], scr[:, 1], ALU.add))
                        dve.tensor_scalar(scr[:, 0], r[:], 0.0, None, ALU.min).then_inc(S("phi_in"), 1)
                        dve.wait_ge(S("phi_out"), n + 1)
                        dve.scalar_tensor_tensor(r[:], r[:], 0.0, scr[:, 1], ALU.max, ALU.add).then_inc(S("rotated"), 1)
                    else:
                        dve.tensor_tensor(r[:], scr[:, 0], scr[:, 1], ALU.add).then_inc(S("rotated"), 1)
                    dve.wait_ge(S("rotated"), n + 1)
                    link(dve.tensor_copy(parts[:, n, 0], r[:]))
                    link(dve.tensor_tensor(scr[:, 0], r[:], parts[:, n, 0], ALU.subtract))
                    link(dve.tensor_copy(parts[:, n, 1], scr[:, 0]))
                    link(dve.tensor_tensor(scr[:, 1], scr[:, 0], parts[:, n, 1], ALU.subtract))
                    dve.tensor_copy(parts[:, n, 2], scr[:, 1]).then_inc(S("parts"), 1)
                    dve.wait_ge(S("parts"), n + 1)

            @block.scalar
            def _(act):
                if phi:
                    for n in range(2):
                        act.wait_ge(S("phi_in"), n + 1)
                        act.activation(scr[:, 1], scr[:, 0], ACT.Exp).then_inc(S("phi_out"), 1)
                act.wait_ge(S("proj_v"), 1)
                for j in range(2):
                    last = act.activation(Vst[:, 4 * j:4 * j + 4, :, 0:DH],
                                          PS[:, j, :].rearrange("p (i h d) -> p i h d", i=4, h=H), ACT.Copy)
                last.then_inc(S("v_out"), 1)

            @block.sync
            def _(sp):
                for n in range(2):
                    sp.wait_ge(S("parts"), n + 1)
                    sp.dma_start(parts_dram[n], parts[:, n]).then_inc(S("parts_out"), 16)
                sp.wait_ge(S("parts_out"), 32)

            @block.gpsimd
            def _(pool):
                pool.memset(Qs[:].bitcast(U32), 0)
                pool.memset(Ks[:].bitcast(U32), 0).then_inc(S("zeroed"), 1)
                pool.memset(Vst[:, :, :, DH:SLOT], 0.0).then_inc(S("zeroed"), 1)
                pool.wait_ge(S("zeroed"), 2)
                pool.memset(Vst[:, :, :, DH:DH + 1], 1.0).then_inc(S("zeroed"), 1)
                if not phi:
                    pool.wait_ge(S("zeroed"), 3)
                    pool.memset(Ks[M_ROW:M_ROW + 3], 1.0)

        def restack(sp, dst, n, g, head0, heads, t0, tn, sem):
            part = (Q_PART, K_PART)[n][g]
            src = parts_dram[n].rearrange("(h d) j t -> d h j t", d=DH)[:, head0:head0 + heads, part, t0:t0 + tn]
            sp.dma_start(dst[DH * g:DH * g + DH], src).then_inc(sem, 16)

        def out_projection(pe_wait, block, y_tok, yT, w, dst, tag):
            @block.tensor
            def _(pe):
                pe_wait(pe)
                for i in range(NT):
                    last = pe.transpose(PS[:, i // 4, 128 * (i % 4):128 * (i % 4) + 128], y_tok[:, i, :], ident[:])
                last.then_inc(S(tag + "_turned"), 1)
                pe.wait_ge(S(tag + "_yT"), 2)
                for i in range(NT):
                    last = pe.matmul(PS[:, 2 + i // 4, 128 * (i % 4):128 * (i % 4) + 128], yT[:, 128 * i:128 * i + 128], w[:], start=True, stop=True)
                last.then_inc(S(tag + "_out"), 1)

            @block.scalar
            def _(act):
                act.wait_ge(S(tag + "_turned"), 1)
                for j in range(2):
                    act.activation(yT[:, 512 * j:512 * j + 512], PS[:, j, :], ACT.Copy).then_inc(S(tag + "_yT"), 1)

            @block.vector
            def _(dve):
                dve.wait_ge(S(tag + "_out"), 1)
                for j in range(2):
                    dve.tensor_tensor(dst[:, 4 * j:4 * j + 4, :], x_tok[:, 4 * j:4 * j + 4, :],
                                      PS[:, 2 + j, :].rearrange("p (i d) -> p i d", i=4), ALU.add)

        x_dram = a["x"].rearrange("b (i p) d -> b p i d", p=128)
        out_dram = out.rearrange("b (i p) d -> b p i d", p=128)

        with nc.Fori(0, B) as b:
            with nc.Block() as block:
                @block.sync
                def _(sp):
                    sp.dma_start(x_tok[:], x_dram[b]).then_inc(S("x_in"), 16)

                layer_norm(block, x_tok, xs_tok, lambda dve: dve.wait_ge(S("x_in"), 16), "ln0")

                @block.tensor
                def _(pe):
                    for i in range(NT):
                        pe.wait_ge(S("ln0_normed"), i + 1)
                        last = pe.transpose(PS[:, i // 4, 128 * (i % 4):128 * (i % 4) + 128], xs_tok[:, i, :], ident[:])
                        if i % 4 == 3:
                            last.then_inc(S("xT_bank"), 1)

                @block.scalar
                def _(act):
                    for j in range(2):
                        act.wait_ge(S("xT_bank"), j + 1)
                        act.activation(xT[:, 512 * j:512 * j + 512], PS[:, j, :], ACT.Copy)
            end_phase()

            with ExitStack() as tmp:
                Vst = sb("Vst", [128, NT, H, SLOT], F32, tmp)
                y_tok = sb("y_tok", [128, NT, D], F32, tmp)
                Qs = sb("Qs", [128, 2, GH, T], BF16, tmp)
                Ks = sb("Ks", [128, 2, GH, T], BF16, tmp)
                with ExitStack() as tmp2:
                    scr = sb("scr", [128, 2, T], F32, tmp2)
                    r_qk = sb("r_qk", [128, T], F32, tmp2)
                    parts = sb("parts", [128, 2, 3, T], BF16, tmp2)
                    with nc.Block() as block:
                        projections(block, w_attn0, xT, False, Vst, r_qk, r_qk, scr, parts, Qs, Ks)
                    end_phase()
                NP = 8
                P = sb("P", [128, NP, 512], F32, tmp)
                O = sb("O", [128, T], F32, tmp)
                yT = sb("yT", [128, T], F32, tmp)
                mx = sb("mx", [128, GH, NT, 2], F32, tmp)
                mT = sb("mT", [GH * NT, 128], F32, tmp)
                mT2 = sb("mT2", [GH * NT, 128], F32, tmp)
                m_parts = sb("m_parts", [GH * NT, 3, 128], BF16, tmp)
                den = sb("den", [128, 4, GH], F32, tmp)
                zero_rows = sb("zero_rows", [3, GH, T], BF16, tmp)

                tiles = [(i, lo, min(lo + 512, 128 * (i + 1))) for i in range(NT) for lo in range(0, 128 * (i + 1), 512)]
                units1 = [(h, *t) for h in range(GH) for t in tiles]
                blocks2 = [(i, max(lo, 128 * i), lo + 512) for i in range(NT) for lo in (0, 512) if lo + 512 > 128 * i]
                U1, U2 = len(units1), len(blocks2) * GH
                assert U1 == U2
                with nc.Block() as block:
                    @block.tensor
                    def _(pe):
                        def max_scores(g, u):
                            h, i, lo, hi = units1[u]
                            n = g * U1 + u
                            if u == 0:
                                pe.wait_ge(S(f"q_in{g}"), 16 * 7)
                                pe.wait_ge(S(f"k_in{g}"), 16 * 6)
                            if n >= 3:
                                pe.wait_ge(S("max_read"), n - 2)
                            diag = hi == 128 * (i + 1)
                            last = pe.matmul(PS[:, n % 3, 0:hi - lo], Qs[:, g % 2, h, 128 * i:128 * i + 128], Ks[:, g % 2, h, lo:hi],
                                             start=True, stop=not diag)
                            if diag:
                                last = pe.matmul(PS[:, n % 3, hi - lo - 128:hi - lo], identb[:], causalb[:, 0, :], start=False, stop=True)
                            last.then_inc(S("max_scores"), 1)

                        def key_scores(g, u):
                            (i, lo, hi), h = blocks2[u // GH], u % GH
                            n = g * U2 + u
                            if u == 0:
                                pe.wait_ge(S("m_in"), 16 * (g + 1))
                            if n >= 2:
                                pe.wait_ge(S("exp"), n - 1)
                            diag = lo == 128 * i
                            last = pe.matmul(PS[:, 3 + n % 2, 0:hi - lo], Ks[:, g % 2, h, 128 * i:128 * i + 128], Qs[:, g % 2, h, lo:hi],
                                             start=True, stop=not diag)
                            if diag:
                                last = pe.matmul(PS[:, 3 + n % 2, 0:128], identb[:], causalb[:, 1, :], start=False, stop=True)
                            last.then_inc(S("key_scores"), 1)

                        def values(g, k):
                            i, lo, hi = blocks2[k]
                            pe.wait_ge(S("exp"), g * U2 + GH * (k + 1))
                            if k == 0 and g:
                                pe.wait_ge(S("O_copied"), g)
                            bank = lo // 512
                            for h in range(GH):
                                n = g * U2 + GH * k + h
                                last = pe.matmul(PS[SLOT * h:SLOT * h + SLOT, 5 + bank, lo - 512 * bank:hi - 512 * bank],
                                                 Vst[:, i, GH * g + h, :], P[:, n % NP, 0:hi - lo],
                                                 start=(i == 0), stop=(i == (3, NT - 1)[bank]))
                            last.then_inc(S("values"), 1)

                        def turn_max(g):
                            pe.wait_ge(S("mx"), g + 1)
                            if g == 1:
                                pe.wait_ge(S("mT_read"), 1)
                            if g >= 2:
                                pe.wait_ge(S("y"), 2 * (g - 1))
                            pe.transpose(PS[0:GH * NT, 7, 0:128], mx[:, :, :, 0], ident[:]).then_inc(S("m_turned"), 1)

                        def turn_out(g):
                            pe.wait_ge(S("O_copied"), g + 1)
                            for j in range(2):
                                pe.wait_ge(S("mT_read"), min(g + 2, HG))
                                if 2 * g + j:
                                    pe.wait_ge(S("y"), 2 * g + j)
                                for k in range(4):
                                    i = 4 * j + k
                                    last = pe.transpose(PS[:, 7, 128 * k:128 * k + 128], O[:, 128 * i:128 * i + 128], ident[:])
                                last.then_inc(S("O_turned"), 1)

                        for u in range(U1):
                            max_scores(0, u)
                        turn_max(0)
                        for g in range(HG):
                            for u in range(U2):
                                if g + 1 < HG:
                                    max_scores(g + 1, u)
                                key_scores(g, u)
                                if u % GH == GH - 1 and u >= GH:
                                    values(g, u // GH - 1)
                            values(g, U2 // GH - 1)
                            if g + 1 < HG:
                                turn_max(g + 1)
                            turn_out(g)

                    @block.vector
                    def _(dve):
                        link = chain(dve, S("attn_dve"))

                        def maxima(g, u):
                            h, i, lo, hi = units1[u]
                            n = g * U1 + u
                            dve.wait_ge(S("max_scores"), n + 1)
                            dve.reduce_max(mx[:, h, i, lo // 512:lo // 512 + 1], PS[:, n % 3, 0:hi - lo], AX.X).then_inc(S("max_read"), 1)

                        def join(g):
                            dve.wait_ge(S("max_read"), (g + 1) * U1)
                            dve.tensor_tensor(mx[:, :, 4:, 0], mx[:, :, 4:, 0], mx[:, :, 4:, 1], ALU.max).then_inc(S("mx"), 1)

                        def split(g):
                            dve.wait_ge(S("m_turned"), g + 1)
                            if g:
                                dve.wait_ge(S("m_out"), 16 * g)
                            link(dve.tensor_scalar(mT[:], PS[0:GH * NT, 7, 0:128], -1.0, None, ALU.mult))
                            dve.tensor_copy(m_parts[:, 0], mT[:]).then_inc(S("mT_read"), 1)
                            dve.wait_ge(S("mT_read"), g + 1)
                            link(dve.tensor_tensor(mT2[:], mT[:], m_parts[:, 0], ALU.subtract))
                            link(dve.tensor_copy(m_parts[:, 1], mT2[:]))
                            link(dve.tensor_tensor(mT[:], mT2[:], m_parts[:, 1], ALU.subtract))
                            dve.tensor_copy(m_parts[:, 2], mT[:]).then_inc(S("m_parts"), 1)
                            dve.wait_ge(S("m_parts"), g + 1)

                        def normalise(g):
                            for j in range(2):
                                dve.wait_ge(S("O_turned"), 2 * g + j + 1)
                                o = PS[:, 7, :].rearrange("p (i h s) -> p i h s", i=4, h=GH)
                                link(dve.reciprocal(den[:], o[:, :, :, DH]))
                                dve.tensor_tensor(y_tok[:, 4 * j:4 * j + 4, 32 * g:32 * g + 32].rearrange("p i (h d) -> p i h d", h=GH),
                                                  o[:, :, :, 0:DH], den[:].unsqueeze(3).to_broadcast([128, 4, GH, DH]), ALU.mult).then_inc(S("y"), 1)
                                dve.wait_ge(S("y"), 2 * g + j + 1)

                        for u in range(U1):
                            maxima(0, u)
                        join(0)
                        split(0)
                        for g in range(HG):
                            if g + 1 < HG:
                                for u in range(U1):
                                    maxima(g + 1, u)
                                join(g + 1)
                                split(g + 1)
                            normalise(g)

                    @block.scalar
                    def _(act):
                        for g in range(HG):
                            for u in range(U2):
                                i, lo, hi = blocks2[u // GH]
                                n = g * U2 + u
                                act.wait_ge(S("key_scores"), n + 1)
                                if n >= NP:
                                    act.wait_ge(S("values"), (n - NP) // GH + 1)
                                act.activation(P[:, n % NP, 0:hi - lo], PS[:, 3 + n % 2, 0:hi - lo], ACT.Exp,
                                               scale=1.0 / math.sqrt(DH)).then_inc(S("exp"), 1)
                            act.wait_ge(S("values"), (g + 1) * len(blocks2))
                            if g:
                                act.wait_ge(S("O_turned"), 2 * g)
                            act.activation(O[:], PS[:, 5:7, :].rearrange("p a b -> p (a b)"), ACT.Copy).then_inc(S("O_copied"), 1)

                    @block.gpsimd
                    def _(pool):
                        pool.memset(zero_rows[:], 0.0).then_inc(S("zero_rows"), 1)

                    @block.sync
                    def _(sp):
                        def stack(g):
                            if g >= 2:
                                sp.wait_ge(S("key_scores"), (g - 1) * U2)
                            sp.dma_start(Qs[M_ROW:M_ROW + 3, g % 2], zero_rows[:]).then_inc(S(f"q_in{g}"), 16)
                            for k in range(6):
                                restack(sp, Qs[:, g % 2], 0, k, GH * g, GH, 0, T, S(f"q_in{g}"))
                                restack(sp, Ks[:, g % 2], 1, k, GH * g, GH, 0, T, S(f"k_in{g}"))

                        sp.wait_ge(S("zero_rows"), 1)
                        stack(0)
                        stack(1)
                        for g in range(HG):
                            sp.wait_ge(S("m_parts"), g + 1)
                            sp.dma_start(max_dram[g].rearrange("j r t -> r j t"), m_parts[:]).then_inc(S("m_out"), 16)
                            sp.wait_ge(S("m_out"), 16 * (g + 1))
                            sp.dma_start(Qs[M_ROW:M_ROW + 3, g % 2], max_dram[g].rearrange("j (h i) t -> j h (i t)", h=GH)).then_inc(S("m_in"), 16)
                            if 1 <= g and g + 1 < HG:
                                stack(g + 1)
                end_phase()
                with nc.Block() as block:
                    out_projection(lambda pe: None, block, y_tok, yT, w_out0, x_tok, "o0")
                end_phase()

            for l in range(DEPTH):
                with ExitStack() as tmp:
                    raw = sb("raw", [128, 2, 3, INNER], F32, tmp)
                    sq = sb("sq", [128, 2, INNER], F32, tmp)
                    ra = sb("ra", [128, 2, INNER], F32, tmp)
                    rb = sb("rb", [128, 2, INNER], F32, tmp)
                    ss = sb("ss", [128, 2, LH], F32, tmp)
                    nrm = sb("nrm", [128, 2, LH], F32, tmp)
                    qk = sb("qk", [128, 2, INNER], F32, tmp)
                    qT = sb("qT", [128, 4, 128], F32, tmp)
                    kT = sb("kT", [128, 4, WIN + T], F32, tmp)
                    V_A = sb("V_A", [128, 2, LH, LD + 1], F32, tmp)
                    V_B = sb("V_B", [128, 2, LH, LD + 1], F32, tmp)
                    sm = sb("sm", [128, LH, 128], F32, tmp)
                    PT = sb("PT", [128, LH, 128], F32, tmp)
                    mxl = sb("mxl", [128, LH], F32, tmp)
                    rd = sb("rd", [128, LH], F32, tmp)
                    o_tok = sb("o_tok", [128, INNER], F32, tmp)
                    oT = sb("oT", [128, 4, 128], F32, tmp)
                    with nc.Block() as block:
                        @block.tensor
                        def _(pe):
                            for i in range(NT):
                                pe.transpose(PS[:, i // 4, 128 * (i % 4):128 * (i % 4) + 128], xs_tok[:, i, :], ident[:]).then_inc(S("h_turned"), 1)

                            def project(i):
                                if i == 0:
                                    pe.wait_ge(S("v_ones"), 1)
                                    pe.wait_ge(S("hT"), 2)
                                else:
                                    pe.wait_ge(S("raw"), i)
                                for n in range(3):
                                    last = pe.matmul(PS[:, n, :], hT[:, 128 * i:128 * i + 128], w_qkv[:, l, INNER * n:INNER * n + INNER], start=True, stop=True)
                                last.then_inc(S("qkv"), 1)

                            def turn_qk(i):
                                pe.wait_ge(S("qk"), i + 1)
                                for n in range(2):
                                    if i:
                                        pe.wait_ge(S(f"bank{3 + n}"), 2 * i)
                                    for k in range(4):
                                        last = pe.transpose(PS[:, 3 + n, 128 * k:128 * k + 128], qk[:, n, 128 * k:128 * k + 128], ident[:])
                                    last.then_inc(S(f"turned{n}"), 1)

                            def scores(i):
                                for n in range(2):
                                    pe.wait_ge(S(f"bank{3 + n}"), 2 * i + 1)
                                if i:
                                    pe.wait_ge(S("o"), i)
                                for g in range(2):
                                    pe.matmul(PS[:, 5 + g, :], identb[:], windowb[:, min(i, 1)].rearrange("p r j -> p (r j)"), start=True, stop=False, skip_group_check=True)
                                for k in range(4):
                                    for w in range(2):
                                        for g in range(2):
                                            last = pe.matmul(PS[64 * w:64 * w + 64, 5 + g, 128 * k:128 * k + 128],
                                                             qT[LD * g:LD * g + LD, k, 64 * w:64 * w + 64],
                                                             kT[LD * g:LD * g + LD, k, 128 * i + 64 * w:128 * i + 64 * w + 128],
                                                             start=False, stop=(k == 3), skip_group_check=True)
                                            if k == 3 and w == 1:
                                                last.then_inc(S("scores"), 1)

                            def turn_p(i):
                                pe.wait_ge(S("p"), i + 1)
                                for g in range(2):
                                    for k in range(4):
                                        last = pe.transpose(PS[:, 3 + g, 128 * k:128 * k + 128], sm[:, 4 * g + k, :], ident[:])
                                    last.then_inc(S(f"turned{g}"), 1)

                            def values(i):
                                pe.wait_ge(S("bank3"), 2 * i + 2)
                                pe.wait_ge(S("bank4"), 2 * i + 2)
                                pe.wait_ge(S(f"v_in{i % 2}"), 32 * (i // 2 + 1))
                                if i:
                                    pe.wait_ge(S(f"v_low{i % 2}"), 16 * ((i + 1) // 2))
                                    pe.wait_ge(S("xs"), i)
                                for g, bank in ((0, 7), (1, 5)):
                                    for k in range(4):
                                        for w, V in ((0, V_B), (1, V_A)):
                                            last = pe.matmul(PS[64 * w:64 * w + 64, bank, 128 * k:128 * k + LD + 1],
                                                             PT[:, 4 * g + k, 64 * w:64 * w + 64], V[:, i % 2, 2 * k + g, :], start=True, stop=True)
                                    last.then_inc(S("pv"), 1)

                            def turn_o(i):
                                pe.wait_ge(S("o"), i + 1)
                                for k in range(4):
                                    last = pe.transpose(PS[:, 6, 128 * k:128 * k + 128], o_tok[:, 128 * k:128 * k + 128], ident[:])
                                last.then_inc(S("o_turned"), 1)

                            def back(i):
                                pe.wait_ge(S("oT"), i + 1)
                                for k in range(4):
                                    last = pe.matmul(PS[:, 7, 0:D], oT[:, k, :], w_o[:, l, k, :], start=(k == 0), stop=(k == 3))
                                last.then_inc(S("back"), 1)

                            project(0)
                            for i in range(NT):
                                turn_qk(i)
                                if i + 1 < NT:
                                    project(i + 1)
                                scores(i)
                                turn_p(i)
                                values(i)
                                turn_o(i)
                                back(i)

                        @block.scalar
                        def _(act):
                            for j in range(2):
                                act.wait_ge(S("h_turned"), 4 * (j + 1))
                                shifted_evac(act, act_copy(act), j, j, None).then_inc(S("hT"), 1)

                            def raw_qkv(i):
                                act.wait_ge(S("qkv"), i + 1)
                                if i >= 2:
                                    act.wait_ge(S("rot"), 2 * (i - 1))
                                    act.wait_ge(S(f"v_in{i % 2}"), 32 * (i // 2))
                                    act.wait_ge(S(f"v_low{(i - 1) % 2}"), 16 * (i // 2))
                                act.activation(raw[:, i % 2].rearrange("p n d -> p (n d)"), PS[:, 0:3, :].rearrange("p n d -> p (n d)"), ACT.Copy).then_inc(S("raw"), 1)
                                act.wait_ge(S("raw"), i + 1)
                                if i:
                                    act.wait_ge(S("ss"), i)
                                act.activation(sq[:], raw[:, i % 2, 0:2], ACT.Square).then_inc(S("sq"), 1)
                                act.wait_ge(S("ss"), i + 1)
                                act.activation(nrm[:], ss[:], ACT.Sqrt).then_inc(S("nrm"), 1)

                            raw_qkv(0)
                            for i in range(NT):
                                act.wait_ge(S("turned0"), 2 * i + 1)
                                act.activation(qT[:].rearrange("p k t -> p (k t)"), PS[:, 3, :], ACT.Copy).then_inc(S("bank3"), 1)
                                act.wait_ge(S("turned1"), 2 * i + 1)
                                act.activation(kT[:, :, WIN + 128 * i:WIN + 128 * i + 128], PS[:, 4, :].rearrange("p (k t) -> p k t", k=4), ACT.Copy).then_inc(S("bank4"), 1)
                                if i + 1 < NT:
                                    raw_qkv(i + 1)
                                act.wait_ge(S("less_max"), i + 1)
                                act.activation(sm[:], sm[:], ACT.Exp).then_inc(S("p"), 1)
                                for g in range(2):
                                    act.wait_ge(S(f"turned{g}"), 2 * i + 2)
                                    act.activation(PT[:, 4 * g:4 * g + 4].rearrange("p k t -> p (k t)"), PS[:, 3 + g, :], ACT.Copy).then_inc(S(f"bank{3 + g}"), 1)
                                act.wait_ge(S("o_turned"), i + 1)
                                act.activation(oT[:].rearrange("p k t -> p (k t)"), PS[:, 6, :], ACT.Copy).then_inc(S("oT"), 1)

                        @block.vector
                        def _(dve):
                            link = chain(dve, S("local_dve"))
                            dve.memset(kT[:, :, 0:WIN], 0.0)
                            dve.memset(V_B[0:64, 0, :, 0:LD], 0.0)
                            dve.memset(hT[64:128, 0:1], 0.0)
                            for V in (V_A, V_B):
                                last = dve.memset(V[:, :, :, LD:LD + 1], 1.0)
                            last.then_inc(S("v_ones"), 1)

                            def rotate(i):
                                dve.wait_ge(S("raw"), i + 1)
                                for n in range(2):
                                    x = raw[:, i % 2, n].rearrange("p (h a d) -> p h a d", h=LH, a=2)
                                    cos = xpos[:, l, 2 * n, i].unsqueeze(1).to_broadcast([128, LH, LD])
                                    sin = xpos[:, l, 2 * n + 1, i].rearrange("p (a d) -> p a d", a=2).unsqueeze(1).to_broadcast([128, LH, 2, LD // 2])
                                    dve.tensor_tensor(ra[:, n].rearrange("p (h d) -> p h d", h=LH), raw[:, i % 2, n].rearrange("p (h d) -> p h d", h=LH), cos, ALU.mult)
                                    dve.tensor_tensor(rb[:, n].rearrange("p (h a d) -> p h a d", h=LH, a=2), x[:, :, ::-1, :], sin, ALU.mult).then_inc(S("rot"), 1)
                                dve.wait_ge(S("rot"), 2 * (i + 1))
                                link(dve.tensor_tensor(ra[:], ra[:], rb[:], ALU.add))
                                dve.wait_ge(S("sq"), i + 1)
                                dve.reduce_sum(ss[:], sq[:].rearrange("p n (h d) -> p n h d", h=LH), AX.X).then_inc(S("ss"), 1)
                                dve.wait_ge(S("nrm"), i + 1)
                                link(dve.tensor_scalar(nrm[:], nrm[:], 1e-12, None, ALU.max))
                                link(dve.reciprocal(nrm[:], nrm[:]))
                                if i:
                                    dve.wait_ge(S("turned1"), 2 * i - 1)
                                dve.tensor_tensor(qk[:].rearrange("p n (h d) -> p (n h) d", h=LH), ra[:].rearrange("p n (h d) -> p (n h) d", h=LH),
                                                  nrm[:].rearrange("p n h -> p (n h)").unsqueeze(2).to_broadcast([128, 2 * LH, LD]), ALU.mult).then_inc(S("qk"), 1)

                            rotate(0)
                            for i in range(NT):
                                if i + 1 < NT:
                                    rotate(i + 1)
                                if i:
                                    dve.wait_ge(S("turned1"), 2 * i)
                                for g in range(2):
                                    dve.wait_ge(S("scores"), 2 * i + g + 1)
                                    s = PS[:, 5 + g, :].rearrange("p (k j) -> p k j", k=4)
                                    link(dve.reduce_max(mxl[:, 4 * g:4 * g + 4], s, AX.X))
                                    last = dve.tensor_tensor(sm[:, 4 * g:4 * g + 4, :], s, mxl[:, 4 * g:4 * g + 4].unsqueeze(2).to_broadcast([128, 4, 128]), ALU.subtract)
                                last.then_inc(S("less_max"), 1)
                                if i:
                                    dve.wait_ge(S("o_turned"), i)
                                for g, bank in ((0, 7), (1, 5)):
                                    dve.wait_ge(S("pv"), 2 * i + g + 1)
                                    o = PS[:, bank, :].rearrange("p (k s) -> p k s", k=4)
                                    link(dve.reciprocal(rd[:, 4 * g:4 * g + 4], o[:, :, LD]))
                                    last = dve.tensor_tensor(o_tok[:].rearrange("p (k g d) -> p k g d", k=4, g=2)[:, :, g, :], o[:, :, 0:LD],
                                                             rd[:, 4 * g:4 * g + 4].unsqueeze(2).to_broadcast([128, 4, LD]), ALU.mult)
                                last.then_inc(S("o"), 1)
                                dve.wait_ge(S("o"), i + 1)
                                dve.wait_ge(S("back"), i + 1)
                                dve.tensor_tensor(xs_tok[:, i, :], xs_tok[:, i, :], PS[:, 7, 0:D], ALU.add).then_inc(S("xs"), 1)

                        @block.sync
                        def _(sp):
                            sp.wait_ge(S("v_ones"), 1)
                            for i in range(NT):
                                sp.wait_ge(S("raw"), i + 1)
                                v = raw[:, i % 2, 2].rearrange("p (h d) -> p h d", h=LH)
                                if i >= 2:
                                    sp.wait_ge(S("pv"), 2 * (i - 1))
                                sp.dma_start(V_A[:, i % 2, :, 0:LD], v).then_inc(S(f"v_in{i % 2}"), 16)
                                sp.dma_start(V_B[64:128, i % 2, :, 0:LD], v[0:64]).then_inc(S(f"v_in{i % 2}"), 16)
                                if i + 1 < NT:
                                    if i >= 1:
                                        sp.wait_ge(S("pv"), 2 * i)
                                    sp.dma_start(V_B[0:64, (i + 1) % 2, :, 0:LD], v[64:128]).then_inc(S(f"v_low{(i + 1) % 2}"), 16)
                    end_phase()

                with ExitStack() as tmp:
                    hs = sb("hs", [128, NT, D], F32, tmp)
                    hn = sb("hn", [128, T], F32, tmp)
                    gl = sb("gl", [128, 2, 512], F32, tmp)
                    hid = sb("hid", [128, 3, T], F32, tmp)
                    with nc.Block() as block:
                        @block.sync
                        def _(sp):
                            sp.dma_start(hs[1:128, :, 64:], xs_tok[0:127, :, 64:]).then_inc(S("shift"), 16)
                            sp.dma_start(hs[0:1, 1:, 64:], xs_tok[127:128, 0:NT - 1, 64:]).then_inc(S("shift"), 16)

                        @block.gpsimd
                        def _(pool):
                            pool.memset(hs[0:1, 0, 64:], 0.0).then_inc(S("first"), 1)

                        def ready(dve):
                            link = chain(dve, S("hs_dve"))
                            link(dve.tensor_copy(hs[:, :, 0:64], xs_tok[:, :, 0:64]))
                            dve.wait_ge(S("first"), 1)
                            dve.wait_ge(S("shift"), 32)

                        layer_norm(block, hs, hs, ready, "lnf")

                        @block.tensor
                        def _(pe):
                            for i in range(NT):
                                pe.wait_ge(S("lnf_normed"), i + 1)
                                last = pe.transpose(PS[:, i // 4, 128 * (i % 4):128 * (i % 4) + 128], hs[:, i, :], ident[:])
                                if i % 4 == 3:
                                    last.then_inc(S("hn_turned"), 1)

                            def up(n):
                                j, (c0, cw) = n // 3, HID_CHUNKS[n % 3]
                                pe.wait_ge(S("hn"), j + 1)
                                if n >= 2:
                                    pe.wait_ge(S("hid"), n - 1)
                                for k in range(2):
                                    last = pe.matmul(PS[0:cw, 2 + 2 * (n % 2) + k, :], w_up[:, l, HID * k + c0:HID * k + c0 + cw], hn[:, 512 * j:512 * j + 512], start=True, stop=True)
                                last.then_inc(S("up"), 1)

                            def down(j):
                                pe.wait_ge(S("hid"), 3 * (j + 1))
                                for k in range(4):
                                    i = 4 * j + k
                                    for n, (c0, cw) in enumerate(HID_CHUNKS):
                                        last = pe.matmul(PS[:, 6 + j, 128 * k:128 * k + 128], hid[0:cw, n, 128 * i:128 * i + 128], w_down[0:cw, l, n, :], start=(n == 0), stop=(n == 2))
                                last.then_inc(S("down"), 1)

                            for n in range(5):
                                up(n)
                            down(0)
                            up(5)
                            down(1)

                        @block.scalar
                        def _(act):
                            for n in range(6):
                                cw = HID_CHUNKS[n % 3][1]
                                act.wait_ge(S("up"), n + 1)
                                if n >= 2:
                                    act.wait_ge(S("hid"), n - 1)
                                act.activation(gl[0:cw, n % 2, :], PS[0:cw, 3 + 2 * (n % 2), :], ACT.Gelu, bias=b_up[0:cw, l, 1, n % 3:n % 3 + 1]).then_inc(S("gelu"), 1)

                        @block.vector
                        def _(dve):
                            for j in range(2):
                                dve.wait_ge(S("hn_turned"), j + 1)
                                dve.tensor_scalar(hn[:, 512 * j:512 * j + 512], PS[:, j, :], ln_gb[:, l, 0:1], ln_gb[:, l, 1:2], ALU.mult, ALU.add).then_inc(S("hn"), 1)
                            dve.tensor_tensor(xs_tok[:], xs_tok[:], b_down[:, l].unsqueeze(1).to_broadcast([128, NT, D]), ALU.add).then_inc(S("xb"), 1)
                            for n in range(6):
                                j, cw = n // 3, HID_CHUNKS[n % 3][1]
                                dve.wait_ge(S("gelu"), n + 1)
                                dve.scalar_tensor_tensor(hid[0:cw, n % 3, 512 * j:512 * j + 512], PS[0:cw, 2 + 2 * (n % 2), :], b_up[0:cw, l, 0, n % 3:n % 3 + 1],
                                                         gl[0:cw, n % 2, :], ALU.add, ALU.mult).then_inc(S("hid"), 1)
                            dve.wait_ge(S("xb"), 1)
                            for j in range(2):
                                dve.wait_ge(S("down"), j + 1)
                                dve.tensor_tensor(xs_tok[:, 4 * j:4 * j + 4, :], xs_tok[:, 4 * j:4 * j + 4, :], PS[:, 6 + j, :].rearrange("p (i d) -> p i d", i=4), ALU.add)
                    end_phase()

            with nc.Block() as block:
                def both(dve):
                    link = chain(dve, S("both"))
                    link(dve.tensor_tensor(x_tok[:], x_tok[:], xs_tok[:], ALU.add))

                layer_norm(block, x_tok, xs_tok, both, "ln1")

                @block.tensor
                def _(pe):
                    for i in range(NT):
                        pe.wait_ge(S("ln1_normed"), i + 1)
                        last = pe.transpose(PS[:, i // 4, 128 * (i % 4):128 * (i % 4) + 128], xs_tok[:, i, :], ident[:])
                        if i % 4 == 3:
                            last.then_inc(S("xT_bank"), 1)

                @block.scalar
                def _(act):
                    for j in range(2):
                        act.wait_ge(S("xT_bank"), j + 1)
                        act.activation(xT[:, 512 * j:512 * j + 512], PS[:, j, :], ACT.Copy)
            end_phase()

            with ExitStack() as tmp:
                Vst = sb("Vst1", [128, NT, H, SLOT], F32, tmp)
                r_q = sb("r_q", [128, T], F32, tmp)
                r_k = sb("r_k", [128, T], F32, tmp)
                y_tok = sb("y_tok1", [128, NT, D], F32, tmp)
                QT = 256
                Qs = sb("Qs1", [128, 2, H, QT], BF16, tmp)
                Ks = sb("Ks1", [128, 2, H, QT], BF16, tmp)
                with ExitStack() as tmp2:
                    scr = sb("scr1", [128, 2, T], F32, tmp2)
                    parts = sb("parts1", [128, 2, 3, T], BF16, tmp2)
                    with nc.Block() as block:
                        projections(block, w_attn1, xT, True, Vst, r_q, r_k, scr, parts, Qs, Ks)
                    end_phase()
                k_tok = sb("k_tok", [128, NT, D], F32, tmp)
                A = sb("A", [128, 4, GH, 128], F32, tmp)
                KV = sb("KV", [128, 2, H, SLOT], F32, tmp)
                O = sb("O1", [128, HG, 128], F32, tmp)
                den = sb("den1", [128, HG, GH], F32, tmp)
                yT = sb("yT1", [128, T], F32, tmp)
                with nc.Block() as block:
                    @block.tensor
                    def _(pe):
                        def chunk_scores(i, g):
                            n = HG * i + g
                            if g == 0 and i % 2 == 0:
                                pe.wait_ge(S(f"q_in{i // 2}"), 16 * 6)
                                pe.wait_ge(S(f"k_in{i // 2}"), 16 * 6)
                            if n >= 2:
                                pe.wait_ge(S("kept"), n - 1)
                            for k in range(GH):
                                t0 = 128 * (i % 2)
                                last = pe.matmul(PS[:, 2 + n % 2, 128 * k:128 * k + 128], Ks[:, i // 2 % 2, GH * g + k, t0:t0 + 128],
                                                 Qs[:, i // 2 % 2, GH * g + k, t0:t0 + 128], start=True, stop=True)
                            last.then_inc(S("a_scores"), 1)

                        def chunk_out(i, g):
                            n = HG * i + g
                            if g == 0 and i >= 2:
                                pe.wait_ge(S("O_copied"), i - 1)
                            if i:
                                if g == 0:
                                    pe.wait_ge(S("state"), i)
                                pe.matmul(PS[:, 4 + i % 2, 128 * g:128 * g + 128], KV[:, i % 2, GH * g:GH * g + GH, :].rearrange("p h s -> p (h s)"),
                                          r_q[:, 128 * i:128 * i + 128], start=True, stop=False, skip_group_check=True)
                            pe.wait_ge(S("kept"), n + 1)
                            for k in range(GH):
                                last = pe.matmul(PS[SLOT * k:SLOT * k + SLOT, 4 + i % 2, 128 * g:128 * g + 128], Vst[:, i, GH * g + k, :], A[:, n % 4, k, :],
                                                 start=(i == 0), stop=True, skip_group_check=True)
                            last.then_inc(S("a_out"), 1)

                        def state(i):
                            pe.wait_ge(S("k_tok"), 1)
                            if i:
                                pe.wait_ge(S("state"), i)
                            pe.matmul(PS[:, 6, :], k_tok[:, i, :], Vst[:, i].rearrange("p h s -> p (h s)"), start=(i == 0), stop=True, skip_group_check=True).then_inc(S("summed"), 1)

                        def turn_out(i):
                            pe.wait_ge(S("O_copied"), i + 1)
                            if i:
                                pe.wait_ge(S("y"), i)
                            for g in range(HG):
                                last = pe.transpose(PS[:, 7, 128 * g:128 * g + 128], O[:, g, :], ident[:])
                            last.then_inc(S("O_turned"), 1)

                        for i in range(NT):
                            chunk_scores(i, 0)
                            for g in range(HG):
                                if g + 1 < HG:
                                    chunk_scores(i, g + 1)
                                chunk_out(i, g)
                            if i + 1 < NT:
                                state(i)
                            if i:
                                turn_out(i - 1)
                        turn_out(NT - 1)

                    @block.vector
                    def _(dve):
                        link = chain(dve, S("lin_dve"))
                        for j in range(2):
                            last = dve.tensor_copy(k_tok[:, 4 * j:4 * j + 4, :], PS[:, j, :].rearrange("p (i d) -> p i d", i=4))
                        last.then_inc(S("k_tok"), 1)

                        def normalise(i):
                            dve.wait_ge(S("O_turned"), i + 1)
                            o = PS[:, 7, :].rearrange("p (g h s) -> p g h s", g=HG, h=GH)
                            link(dve.tensor_scalar(den[:], o[:, :, :, DH], 1e-6, None, ALU.max))
                            link(dve.reciprocal(den[:], den[:]))
                            dve.tensor_tensor(y_tok[:, i, :].rearrange("p (g h d) -> p g h d", g=HG, h=GH), o[:, :, :, 0:DH],
                                              den[:].unsqueeze(3).to_broadcast([128, HG, GH, DH]), ALU.mult).then_inc(S("y"), 1)

                        for i in range(NT):
                            for g in range(HG):
                                n = HG * i + g
                                dve.wait_ge(S("a_scores"), n + 1)
                                if n >= 4:
                                    dve.wait_ge(S("a_out"), n - 3)
                                dve.tensor_tensor(A[:, n % 4], PS[:, 2 + n % 2, :].rearrange("p (k t) -> p k t", k=GH),
                                                  keep[:].unsqueeze(1).to_broadcast([128, GH, 128]), ALU.mult).then_inc(S("kept"), 1)
                            if i + 1 < NT:
                                dve.wait_ge(S("summed"), i + 1)
                                if i:
                                    dve.wait_ge(S("a_out"), HG * i)
                                dve.tensor_tensor(KV[:, (i + 1) % 2], PS[:, 6, :].rearrange("p (h s) -> p h s", h=H),
                                                  head_of[:].unsqueeze(2).to_broadcast([128, H, SLOT]), ALU.mult).then_inc(S("state"), 1)
                            if i:
                                normalise(i - 1)
                        normalise(NT - 1)

                    @block.scalar
                    def _(act):
                        for i in range(NT):
                            act.wait_ge(S("a_out"), HG * (i + 1))
                            if i:
                                act.wait_ge(S("O_turned"), i)
                            act.activation(O[:].rearrange("p g t -> p (g t)"), PS[:, 4 + i % 2, :], ACT.Copy).then_inc(S("O_copied"), 1)

                    @block.sync
                    def _(sp):
                        for q in range(T // QT):
                            if q >= 2:
                                sp.wait_ge(S("a_scores"), 2 * HG * (q - 1))
                            for k in range(6):
                                restack(sp, Qs[:, q % 2], 0, k, 0, H, QT * q, QT, S(f"q_in{q}"))
                                restack(sp, Ks[:, q % 2], 1, k, 0, H, QT * q, QT, S(f"k_in{q}"))
                end_phase()
                with nc.Block() as block:
                    out_projection(lambda pe: None, block, y_tok, yT, w_out1, x_tok, "o1")
                end_phase()

            with ExitStack() as tmp:
                gate = sb("gate", [128, NT, E], F32, tmp)
                gt = sb("gt", [128, NT, E, E], F32, tmp)
                eq = sb("eq", [128, NT, E, E], F32, tmp)
                rank = sb("rank", [128, NT, E], F32, tmp)
                top = sb("top", [128, NT], F32, tmp)
                gw = sb("gw", [128, NT, E], F32, tmp)
                gwT = sb("gwT", [NT * E, 128], F32, tmp)
                hid = sb("hid_e", [128, 2, 4, 512], F32, tmp)
                with nc.Block() as block:
                    jobs = [(e, j) for e in range(E) for j in range(2)]

                    @block.tensor
                    def _(pe):
                        for i in range(NT):
                            last = pe.matmul(PS[:, 7, E * i:E * i + E], xT[:, 128 * i:128 * i + 128], w_gate[:], start=True, stop=True)
                        last.then_inc(S("gates"), 1)

                        def up(n):
                            e, j = jobs[n]
                            for k in range(4):
                                if 4 * n + k >= 3:
                                    pe.wait_ge(S("e_gelu"), 4 * n + k - 2)
                                pe.matmul(PS[:, (4 * n + k) % 3, :], w_e1[:, e, 128 * k:128 * k + 128], xT[:, 512 * j:512 * j + 512], start=True, stop=True).then_inc(S("e_up"), 1)

                        def down(n):
                            e, j = jobs[n]
                            pe.wait_ge(S("e_gelu"), 4 * (n + 1))
                            for i in range(4):
                                if n >= 2 and i == 0:
                                    pe.wait_ge(S("e_added"), n - 1)
                                for k in range(4):
                                    last = pe.matmul(PS[:, 3 + n % 2, 128 * i:128 * i + 128], hid[:, n % 2, k, 128 * i:128 * i + 128], w_e2[:, e, k, :], start=(k == 0), stop=(k == 3))
                            last.then_inc(S("e_down"), 1)

                        up(0)
                        for n in range(len(jobs)):
                            if n + 1 < len(jobs):
                                up(n + 1)
                            if n == 0:
                                pe.wait_ge(S("gw"), 1)
                                pe.transpose(PS[0:NT * E, 7, 0:128], gw[:].rearrange("p i e -> p (i e)"), ident[:]).then_inc(S("gw_turned"), 1)
                                pe.wait_ge(S("gwT"), 1)
                                for i in range(NT):
                                    last = pe.matmul(PS[:, 5 + i // 4, 128 * (i % 4):128 * (i % 4) + 128], gwT[:], b_e2[:, i, :], start=True, stop=True)
                                last.then_inc(S("biased"), 1)
                            down(n)

                    @block.scalar
                    def _(act):
                        act.wait_ge(S("gate_less"), 1)
                        act.activation(gate[:], gate[:], ACT.Exp).then_inc(S("gate_exp"), 1)
                        for n, (e, j) in enumerate(jobs):
                            if n >= 2:
                                act.wait_ge(S("e_down"), n - 1)
                            for k in range(4):
                                act.wait_ge(S("e_up"), 4 * n + k + 1)
                                act.activation(hid[:, n % 2, k, :], PS[:, (4 * n + k) % 3, :], ACT.Gelu, bias=b_e1[:, e, k:k + 1]).then_inc(S("e_gelu"), 1)

                    @block.vector
                    def _(dve):
                        link = chain(dve, S("moe_dve"))
                        shape = [128, NT, E, E]
                        dve.wait_ge(S("gates"), 1)
                        link(dve.tensor_tensor(gate[:], PS[:, 7, 0:NT * E].rearrange("p (i e) -> p i e", i=NT), b_gate[:].unsqueeze(1).to_broadcast([128, NT, E]), ALU.add))
                        mine, other = gate[:].unsqueeze(3).to_broadcast(shape), gate[:].unsqueeze(2).to_broadcast(shape)
                        dve.tensor_tensor(gt[:], other, mine, ALU.is_gt)
                        link(dve.tensor_tensor(eq[:], other, mine, ALU.is_equal))
                        link(dve.tensor_tensor(eq[:].rearrange("p i e f -> p i (e f)"), eq[:].rearrange("p i e f -> p i (e f)"),
                                               tie[:].rearrange("p e f -> p (e f)").unsqueeze(1).to_broadcast([128, NT, E * E]), ALU.mult))
                        link(dve.tensor_tensor(gt[:], gt[:], eq[:], ALU.add))
                        dve.reduce_sum(rank[:], gt[:], AX.X)
                        link(dve.reduce_max(top[:], gate[:], AX.X))
                        dve.tensor_tensor(gate[:], gate[:], top[:].unsqueeze(2).to_broadcast([128, NT, E]), ALU.subtract).then_inc(S("gate_less"), 1)
                        link(dve.tensor_scalar(rank[:], rank[:], 2.0, None, ALU.is_lt))
                        dve.wait_ge(S("gate_exp"), 1)
                        link(dve.tensor_tensor(gw[:], gate[:], rank[:], ALU.mult))
                        link(dve.reduce_sum(top[:], gw[:], AX.X))
                        link(dve.reciprocal(top[:], top[:]))
                        dve.tensor_tensor(gw[:], gw[:], top[:].unsqueeze(2).to_broadcast([128, NT, E]), ALU.mult).then_inc(S("gw"), 1)
                        dve.wait_ge(S("gw_turned"), 1)
                        dve.tensor_copy(gwT[:], PS[0:NT * E, 7, 0:128]).then_inc(S("gwT"), 1)
                        dve.wait_ge(S("biased"), 1)
                        for j in range(2):
                            link(dve.tensor_tensor(x_tok[:, 4 * j:4 * j + 4, :], x_tok[:, 4 * j:4 * j + 4, :], PS[:, 5 + j, :].rearrange("p (i d) -> p i d", i=4), ALU.add))
                        for n, (e, j) in enumerate(jobs):
                            dve.wait_ge(S("e_down"), n + 1)
                            if n >= 2:
                                dve.wait_ge(S("e_added"), n - 1)
                            for k in range(4):
                                i = 4 * j + k
                                last = dve.scalar_tensor_tensor(x_tok[:, i, :], PS[:, 3 + n % 2, 128 * k:128 * k + 128], gw[:, i, e:e + 1], x_tok[:, i, :], ALU.mult, ALU.add)
                            last.then_inc(S("e_added"), 1)

                    @block.sync
                    def _(sp):
                        sp.wait_ge(S("e_added"), len(jobs))
                        sp.dma_start(out_dram[b], x_tok[:]).then_inc(S("out"), 16)
                        sp.wait_ge(S("out"), 16)
            end_phase()


def lay_out(**i):
    import numpy as np
    n = {k: np.asarray(v) for k, v in i.items()}
    rot = (np.arange(D) // DH) * DH + (np.arange(D) % DH + DH // 2) % DH
    a = {"x": n["L0_attn_x"]}
    w = n["L0_attn_W_qkv"]
    q, k, v = w[:, :D], w[:, D:2 * D], w[:, 2 * D:]
    a["w_attn0"] = np.stack([q, q[:, rot], k, k[:, rot], v], axis=1)
    a["w_out0"] = n["L0_attn_W_o"]
    q, k, v = n["L1_attn_Wq"].T, n["L1_attn_Wk"].T, n["L1_attn_Wv"].T
    a["w_attn1"] = np.stack([q, q[:, rot], k, k[:, rot], v], axis=1)
    a["w_out1"] = n["L1_attn_Wo"].T
    a["w_qkv"] = n["L0_ffn_wqkv"].transpose(1, 0, 2)
    a["w_o"] = n["L0_ffn_wo"].reshape(DEPTH, 4, 128, D).transpose(2, 0, 1, 3)
    a["w_up"] = n["L0_ffn_w1"].transpose(1, 0, 2)
    pad = np.zeros((DEPTH, 384, D), n["L0_ffn_w2"].dtype)
    pad[:, :HID] = n["L0_ffn_w2"]
    a["w_down"] = pad.reshape(DEPTH, 3, 128, D).transpose(2, 0, 1, 3)
    pad = np.zeros((DEPTH, 2, 384), n["L0_ffn_b1"].dtype)
    pad[:, :, :HID] = n["L0_ffn_b1"].reshape(DEPTH, 2, HID)
    a["b_up"] = pad.reshape(DEPTH, 2, 3, 128).transpose(3, 0, 1, 2)
    a["b_down"] = n["L0_ffn_b2"]
    a["ln_gb"] = np.stack([n["L0_ffn_ln_g"].T, n["L0_ffn_ln_b"].T], axis=2)
    qs, ks = n["L0_ffn_q_scale"], n["L0_ffn_k_scale"]
    swap = (np.arange(LD) + LD // 2) % LD
    a["scales"] = np.stack([qs, qs[:, swap], ks, ks[:, swap]], axis=1)
    a["w_gate"] = n["L1_ffn_gate_w"].T
    a["b_gate"] = n["L1_ffn_gate_b"]
    a["w_e1"] = n["L1_ffn_w1"].transpose(1, 0, 2)
    a["b_e1"] = n["L1_ffn_b1"].reshape(E, 4, 128).transpose(2, 0, 1)
    a["w_e2"] = n["L1_ffn_w2"].reshape(E, 4, 128, D).transpose(2, 0, 1, 3)
    blk = np.zeros((NT, E, NT, D), n["L1_ffn_b2"].dtype)
    for t in range(NT):
        blk[t, :, t] = n["L1_ffn_b2"]
    a["b_e2"] = blk.reshape(NT * E, NT, D)
    return {k: np.ascontiguousarray(v) for k, v in a.items()}


def kernel(**inputs):
    import numpy as _np
    import concourse.bacc as _bacc
    from concourse import mybir as _mybir
    from concourse.bass_utils import run_bass_kernel_spmd as _run

    nc = _bacc.Bacc("TRN2", target_bir_lowering=False, num_devices=1)
    arrays = {}

    def feed(tag, group):
        aps = {}
        for name, v in group.items():
            arrays[f"{tag}_{name}"] = v
            aps[name] = nc.dram_tensor(f"{tag}_{name}", v.shape, _mybir.dt.from_np(v.dtype), kind="ExternalInput").ap()
        return aps

    a = feed("in", lay_out(**inputs))
    c = feed("const", constant_arrays())
    out = nc.dram_tensor("out_0", (B, T, D), _mybir.dt.float32, kind="ExternalOutput").ap()
    build(nc, a, c, out)
    r = _run(nc, [arrays], core_ids=[0])
    return r.results[0]["out_0"]
```

```python
import math
from contextlib import ExitStack

import numpy as np
import concourse.bass as bass
from concourse import mybir

F32 = mybir.dt.float32
BF16 = mybir.dt.bfloat16
U32 = mybir.dt.uint32
ALU = mybir.AluOpType
ACT = mybir.ActivationFunctionType
AX = mybir.AxisListType

B, T, D = 4, 1024, 128
NT = T // 128
H, DH = 16, 8
HG, GH = 4, 4
SLOT = 32
DEPTH, LH, LD = 2, 8, 64
INNER = LH * LD
WIN = 64
HID = int(D * 4 * 2 / 3)
HID_CHUNKS = [(0, 128), (128, 128), (256, HID - 256)]
E, EH = 8, 512
BIG = 1e30
M_ROW = 64
Q_PART = [0, 0, 1, 1, 0, 2]
K_PART = [0, 1, 0, 1, 2, 0]


def constant_arrays():
    c = {}
    c["ident"] = np.eye(128, dtype=np.float32)
    p, j = np.arange(128)[:, None], np.arange(128)[None, :]
    tri = np.stack([np.where(j > p, -BIG, 0.0), np.where(p > j, -BIG, 0.0)], axis=1)
    c["causal"] = tri.astype(np.float32)
    c["keep"] = (j >= p).astype(np.float32)
    q = p % WIN
    allowed = (q <= j - 0) & (j <= q + WIN)
    window = np.where(allowed, 0.0, -BIG)
    first = np.where(allowed & ~((p < WIN) & (j < WIN)), 0.0, -BIG)
    c["window"] = np.stack([first, window], axis=1).astype(np.float32)
    c["head_of"] = (p // DH == np.arange(H)[None, :]).astype(np.float32)
    half = DH // 2
    theta = (np.float32(1.0) / np.float32(10000.0) ** (np.arange(half, dtype=np.float32) / np.float32(half)))
    ang = np.arange(T, dtype=np.float32)[:, None] * theta.astype(np.float32)[None, :]
    cos, sin = np.cos(ang.astype(np.float64)), np.sin(ang.astype(np.float64))
    d = np.arange(D) % DH
    c["rope"] = np.stack([cos.T[d % half], sin.T[d % half] * np.where(d < half, -1.0, 1.0)[:, None]], axis=1).astype(np.float32)
    idx = np.arange(0, LD, 2, dtype=np.float32)
    inv = (np.float32(1.0) / np.float32(10000.0) ** (idx / np.float32(LD))).astype(np.float32)
    t = np.arange(T, dtype=np.float32)
    fr = (t[:, None] * inv[None, :]).astype(np.float32)
    fr = np.concatenate([fr, fr], -1).astype(np.float64)
    base = ((idx + np.float32(0.4 * LD)) / np.float32(1.4 * LD)).astype(np.float32)
    power = ((t - T // 2) / np.float32(WIN // 2)).astype(np.float32)
    sc = base[None, :].astype(np.float64) ** power[:, None].astype(np.float64)
    sc = np.concatenate([sc, sc], -1)
    sign = np.where(np.arange(LD) < LD // 2, -1.0, 1.0)[None, :]
    tabs = np.stack([np.cos(fr) * sc * 8.0, np.sin(fr) * sc * sign * 8.0,
                     np.cos(fr) / sc, np.sin(fr) / sc * sign], axis=0)
    c["xpos"] = tabs.reshape(4, NT, 128, LD).transpose(2, 0, 1, 3).astype(np.float32).copy()
    return c


def build(nc, a, c, out):
    ctx = ExitStack()
    with ctx:
        taken = {}

        def sb(name, shape, dt=F32, where=ctx):
            taken[name] = taken.get(name, 0) + 1
            return where.enter_context(nc.sbuf_tensor(name if taken[name] == 1 else f"{name}_{taken[name]}", shape, dt))

        sems = {}

        def S(name):
            if name not in sems:
                sems[name] = ctx.enter_context(nc.semaphore(name))
            return sems[name]

        PS = ctx.enter_context(nc.psum_tensor("PS", [128, 8, 512], F32))

        parts_dram = nc.dram_tensor("parts_dram", (2, 128, 3, T), BF16, kind="Internal").ap()
        max_dram = nc.dram_tensor("max_dram", (HG, 3, GH * NT, 128), BF16, kind="Internal").ap()

        w_attn0 = sb("w_attn0", [128, 5, D])
        w_out0 = sb("w_out0", [128, D])
        w_attn1 = sb("w_attn1", [128, 5, D])
        w_out1 = sb("w_out1", [128, D])
        w_qkv = sb("w_qkv", [128, DEPTH, 3 * INNER])
        w_o = sb("w_o", [128, DEPTH, 4, D])
        w_up = sb("w_up", [128, DEPTH, 2 * HID])
        w_down = sb("w_down", [128, DEPTH, 3, D])
        b_up = sb("b_up", [128, DEPTH, 2, 3])
        b_down = sb("b_down", [128, DEPTH, D])
        ln_gb = sb("ln_gb", [128, DEPTH, 2])
        w_gate = sb("w_gate", [128, E])
        b_gate = sb("b_gate", [128, E])
        b_e1 = sb("b_e1", [128, E, 4])
        b_e2 = sb("b_e2", [NT * E, NT, D])
        ident = sb("ident", [128, 128])
        identb = sb("identb", [128, 128], BF16)
        causalb = sb("causalb", [128, 2, 128], BF16)
        keep = sb("keep", [128, 128])
        windowb = sb("windowb", [128, 2, 4, 128], BF16)
        head_of = sb("head_of", [128, H])
        rope = sb("rope", [128, 2, T])
        xpos = sb("xpos", [128, DEPTH, 4, NT, LD])
        minus_half = sb("minus_half", [128, 2 * LH])
        tie = sb("tie", [128, E, E])
        x_tok = sb("x_tok", [128, NT, D])
        xs_tok = sb("xs_tok", [128, NT, D])
        xT = sb("xT", [128, T])
        hT = sb("hT", [128, T])

        def chain(eng, sem):
            n = [0]

            def link(ins):
                n[0] += 1
                ins.then_inc(sem, 1)
                eng.wait_ge(sem, n[0])
            return link

        def end_phase():
            nc.all_engine_barrier()
            for s in sems.values():
                nc.gpsimd.sem_clear(s)
            nc.all_engine_barrier()

        with ExitStack() as tmp:
            windowf = sb("windowf", [128, 2, 128], F32, tmp)
            causalf = sb("causalf", [128, 2, 128], F32, tmp)
            xposf = sb("xposf", [128, 4, NT, LD], F32, tmp)
            scales = sb("scales", [128, DEPTH, 4, LD], F32, tmp)
            loads = [
                (w_attn0[:], a["w_attn0"]), (w_out0[:], a["w_out0"]), (w_attn1[:], a["w_attn1"]), (w_out1[:], a["w_out1"]),
                (w_qkv[:], a["w_qkv"]), (w_o[:], a["w_o"]), (w_up[:], a["w_up"]),
                (w_down[:], a["w_down"]), (b_up[:], a["b_up"]),
                (b_down[:], a["b_down"].partition_broadcast(128)), (ln_gb[:], a["ln_gb"]),
                (w_gate[:], a["w_gate"]), (b_gate[:], a["b_gate"].partition_broadcast(128)),
                (b_e1[:], a["b_e1"]), (b_e2[:], a["b_e2"]),
                (ident[:], c["ident"]), (causalf[:], c["causal"]), (keep[:], c["keep"]), (windowf[:], c["window"]),
                (head_of[:], c["head_of"]), (rope[:], c["rope"]), (xposf[:], c["xpos"]),
                (scales[:], a["scales"].partition_broadcast(128)),
            ]
            with nc.Block() as block:
                @block.sync
                def _(sp):
                    for dst, src in loads:
                        sp.dma_start(dst, src).then_inc(S("weights_in"), 16)
                    sp.wait_ge(S("weights_in"), 16 * len(loads))

                @block.gpsimd
                def _(pool):
                    pool.memset(tie[:], 1.0).then_inc(S("tie"), 1)
                    pool.wait_ge(S("tie"), 1)
                    pool.affine_select(out=tie[:], in_=tie[:], compare_op=ALU.is_gt, fill=0.0,
                                       base=0, pattern=[[1, E], [-1, E]], channel_multiplier=0).then_inc(S("tie"), 1)
                    pool.wait_ge(S("tie"), 2)
                    pool.memset(minus_half[:], -0.5)

                @block.vector
                def _(dve):
                    dve.wait_ge(S("weights_in"), 16 * len(loads))
                    dve.tensor_copy(identb[:], ident[:])
                    dve.tensor_copy(causalb[:], causalf[:])
                    for r in range(4):
                        dve.tensor_copy(windowb[:, :, r, :], windowf[:])
                    for l in range(DEPTH):
                        for k in range(4):
                            dve.tensor_tensor(xpos[:, l, k], xposf[:, k], scales[:, l, k].unsqueeze(1).to_broadcast([128, NT, LD]), ALU.mult)
        end_phase()

        def layer_norm(block, x, dst, ready, tag, before_pow=None):
            @block.vector
            def _(dve):
                link = chain(dve, S(tag + "_dve"))
                ready(dve)
                for i in range(NT):
                    last = dve.bn_stats(stats[:, i, :], x[:, i, :])
                link(last)
                for i in range(NT):
                    last = dve.bn_aggr(mean_var[:, i, :], stats[:, i, :])
                link(last)
                dve.tensor_scalar(var_eps[:], mean_var[:, :, 1], 1e-5, None, ALU.add).then_inc(S(tag + "_var"), 1)
                dve.wait_ge(S(tag + "_rstd"), 1)
                for i in range(NT):
                    dve.tensor_scalar(dst[:, i, :], x[:, i, :], mean_var[:, i, 0:1], rstd[:, i:i + 1],
                                      ALU.subtract, ALU.mult).then_inc(S(tag + "_normed"), 1)

            @block.gpsimd
            def _(pool):
                if before_pow:
                    before_pow(pool)
                pool.wait_ge(S(tag + "_var"), 1)
                pool.tensor_tensor(rstd[:], var_eps[:], minus_half[:, 0:NT], ALU.pow).then_inc(S(tag + "_rstd"), 1)

        stats = sb("stats", [128, NT, 6])
        mean_var = sb("mean_var", [128, NT, 2])
        var_eps = sb("var_eps", [128, NT])
        rstd = sb("rstd", [128, NT])

        def shifted_evac(eng, copy, bank, half, sem):
            t0 = 512 * half
            copy(hT[0:64, t0:t0 + 512], PS[0:64, bank, :])
            n = 512 if half == 0 else 511
            return copy(hT[64:128, t0 + 1:t0 + 1 + n], PS[64:128, bank, 0:n])

        def act_copy(act):
            return lambda o, i: act.activation(o, i, ACT.Copy)

        def projections(block, w, xT, phi, Vst, r_q, r_k, scr, parts, Qs, Ks):
            @block.tensor
            def _(pe):
                for n in range(4):
                    for j in range(2):
                        last = pe.matmul(PS[:, 2 * n + j, :], w[:, n, :], xT[:, 512 * j:512 * j + 512], start=True, stop=True)
                    last.then_inc(S("proj"), 1)
                pe.wait_ge(S("proj_read"), 1)
                for i in range(NT):
                    last = pe.matmul(PS[:, i // 4, 128 * (i % 4):128 * (i % 4) + 128], xT[:, 128 * i:128 * i + 128], w[:, 4, :], start=True, stop=True)
                last.then_inc(S("proj_v"), 1)
                if phi:
                    pe.wait_ge(S("rotated"), 2)
                    pe.wait_ge(S("v_out"), 1)
                    for i in range(NT):
                        last = pe.transpose(PS[:, i // 4, 128 * (i % 4):128 * (i % 4) + 128], r_k[:, 128 * i:128 * i + 128], ident[:])
                    last.then_inc(S("k_turned"), 1)

            @block.vector
            def _(dve):
                link = chain(dve, S("proj_dve"))
                for n, r in enumerate((r_q, r_k)):
                    dve.wait_ge(S("proj"), 2 * n + 1)
                    dve.tensor_tensor(scr[:, 0], PS[:, 4 * n:4 * n + 2, :].rearrange("p a b -> p (a b)"), rope[:, 0], ALU.mult).then_inc(S("proj_read"), 1)
                    dve.wait_ge(S("proj"), 2 * n + 2)
                    dve.wait_ge(S("proj_read"), n + 1)
                    link(dve.tensor_tensor(scr[:, 1], PS[:, 4 * n + 2:4 * n + 4, :].rearrange("p a b -> p (a b)"), rope[:, 1], ALU.mult))
                    if phi:
                        link(dve.tensor_tensor(r[:], scr[:, 0], scr[:, 1], ALU.add))
                        dve.tensor_scalar(scr[:, 0], r[:], 0.0, None, ALU.min).then_inc(S("phi_in"), 1)
                        dve.wait_ge(S("phi_out"), n + 1)
                        dve.scalar_tensor_tensor(r[:], r[:], 0.0, scr[:, 1], ALU.max, ALU.add).then_inc(S("rotated"), 1)
                    else:
                        dve.tensor_tensor(r[:], scr[:, 0], scr[:, 1], ALU.add).then_inc(S("rotated"), 1)
                    dve.wait_ge(S("rotated"), n + 1)
                    link(dve.tensor_copy(parts[:, n, 0], r[:]))
                    link(dve.tensor_tensor(scr[:, 0], r[:], parts[:, n, 0], ALU.subtract))
                    link(dve.tensor_copy(parts[:, n, 1], scr[:, 0]))
                    link(dve.tensor_tensor(scr[:, 1], scr[:, 0], parts[:, n, 1], ALU.subtract))
                    dve.tensor_copy(parts[:, n, 2], scr[:, 1]).then_inc(S("parts"), 1)
                    dve.wait_ge(S("parts"), n + 1)

            @block.scalar
            def _(act):
                if phi:
                    for n in range(2):
                        act.wait_ge(S("phi_in"), n + 1)
                        act.activation(scr[:, 1], scr[:, 0], ACT.Exp).then_inc(S("phi_out"), 1)
                act.wait_ge(S("proj_v"), 1)
                for j in range(2):
                    last = act.activation(Vst[:, 4 * j:4 * j + 4, :, 0:DH],
                                          PS[:, j, :].rearrange("p (i h d) -> p i h d", i=4, h=H), ACT.Copy)
                last.then_inc(S("v_out"), 1)

            @block.sync
            def _(sp):
                for n in range(2):
                    sp.wait_ge(S("parts"), n + 1)
                    sp.dma_start(parts_dram[n], parts[:, n]).then_inc(S("parts_out"), 16)
                sp.wait_ge(S("parts_out"), 32)

            @block.gpsimd
            def _(pool):
                pool.memset(Qs[:].bitcast(U32), 0)
                pool.memset(Ks[:].bitcast(U32), 0).then_inc(S("zeroed"), 1)
                pool.memset(Vst[:, :, :, DH:SLOT], 0.0).then_inc(S("zeroed"), 1)
                pool.wait_ge(S("zeroed"), 2)
                pool.memset(Vst[:, :, :, DH:DH + 1], 1.0).then_inc(S("zeroed"), 1)
                if not phi:
                    pool.wait_ge(S("zeroed"), 3)
                    pool.memset(Ks[M_ROW:M_ROW + 3], 1.0)

        def restack(sp, dst, n, g, head0, heads, t0, tn, sem):
            part = (Q_PART, K_PART)[n][g]
            src = parts_dram[n].rearrange("(h d) j t -> d h j t", d=DH)[:, head0:head0 + heads, part, t0:t0 + tn]
            sp.dma_start(dst[DH * g:DH * g + DH], src).then_inc(sem, 16)

        def out_projection(pe_wait, block, y_tok, yT, w, dst, tag):
            @block.tensor
            def _(pe):
                pe_wait(pe)
                for i in range(NT):
                    last = pe.transpose(PS[:, i // 4, 128 * (i % 4):128 * (i % 4) + 128], y_tok[:, i, :], ident[:])
                last.then_inc(S(tag + "_turned"), 1)
                pe.wait_ge(S(tag + "_yT"), 2)
                for i in range(NT):
                    last = pe.matmul(PS[:, 2 + i // 4, 128 * (i % 4):128 * (i % 4) + 128], yT[:, 128 * i:128 * i + 128], w[:], start=True, stop=True)
                last.then_inc(S(tag + "_out"), 1)

            @block.scalar
            def _(act):
                act.wait_ge(S(tag + "_turned"), 1)
                for j in range(2):
                    act.activation(yT[:, 512 * j:512 * j + 512], PS[:, j, :], ACT.Copy).then_inc(S(tag + "_yT"), 1)

            @block.vector
            def _(dve):
                dve.wait_ge(S(tag + "_out"), 1)
                for j in range(2):
                    dve.tensor_tensor(dst[:, 4 * j:4 * j + 4, :], x_tok[:, 4 * j:4 * j + 4, :],
                                      PS[:, 2 + j, :].rearrange("p (i d) -> p i d", i=4), ALU.add)

        x_dram = a["x"].rearrange("b (i p) d -> b p i d", p=128)
        out_dram = out.rearrange("b (i p) d -> b p i d", p=128)

        with nc.Fori(0, B) as b:
            with nc.Block() as block:
                @block.sync
                def _(sp):
                    sp.dma_start(x_tok[:], x_dram[b]).then_inc(S("x_in"), 16)

                layer_norm(block, x_tok, xs_tok, lambda dve: dve.wait_ge(S("x_in"), 16), "ln0")

                @block.tensor
                def _(pe):
                    for i in range(NT):
                        pe.wait_ge(S("ln0_normed"), i + 1)
                        last = pe.transpose(PS[:, i // 4, 128 * (i % 4):128 * (i % 4) + 128], xs_tok[:, i, :], ident[:])
                        if i % 4 == 3:
                            last.then_inc(S("xT_bank"), 1)

                @block.scalar
                def _(act):
                    for j in range(2):
                        act.wait_ge(S("xT_bank"), j + 1)
                        act.activation(xT[:, 512 * j:512 * j + 512], PS[:, j, :], ACT.Copy)
            end_phase()

            with ExitStack() as tmp:
                Vst = sb("Vst", [128, NT, H, SLOT], F32, tmp)
                y_tok = sb("y_tok", [128, NT, D], F32, tmp)
                Qs = sb("Qs", [128, 3, GH, T], BF16, tmp)
                Ks = sb("Ks", [128, 3, GH, T], BF16, tmp)
                with ExitStack() as tmp2:
                    scr = sb("scr", [128, 2, T], F32, tmp2)
                    r_qk = sb("r_qk", [128, T], F32, tmp2)
                    parts = sb("parts", [128, 2, 3, T], BF16, tmp2)
                    with nc.Block() as block:
                        projections(block, w_attn0, xT, False, Vst, r_qk, r_qk, scr, parts, Qs, Ks)
                    end_phase()
                NP = 8
                P = sb("P", [128, NP, 512], F32, tmp)
                O = sb("O", [128, T], F32, tmp)
                yT = sb("yT", [128, T], F32, tmp)
                mx = sb("mx", [128, 2, GH, NT, 2], F32, tmp)
                mT = sb("mT", [GH * NT, 128], F32, tmp)
                mT2 = sb("mT2", [GH * NT, 128], F32, tmp)
                m_parts = sb("m_parts", [GH * NT, 3, 128], BF16, tmp)
                den = sb("den", [128, 4, GH], F32, tmp)
                zero_rows = sb("zero_rows", [3, GH, T], BF16, tmp)

                tiles = [(i, lo, min(lo + 512, 128 * (i + 1))) for i in range(NT) for lo in range(0, 128 * (i + 1), 512)]
                units1 = [(h, *t) for h in range(GH) for t in tiles]
                blocks2 = [(i, max(lo, 128 * i), lo + 512) for i in range(NT) for lo in (0, 512) if lo + 512 > 128 * i]
                U1, U2 = len(units1), len(blocks2) * GH
                assert U1 == U2
                U = U1
                N_UNITS = HG * U
                LEAD = U + 16
                order = []
                for m in range(N_UNITS + LEAD + 12):
                    n = m - LEAD
                    if m < N_UNITS:
                        order.append(("max", m))
                    g, r = divmod(m - 3, U)
                    if r == U - 1 and 0 <= g < HG:
                        order.append(("turn_max", g))
                    if 0 <= n < N_UNITS:
                        order.append(("key", n))
                    if GH <= n and n % GH == 0 and n // GH <= N_UNITS // GH:
                        order.append(("values", n // GH - 1))
                    for j in range(2):
                        g, r = divmod(n - 6 - 4 * j, U)
                        if r == 0 and 1 <= g:
                            order.append(("turn_out", (g - 1, j)))
                with nc.Block() as block:
                    @block.tensor
                    def _(pe):
                        def max_scores(m):
                            g, u = divmod(m, U)
                            h, i, lo, hi = units1[u]
                            if u == 0:
                                pe.wait_ge(S(f"q_in{g}"), 16 * 7)
                                pe.wait_ge(S(f"k_in{g}"), 16 * 6)
                            if m >= 3:
                                pe.wait_ge(S("max_read"), m - 2)
                            diag = hi == 128 * (i + 1)
                            last = pe.matmul(PS[:, m % 3, 0:hi - lo], Qs[:, g % 3, h, 128 * i:128 * i + 128], Ks[:, g % 3, h, lo:hi],
                                             start=True, stop=not diag)
                            if diag:
                                last = pe.matmul(PS[:, m % 3, hi - lo - 128:hi - lo], identb[:], causalb[:, 0, :], start=False, stop=True)
                            last.then_inc(S("max_scores"), 1)

                        def key_scores(n):
                            g, u = divmod(n, U)
                            (i, lo, hi), h = blocks2[u // GH], u % GH
                            if u == 0:
                                pe.wait_ge(S("m_in"), 16 * (g + 1))
                            if n >= 2:
                                pe.wait_ge(S("exp"), n - 1)
                            diag = lo == 128 * i
                            last = pe.matmul(PS[:, 3 + n % 2, 0:hi - lo], Ks[:, g % 3, h, 128 * i:128 * i + 128], Qs[:, g % 3, h, lo:hi],
                                             start=True, stop=not diag)
                            if diag:
                                last = pe.matmul(PS[:, 3 + n % 2, 0:128], identb[:], causalb[:, 1, :], start=False, stop=True)
                            last.then_inc(S("key_scores"), 1)

                        def values(v):
                            g, k = divmod(v, len(blocks2))
                            i, lo, hi = blocks2[k]
                            pe.wait_ge(S("exp"), GH * (v + 1))
                            if k == 0 and g:
                                pe.wait_ge(S("O_copied"), g)
                            bank = lo // 512
                            for h in range(GH):
                                last = pe.matmul(PS[SLOT * h:SLOT * h + SLOT, 5 + bank, lo - 512 * bank:hi - 512 * bank],
                                                 Vst[:, i, GH * g + h, :], P[:, (GH * v + h) % NP, 0:hi - lo],
                                                 start=(i == 0), stop=(i == (3, NT - 1)[bank]))
                            last.then_inc(S("values"), 1)

                        def turn_max(g):
                            pe.wait_ge(S("mx"), g + 1)
                            if g == 1:
                                pe.wait_ge(S("mT_read"), 1)
                            if g >= 2:
                                pe.wait_ge(S("y"), 2 * (g - 1))
                            pe.transpose(PS[0:GH * NT, 7, 0:128], mx[:, g % 2, :, :, 0], ident[:]).then_inc(S("m_turned"), 1)

                        def turn_out(g, j):
                            pe.wait_ge(S("O_copied"), g + 1)
                            pe.wait_ge(S("mT_read"), min(g + 2, HG))
                            if 2 * g + j:
                                pe.wait_ge(S("y"), 2 * g + j)
                            for k in range(4):
                                i = 4 * j + k
                                last = pe.transpose(PS[:, 7, 128 * k:128 * k + 128], O[:, 128 * i:128 * i + 128], ident[:])
                            last.then_inc(S("O_turned"), 1)

                        for step, k in order:
                            if step == "max":
                                max_scores(k)
                            elif step == "key":
                                key_scores(k)
                            elif step == "values":
                                values(k)
                            elif step == "turn_max":
                                turn_max(k)
                            else:
                                turn_out(*k)

                    @block.vector
                    def _(dve):
                        link = chain(dve, S("attn_dve"))

                        def maxima(m):
                            g, u = divmod(m, U)
                            h, i, lo, hi = units1[u]
                            if u == 0 and g >= 2:
                                dve.wait_ge(S("m_turned"), g - 1)
                            dve.wait_ge(S("max_scores"), m + 1)
                            dve.reduce_max(mx[:, g % 2, h, i, lo // 512:lo // 512 + 1], PS[:, m % 3, 0:hi - lo], AX.X).then_inc(S("max_read"), 1)

                        def join(g):
                            dve.wait_ge(S("max_read"), (g + 1) * U)
                            dve.tensor_tensor(mx[:, g % 2, :, 4:, 0], mx[:, g % 2, :, 4:, 0], mx[:, g % 2, :, 4:, 1], ALU.max).then_inc(S("mx"), 1)

                        def split(g):
                            dve.wait_ge(S("m_turned"), g + 1)
                            if g:
                                dve.wait_ge(S("m_out"), 16 * g)
                            link(dve.tensor_scalar(mT[:], PS[0:GH * NT, 7, 0:128], -1.0, None, ALU.mult))
                            dve.tensor_copy(m_parts[:, 0], mT[:]).then_inc(S("mT_read"), 1)
                            dve.wait_ge(S("mT_read"), g + 1)
                            link(dve.tensor_tensor(mT2[:], mT[:], m_parts[:, 0], ALU.subtract))
                            link(dve.tensor_copy(m_parts[:, 1], mT2[:]))
                            link(dve.tensor_tensor(mT[:], mT2[:], m_parts[:, 1], ALU.subtract))
                            dve.tensor_copy(m_parts[:, 2], mT[:]).then_inc(S("m_parts"), 1)
                            dve.wait_ge(S("m_parts"), g + 1)

                        def normalise(g, j):
                            dve.wait_ge(S("O_turned"), 2 * g + j + 1)
                            o = PS[:, 7, :].rearrange("p (i h s) -> p i h s", i=4, h=GH)
                            link(dve.reciprocal(den[:], o[:, :, :, DH]))
                            dve.tensor_tensor(y_tok[:, 4 * j:4 * j + 4, 32 * g:32 * g + 32].rearrange("p i (h d) -> p i h d", h=GH),
                                              o[:, :, :, 0:DH], den[:].unsqueeze(3).to_broadcast([128, 4, GH, DH]), ALU.mult).then_inc(S("y"), 1)
                            dve.wait_ge(S("y"), 2 * g + j + 1)

                        for step, k in order:
                            if step == "max":
                                maxima(k)
                                if k % U == U - 1:
                                    join(k // U)
                            elif step == "turn_max":
                                split(k)
                            elif step == "turn_out":
                                normalise(*k)

                    @block.scalar
                    def _(act):
                        def copy_out(act, g):
                            act.wait_ge(S("values"), (g + 1) * len(blocks2))
                            if g:
                                act.wait_ge(S("O_turned"), 2 * g)
                            act.activation(O[:], PS[:, 5:7, :].rearrange("p a b -> p (a b)"), ACT.Copy).then_inc(S("O_copied"), 1)

                        for n in range(N_UNITS):
                            g, u = divmod(n, U)
                            i, lo, hi = blocks2[u // GH]
                            if u == 2 and g:
                                copy_out(act, g - 1)
                            act.wait_ge(S("key_scores"), n + 1)
                            if n >= NP:
                                act.wait_ge(S("values"), (n - NP) // GH + 1)
                            act.activation(P[:, n % NP, 0:hi - lo], PS[:, 3 + n % 2, 0:hi - lo], ACT.Exp,
                                           scale=1.0 / math.sqrt(DH)).then_inc(S("exp"), 1)
                        copy_out(act, HG - 1)

                    @block.gpsimd
                    def _(pool):
                        pool.memset(zero_rows[:], 0.0).then_inc(S("zero_rows"), 1)

                    @block.sync
                    def _(sp):
                        def stack(g):
                            if g >= 3:
                                sp.wait_ge(S("key_scores"), (g - 2) * U)
                            sp.dma_start(Qs[M_ROW:M_ROW + 3, g % 3], zero_rows[:]).then_inc(S(f"q_in{g}"), 16)
                            for k in range(6):
                                restack(sp, Qs[:, g % 3], 0, k, GH * g, GH, 0, T, S(f"q_in{g}"))
                                restack(sp, Ks[:, g % 3], 1, k, GH * g, GH, 0, T, S(f"k_in{g}"))

                        sp.wait_ge(S("zero_rows"), 1)
                        for g in range(3):
                            stack(g)
                        for g in range(HG):
                            sp.wait_ge(S("m_parts"), g + 1)
                            sp.dma_start(max_dram[g].rearrange("j r t -> r j t"), m_parts[:]).then_inc(S("m_out"), 16)
                            sp.wait_ge(S("m_out"), 16 * (g + 1))
                            sp.dma_start(Qs[M_ROW:M_ROW + 3, g % 3], max_dram[g].rearrange("j (h i) t -> j h (i t)", h=GH)).then_inc(S("m_in"), 16)
                            if g == 1:
                                stack(3)
                end_phase()
                with nc.Block() as block:
                    out_projection(lambda pe: None, block, y_tok, yT, w_out0, x_tok, "o0")
                end_phase()

            for l in range(DEPTH):
                with ExitStack() as tmp:
                    NV = 4
                    raw = sb("raw", [128, 2, 3, INNER], F32, tmp)
                    sq = sb("sq", [128, 2, INNER], F32, tmp)
                    ra = sb("ra", [128, 2, INNER], F32, tmp)
                    rb = sb("rb", [128, 2, INNER], F32, tmp)
                    ss = sb("ss", [128, 2, LH], F32, tmp)
                    nrm = sb("nrm", [128, 2, LH], F32, tmp)
                    qk = sb("qk", [128, 2, INNER], F32, tmp)
                    qT = sb("qT", [128, 2, 4, 128], F32, tmp)
                    kT = sb("kT", [128, 4, WIN + T], F32, tmp)
                    V_A = sb("V_A", [128, NV, LH, LD + 1], F32, tmp)
                    V_B = sb("V_B", [128, NV, LH, LD + 1], F32, tmp)
                    sm = sb("sm", [128, 2, LH, 128], F32, tmp)
                    PT = sb("PT", [128, LH, 128], F32, tmp)
                    mxl = sb("mxl", [128, LH], F32, tmp)
                    rd = sb("rd", [128, LH], F32, tmp)
                    o_tok = sb("o_tok", [128, INNER], F32, tmp)
                    oT = sb("oT", [128, 4, 128], F32, tmp)
                    with nc.Block() as block:
                        OUT_BANK = {0: 7, 1: 2}

                        def low_uses(i):
                            return (i - 1) // NV + 1 if i % NV else i // NV

                        @block.tensor
                        def _(pe):
                            for i in range(NT):
                                pe.transpose(PS[:, i // 4, 128 * (i % 4):128 * (i % 4) + 128], xs_tok[:, i, :], ident[:]).then_inc(S("h_turned"), 1)

                            def project_qk(i):
                                if i == 0:
                                    pe.wait_ge(S("set"), 1)
                                    pe.wait_ge(S("hT"), 2)
                                else:
                                    pe.wait_ge(S("raw_qk"), i)
                                for n in range(2):
                                    last = pe.matmul(PS[:, n, :], hT[:, 128 * i:128 * i + 128], w_qkv[:, l, INNER * n:INNER * n + INNER], start=True, stop=True)
                                last.then_inc(S("qk_made"), 1)

                            def project_v(i):
                                if i:
                                    pe.wait_ge(S("raw_v"), i)
                                if i >= 4:
                                    pe.wait_ge(S("o"), i - 3)
                                pe.matmul(PS[:, 2, :], hT[:, 128 * i:128 * i + 128], w_qkv[:, l, 2 * INNER:3 * INNER], start=True, stop=True).then_inc(S("v_made"), 1)

                            def turn_o(i):
                                pe.wait_ge(S("o"), i + 1)
                                for k in range(4):
                                    last = pe.transpose(PS[:, 3, 128 * k:128 * k + 128], o_tok[:, 128 * k:128 * k + 128], ident[:])
                                last.then_inc(S("o_turned"), 1)

                            def turn_p(g, i):
                                if g == 1:
                                    pe.wait_ge(S("p"), i + 1)
                                elif i >= 1:
                                    pe.wait_ge(S("o_features"), i)
                                for k in range(4):
                                    last = pe.transpose(PS[:, 3 + g, 128 * k:128 * k + 128], sm[:, i % 2, 4 * g + k, :], ident[:])
                                last.then_inc(S(f"turned_p{g}"), 1)

                            def turn_qk(n, i):
                                if n == 1:
                                    pe.wait_ge(S("qk"), i + 1)
                                if i >= 2:
                                    pe.wait_ge(S(f"p_features{n}"), i - 1)
                                for k in range(4):
                                    last = pe.transpose(PS[:, 3 + n, 128 * k:128 * k + 128], qk[:, n, 128 * k:128 * k + 128], ident[:])
                                last.then_inc(S(f"turned_qk{n}"), 1)

                            def back(i):
                                pe.wait_ge(S("o_features"), i + 1)
                                if i:
                                    pe.wait_ge(S("xs"), i)
                                for k in range(4):
                                    last = pe.matmul(PS[:, 7, 512 - D:512], oT[:, k, :], w_o[:, l, k, :], start=(k == 0), stop=(k == 3))
                                last.then_inc(S("back"), 1)

                            def scores(i):
                                for n in range(2):
                                    pe.wait_ge(S(f"qk_features{n}"), i + 1)
                                if i:
                                    pe.wait_ge(S("less_max"), i)
                                for g in range(2):
                                    pe.matmul(PS[:, 5 + g, :], identb[:], windowb[:, min(i, 1)].rearrange("p r j -> p (r j)"), start=True, stop=False, skip_group_check=True)
                                for k in range(4):
                                    for w in range(2):
                                        for g in range(2):
                                            last = pe.matmul(PS[64 * w:64 * w + 64, 5 + g, 128 * k:128 * k + 128],
                                                             qT[LD * g:LD * g + LD, i % 2, k, 64 * w:64 * w + 64],
                                                             kT[LD * g:LD * g + LD, k, 128 * i + 64 * w:128 * i + 64 * w + 128],
                                                             start=False, stop=(k == 3), skip_group_check=True)
                                            if k == 3 and w == 1:
                                                last.then_inc(S("scores"), 1)

                            def values(g, i):
                                if g == 1:
                                    pe.wait_ge(S(f"v_in{i % NV}"), 32 * (i // NV + 1))
                                    if i:
                                        pe.wait_ge(S(f"v_low{i % NV}"), 16 * low_uses(i))
                                    pe.wait_ge(S("raw_v"), min(i + 4, NT))
                                elif i:
                                    pe.wait_ge(S("o"), i)
                                pe.wait_ge(S(f"p_features{g}"), i + 1)
                                for k in range(4):
                                    for w, V in ((0, V_B), (1, V_A)):
                                        last = pe.matmul(PS[64 * w:64 * w + 64, OUT_BANK[g], (LD + 1) * k:(LD + 1) * (k + 1)],
                                                         PT[:, 4 * g + k, 64 * w:64 * w + 64], V[:, i % NV, 2 * k + g, :], start=True, stop=True)
                                last.then_inc(S("pv"), 1)

                            for i in range(2):
                                project_qk(i)
                                project_v(i)
                            turn_qk(1, 0)
                            turn_qk(0, 0)
                            for s in range(NT + 2):
                                if s + 2 < NT:
                                    project_qk(s + 2)
                                if s < NT:
                                    scores(s)
                                if 1 <= s <= NT:
                                    turn_p(1, s - 1)
                                if s >= 2:
                                    turn_o(s - 2)
                                if s + 2 < NT:
                                    project_v(s + 2)
                                if 1 <= s <= NT:
                                    turn_p(0, s - 1)
                                if s + 1 < NT:
                                    turn_qk(1, s + 1)
                                if s >= 2:
                                    back(s - 2)
                                if 1 <= s <= NT:
                                    values(1, s - 1)
                                if s + 1 < NT:
                                    turn_qk(0, s + 1)
                                if 1 <= s <= NT:
                                    values(0, s - 1)

                        @block.scalar
                        def _(act):
                            for j in range(2):
                                act.wait_ge(S("h_turned"), 4 * (j + 1))
                                shifted_evac(act, act_copy(act), j, j, None).then_inc(S("hT"), 1)

                            def raw_qk(i):
                                act.wait_ge(S("qk_made"), i + 1)
                                if i >= 2:
                                    act.wait_ge(S("rot"), 2 * (i - 1))
                                act.activation(raw[:, i % 2, 0:2].rearrange("p n d -> p (n d)"), PS[:, 0:2, :].rearrange("p n d -> p (n d)"), ACT.Copy).then_inc(S("raw_qk"), 1)
                                act.wait_ge(S("raw_qk"), i + 1)
                                if i:
                                    act.wait_ge(S("ss"), i)
                                act.activation(sq[:], raw[:, i % 2, 0:2], ACT.Square).then_inc(S("sq"), 1)

                            def raw_v(i):
                                act.wait_ge(S("v_made"), i + 1)
                                if i >= 2:
                                    act.wait_ge(S(f"v_in{(i - 2) % NV}"), 32 * ((i - 2) // NV + 1))
                                    act.wait_ge(S(f"v_low{(i - 1) % NV}"), 16 * low_uses(i - 1))
                                act.activation(raw[:, i % 2, 2], PS[:, 2, :], ACT.Copy).then_inc(S("raw_v"), 1)

                            def weights_out(g, i):
                                act.wait_ge(S(f"turned_p{g}"), i + 1)
                                act.activation(PT[:, 4 * g:4 * g + 4].rearrange("p k t -> p (k t)"), PS[:, 3 + g, :], ACT.Copy).then_inc(S(f"p_features{g}"), 1)

                            def q_out(i):
                                act.wait_ge(S("turned_qk0"), i + 1)
                                act.activation(qT[:, i % 2].rearrange("p k t -> p (k t)"), PS[:, 3, :], ACT.Copy).then_inc(S("qk_features0"), 1)

                            def k_out(i):
                                act.wait_ge(S("turned_qk1"), i + 1)
                                act.activation(kT[:, :, WIN + 128 * i:WIN + 128 * i + 128], PS[:, 4, :].rearrange("p (k t) -> p k t", k=4), ACT.Copy).then_inc(S("qk_features1"), 1)

                            for i in range(2):
                                raw_qk(i)
                                raw_v(i)
                            k_out(0)
                            q_out(0)
                            for s in range(NT + 2):
                                if s + 2 < NT:
                                    raw_qk(s + 2)
                                if 1 <= s <= NT:
                                    weights_out(1, s - 1)
                                if s >= 2:
                                    act.wait_ge(S("o_turned"), s - 1)
                                    act.activation(oT[:].rearrange("p k t -> p (k t)"), PS[:, 3, :], ACT.Copy).then_inc(S("o_features"), 1)
                                if s + 2 < NT:
                                    raw_v(s + 2)
                                if 1 <= s <= NT:
                                    weights_out(0, s - 1)
                                if s + 1 < NT:
                                    k_out(s + 1)
                                if s < NT:
                                    act.wait_ge(S("less_max"), s + 1)
                                    act.activation(sm[:, s % 2], sm[:, s % 2], ACT.Exp).then_inc(S("p"), 1)
                                if s + 1 < NT:
                                    q_out(s + 1)

                        @block.vector
                        def _(dve):
                            link = chain(dve, S("local_dve"))
                            dve.memset(kT[:, :, 0:WIN], 0.0)
                            dve.memset(V_B[0:64, 0, :, 0:LD], 0.0)
                            dve.memset(hT[64:128, 0:1], 0.0)
                            for V in (V_A, V_B):
                                last = dve.memset(V[:, :, :, LD:LD + 1], 1.0)
                            last.then_inc(S("set"), 1)

                            def rotate(i):
                                dve.wait_ge(S("sq"), i + 1)
                                dve.reduce_sum(ss[:], sq[:].rearrange("p n (h d) -> p n h d", h=LH), AX.X).then_inc(S("ss"), 1)
                                if i:
                                    dve.wait_ge(S("qk"), i)
                                for n in range(2):
                                    x = raw[:, i % 2, n].rearrange("p (h a d) -> p h a d", h=LH, a=2)
                                    cos = xpos[:, l, 2 * n, i].unsqueeze(1).to_broadcast([128, LH, LD])
                                    sin = xpos[:, l, 2 * n + 1, i].rearrange("p (a d) -> p a d", a=2).unsqueeze(1).to_broadcast([128, LH, 2, LD // 2])
                                    dve.tensor_tensor(ra[:, n].rearrange("p (h d) -> p h d", h=LH), raw[:, i % 2, n].rearrange("p (h d) -> p h d", h=LH), cos, ALU.mult)
                                    dve.tensor_tensor(rb[:, n].rearrange("p (h a d) -> p h a d", h=LH, a=2), x[:, :, ::-1, :], sin, ALU.mult).then_inc(S("rot"), 1)
                                dve.wait_ge(S("rot"), 2 * (i + 1))
                                link(dve.tensor_tensor(ra[:], ra[:], rb[:], ALU.add))
                                dve.wait_ge(S("nrm"), i + 1)
                                if i:
                                    dve.wait_ge(S("turned_qk0"), i)
                                dve.tensor_tensor(qk[:].rearrange("p n (h d) -> p (n h) d", h=LH), ra[:].rearrange("p n (h d) -> p (n h) d", h=LH),
                                                  nrm[:].rearrange("p n h -> p (n h)").unsqueeze(2).to_broadcast([128, 2 * LH, LD]), ALU.mult).then_inc(S("qk"), 1)

                            def less_max(i):
                                if i >= 2:
                                    dve.wait_ge(S("turned_p0"), i - 1)
                                for g in range(2):
                                    dve.wait_ge(S("scores"), 2 * i + 2)
                                    s = PS[:, 5 + g, :].rearrange("p (k j) -> p k j", k=4)
                                    link(dve.reduce_max(mxl[:, 4 * g:4 * g + 4], s, AX.X))
                                    last = dve.tensor_tensor(sm[:, i % 2, 4 * g:4 * g + 4, :], s, mxl[:, 4 * g:4 * g + 4].unsqueeze(2).to_broadcast([128, 4, 128]), ALU.subtract)
                                last.then_inc(S("less_max"), 1)

                            def over_sum(i):
                                if i:
                                    dve.wait_ge(S("o_turned"), i)
                                for g in (1, 0):
                                    dve.wait_ge(S("pv"), 2 * i + 2 - g)
                                    o = PS[:, OUT_BANK[g], 0:4 * (LD + 1)].rearrange("p (k s) -> p k s", k=4)
                                    link(dve.reciprocal(rd[:, 4 * g:4 * g + 4], o[:, :, LD]))
                                    last = dve.tensor_tensor(o_tok[:].rearrange("p (k g d) -> p k g d", k=4, g=2)[:, :, g, :], o[:, :, 0:LD],
                                                             rd[:, 4 * g:4 * g + 4].unsqueeze(2).to_broadcast([128, 4, LD]), ALU.mult)
                                last.then_inc(S("o"), 1)

                            rotate(0)
                            rotate(1)
                            for s in range(NT + 2):
                                if s < NT:
                                    less_max(s)
                                if s + 2 < NT:
                                    rotate(s + 2)
                                if 1 <= s <= NT:
                                    over_sum(s - 1)
                                if s >= 2:
                                    dve.wait_ge(S("back"), s - 1)
                                    dve.tensor_tensor(xs_tok[:, s - 2, :], xs_tok[:, s - 2, :], PS[:, 7, 512 - D:512], ALU.add).then_inc(S("xs"), 1)

                        @block.gpsimd
                        def _(pool):
                            for i in range(NT):
                                pool.wait_ge(S("ss"), i + 1)
                                if i:
                                    pool.wait_ge(S("qk"), i)
                                pool.tensor_scalar(nrm[:], ss[:], 1e-24, None, ALU.max).then_inc(S("norm2"), 1)
                                pool.wait_ge(S("norm2"), i + 1)
                                pool.tensor_tensor(nrm[:].rearrange("p n h -> p (n h)"), nrm[:].rearrange("p n h -> p (n h)"), minus_half[:, 0:2 * LH], ALU.pow).then_inc(S("nrm"), 1)

                        @block.sync
                        def _(sp):
                            sp.wait_ge(S("set"), 1)
                            for i in range(NT):
                                sp.wait_ge(S("raw_v"), i + 1)
                                v = raw[:, i % 2, 2].rearrange("p (h d) -> p h d", h=LH)
                                if i >= NV:
                                    sp.wait_ge(S("pv"), 2 * (i - NV + 1))
                                sp.dma_start(V_A[:, i % NV, :, 0:LD], v).then_inc(S(f"v_in{i % NV}"), 16)
                                sp.dma_start(V_B[64:128, i % NV, :, 0:LD], v[0:64]).then_inc(S(f"v_in{i % NV}"), 16)
                                if i + 1 < NT:
                                    if i + 1 >= NV:
                                        sp.wait_ge(S("pv"), 2 * (i + 2 - NV))
                                    sp.dma_start(V_B[0:64, (i + 1) % NV, :, 0:LD], v[64:128]).then_inc(S(f"v_low{(i + 1) % NV}"), 16)
                    end_phase()

                with ExitStack() as tmp:
                    hs = sb("hs", [128, NT, D], F32, tmp)
                    hn = sb("hn", [128, T], F32, tmp)
                    gl = sb("gl", [128, 2, 512], F32, tmp)
                    hid = sb("hid", [128, 3, T], F32, tmp)
                    with nc.Block() as block:
                        @block.sync
                        def _(sp):
                            sp.dma_start(hs[1:128, :, 64:], xs_tok[0:127, :, 64:]).then_inc(S("shift"), 16)
                            sp.dma_start(hs[0:1, 1:, 64:], xs_tok[127:128, 0:NT - 1, 64:]).then_inc(S("shift"), 16)

                        def first_token(pool):
                            pool.memset(hs[0:1, 0, 64:], 0.0).then_inc(S("first"), 1)

                        def ready(dve):
                            link = chain(dve, S("hs_dve"))
                            link(dve.tensor_copy(hs[:, :, 0:64], xs_tok[:, :, 0:64]))
                            dve.wait_ge(S("first"), 1)
                            dve.wait_ge(S("shift"), 32)

                        layer_norm(block, hs, hs, ready, "lnf", first_token)

                        @block.tensor
                        def _(pe):
                            for i in range(NT):
                                pe.wait_ge(S("lnf_normed"), i + 1)
                                last = pe.transpose(PS[:, i // 4, 128 * (i % 4):128 * (i % 4) + 128], hs[:, i, :], ident[:])
                                if i % 4 == 3:
                                    last.then_inc(S("hn_turned"), 1)

                            def up(n):
                                j, (c0, cw) = n // 3, HID_CHUNKS[n % 3]
                                pe.wait_ge(S("hn"), j + 1)
                                if n >= 2:
                                    pe.wait_ge(S("hid"), n - 1)
                                for k in range(2):
                                    last = pe.matmul(PS[0:cw, 2 + 2 * (n % 2) + k, :], w_up[:, l, HID * k + c0:HID * k + c0 + cw], hn[:, 512 * j:512 * j + 512], start=True, stop=True)
                                last.then_inc(S("up"), 1)

                            def down(j):
                                pe.wait_ge(S("hid"), 3 * (j + 1))
                                for k in range(4):
                                    i = 4 * j + k
                                    for n, (c0, cw) in enumerate(HID_CHUNKS):
                                        last = pe.matmul(PS[:, 6 + j, 128 * k:128 * k + 128], hid[0:cw, n, 128 * i:128 * i + 128], w_down[0:cw, l, n, :], start=(n == 0), stop=(n == 2))
                                last.then_inc(S("down"), 1)

                            for n in range(5):
                                up(n)
                            down(0)
                            up(5)
                            down(1)

                        @block.scalar
                        def _(act):
                            for n in range(6):
                                cw = HID_CHUNKS[n % 3][1]
                                act.wait_ge(S("up"), n + 1)
                                if n >= 2:
                                    act.wait_ge(S("hid"), n - 1)
                                act.activation(gl[0:cw, n % 2, :], PS[0:cw, 3 + 2 * (n % 2), :], ACT.Gelu, bias=b_up[0:cw, l, 1, n % 3:n % 3 + 1]).then_inc(S("gelu"), 1)

                        @block.vector
                        def _(dve):
                            for j in range(2):
                                dve.wait_ge(S("hn_turned"), j + 1)
                                dve.tensor_scalar(hn[:, 512 * j:512 * j + 512], PS[:, j, :], ln_gb[:, l, 0:1], ln_gb[:, l, 1:2], ALU.mult, ALU.add).then_inc(S("hn"), 1)
                            dve.tensor_tensor(xs_tok[:], xs_tok[:], b_down[:, l].unsqueeze(1).to_broadcast([128, NT, D]), ALU.add).then_inc(S("xb"), 1)
                            for n in range(6):
                                j, cw = n // 3, HID_CHUNKS[n % 3][1]
                                dve.wait_ge(S("gelu"), n + 1)
                                dve.scalar_tensor_tensor(hid[0:cw, n % 3, 512 * j:512 * j + 512], PS[0:cw, 2 + 2 * (n % 2), :], b_up[0:cw, l, 0, n % 3:n % 3 + 1],
                                                         gl[0:cw, n % 2, :], ALU.add, ALU.mult).then_inc(S("hid"), 1)
                            dve.wait_ge(S("xb"), 1)
                            for j in range(2):
                                dve.wait_ge(S("down"), j + 1)
                                dve.tensor_tensor(xs_tok[:, 4 * j:4 * j + 4, :], xs_tok[:, 4 * j:4 * j + 4, :], PS[:, 6 + j, :].rearrange("p (i d) -> p i d", i=4), ALU.add)
                    end_phase()

            with nc.Block() as block:
                def both(dve):
                    link = chain(dve, S("both"))
                    link(dve.tensor_tensor(x_tok[:], x_tok[:], xs_tok[:], ALU.add))

                layer_norm(block, x_tok, xs_tok, both, "ln1")

                @block.tensor
                def _(pe):
                    for i in range(NT):
                        pe.wait_ge(S("ln1_normed"), i + 1)
                        last = pe.transpose(PS[:, i // 4, 128 * (i % 4):128 * (i % 4) + 128], xs_tok[:, i, :], ident[:])
                        if i % 4 == 3:
                            last.then_inc(S("xT_bank"), 1)

                @block.scalar
                def _(act):
                    for j in range(2):
                        act.wait_ge(S("xT_bank"), j + 1)
                        act.activation(xT[:, 512 * j:512 * j + 512], PS[:, j, :], ACT.Copy)
            end_phase()

            with ExitStack() as second:
                w_e1 = sb("w_e1", [128, E, EH], F32, second)
                w_e2 = sb("w_e2", [128, E, 4, D], F32, second)

                with ExitStack() as tmp:
                    Vst = sb("Vst1", [128, NT, H, SLOT], F32, tmp)
                    r_q = sb("r_q", [128, T], F32, tmp)
                    r_k = sb("r_k", [128, T], F32, tmp)
                    y_tok = sb("y_tok1", [128, NT, D], F32, tmp)
                    QT = 256
                    Qs = sb("Qs1", [128, 2, H, QT], BF16, tmp)
                    Ks = sb("Ks1", [128, 2, H, QT], BF16, tmp)
                    with ExitStack() as tmp2:
                        scr = sb("scr1", [128, 2, T], F32, tmp2)
                        parts = sb("parts1", [128, 2, 3, T], BF16, tmp2)
                        with nc.Block() as block:
                            projections(block, w_attn1, xT, True, Vst, r_q, r_k, scr, parts, Qs, Ks)
                        end_phase()
                    k_tok = sb("k_tok", [128, NT, D], F32, tmp)
                    A = sb("A", [128, 4, GH, 128], F32, tmp)
                    KV = sb("KV", [128, 2, H, SLOT], F32, tmp)
                    O = sb("O1", [128, HG, 128], F32, tmp)
                    den = sb("den1", [128, HG, GH], F32, tmp)
                    yT = sb("yT1", [128, T], F32, tmp)
                    with nc.Block() as block:
                        @block.tensor
                        def _(pe):
                            def chunk_scores(i, g):
                                n = HG * i + g
                                if g == 0 and i % 2 == 0:
                                    pe.wait_ge(S(f"q_in{i // 2}"), 16 * 6)
                                    pe.wait_ge(S(f"k_in{i // 2}"), 16 * 6)
                                if n >= 2:
                                    pe.wait_ge(S("kept"), n - 1)
                                for k in range(GH):
                                    t0 = 128 * (i % 2)
                                    last = pe.matmul(PS[:, 2 + n % 2, 128 * k:128 * k + 128], Ks[:, i // 2 % 2, GH * g + k, t0:t0 + 128],
                                                     Qs[:, i // 2 % 2, GH * g + k, t0:t0 + 128], start=True, stop=True)
                                last.then_inc(S("a_scores"), 1)

                            def chunk_out(i, g):
                                n = HG * i + g
                                if g == 0 and i >= 2:
                                    pe.wait_ge(S("O_copied"), i - 1)
                                if i:
                                    if g == 0:
                                        pe.wait_ge(S("state"), i)
                                    pe.matmul(PS[:, 4 + i % 2, 128 * g:128 * g + 128], KV[:, i % 2, GH * g:GH * g + GH, :].rearrange("p h s -> p (h s)"),
                                              r_q[:, 128 * i:128 * i + 128], start=True, stop=False, skip_group_check=True)
                                pe.wait_ge(S("kept"), n + 1)
                                for k in range(GH):
                                    last = pe.matmul(PS[SLOT * k:SLOT * k + SLOT, 4 + i % 2, 128 * g:128 * g + 128], Vst[:, i, GH * g + k, :], A[:, n % 4, k, :],
                                                     start=(i == 0), stop=True, skip_group_check=True)
                                last.then_inc(S("a_out"), 1)

                            def state(i):
                                pe.wait_ge(S("k_tok"), 1)
                                if i:
                                    pe.wait_ge(S("state"), i)
                                pe.matmul(PS[:, 6, :], k_tok[:, i, :], Vst[:, i].rearrange("p h s -> p (h s)"), start=(i == 0), stop=True, skip_group_check=True).then_inc(S("summed"), 1)

                            def turn_out(i):
                                pe.wait_ge(S("O_copied"), i + 1)
                                if i:
                                    pe.wait_ge(S("y"), i)
                                for g in range(HG):
                                    last = pe.transpose(PS[:, 7, 128 * g:128 * g + 128], O[:, g, :], ident[:])
                                last.then_inc(S("O_turned"), 1)

                            for i in range(NT):
                                chunk_scores(i, 0)
                                for g in range(HG):
                                    if g + 1 < HG:
                                        chunk_scores(i, g + 1)
                                    chunk_out(i, g)
                                if i + 1 < NT:
                                    state(i)
                                if i:
                                    turn_out(i - 1)
                            turn_out(NT - 1)

                        @block.vector
                        def _(dve):
                            link = chain(dve, S("lin_dve"))
                            for j in range(2):
                                last = dve.tensor_copy(k_tok[:, 4 * j:4 * j + 4, :], PS[:, j, :].rearrange("p (i d) -> p i d", i=4))
                            last.then_inc(S("k_tok"), 1)

                            def normalise(i):
                                dve.wait_ge(S("O_turned"), i + 1)
                                o = PS[:, 7, :].rearrange("p (g h s) -> p g h s", g=HG, h=GH)
                                link(dve.tensor_scalar(den[:], o[:, :, :, DH], 1e-6, None, ALU.max))
                                link(dve.reciprocal(den[:], den[:]))
                                dve.tensor_tensor(y_tok[:, i, :].rearrange("p (g h d) -> p g h d", g=HG, h=GH), o[:, :, :, 0:DH],
                                                  den[:].unsqueeze(3).to_broadcast([128, HG, GH, DH]), ALU.mult).then_inc(S("y"), 1)

                            for i in range(NT):
                                for g in range(HG):
                                    n = HG * i + g
                                    dve.wait_ge(S("a_scores"), n + 1)
                                    if n >= 4:
                                        dve.wait_ge(S("a_out"), n - 3)
                                    dve.tensor_tensor(A[:, n % 4], PS[:, 2 + n % 2, :].rearrange("p (k t) -> p k t", k=GH),
                                                      keep[:].unsqueeze(1).to_broadcast([128, GH, 128]), ALU.mult).then_inc(S("kept"), 1)
                                if i + 1 < NT:
                                    dve.wait_ge(S("summed"), i + 1)
                                    if i:
                                        dve.wait_ge(S("a_out"), HG * i)
                                    dve.tensor_tensor(KV[:, (i + 1) % 2], PS[:, 6, :].rearrange("p (h s) -> p h s", h=H),
                                                      head_of[:].unsqueeze(2).to_broadcast([128, H, SLOT]), ALU.mult).then_inc(S("state"), 1)
                                if i:
                                    normalise(i - 1)
                            normalise(NT - 1)

                        @block.scalar
                        def _(act):
                            for i in range(NT):
                                act.wait_ge(S("a_out"), HG * (i + 1))
                                if i:
                                    act.wait_ge(S("O_turned"), i)
                                act.activation(O[:].rearrange("p g t -> p (g t)"), PS[:, 4 + i % 2, :], ACT.Copy).then_inc(S("O_copied"), 1)

                        @block.sync
                        def _(sp):
                            sp.dma_start(w_e1[:], a["w_e1"]).then_inc(S("experts_in"), 16)
                            sp.dma_start(w_e2[:], a["w_e2"]).then_inc(S("experts_in"), 16)
                            for q in range(T // QT):
                                if q >= 2:
                                    sp.wait_ge(S("a_scores"), 2 * HG * (q - 1))
                                for k in range(6):
                                    restack(sp, Qs[:, q % 2], 0, k, 0, H, QT * q, QT, S(f"q_in{q}"))
                                    restack(sp, Ks[:, q % 2], 1, k, 0, H, QT * q, QT, S(f"k_in{q}"))
                            sp.wait_ge(S("experts_in"), 32)
                    end_phase()
                    with nc.Block() as block:
                        out_projection(lambda pe: None, block, y_tok, yT, w_out1, x_tok, "o1")
                    end_phase()

                with ExitStack() as tmp:
                    gate = sb("gate", [128, NT, E], F32, tmp)
                    gt = sb("gt", [128, NT, E, E], F32, tmp)
                    eq = sb("eq", [128, NT, E, E], F32, tmp)
                    rank = sb("rank", [128, NT, E], F32, tmp)
                    top = sb("top", [128, NT], F32, tmp)
                    gw = sb("gw", [128, NT, E], F32, tmp)
                    gwT = sb("gwT", [NT * E, 128], F32, tmp)
                    hid = sb("hid_e", [128, 2, 4, 512], F32, tmp)
                    with nc.Block() as block:
                        jobs = [(e, j) for e in range(E) for j in range(2)]

                        @block.tensor
                        def _(pe):
                            for i in range(NT):
                                last = pe.matmul(PS[:, 7, E * i:E * i + E], xT[:, 128 * i:128 * i + 128], w_gate[:], start=True, stop=True)
                            last.then_inc(S("gates"), 1)

                            def up(n):
                                e, j = jobs[n]
                                for k in range(4):
                                    if 4 * n + k >= 3:
                                        pe.wait_ge(S("e_gelu"), 4 * n + k - 2)
                                    pe.matmul(PS[:, (4 * n + k) % 3, :], w_e1[:, e, 128 * k:128 * k + 128], xT[:, 512 * j:512 * j + 512], start=True, stop=True).then_inc(S("e_up"), 1)

                            def down(n):
                                e, j = jobs[n]
                                pe.wait_ge(S("e_gelu"), 4 * (n + 1))
                                for i in range(4):
                                    if n >= 2 and i == 0:
                                        pe.wait_ge(S("e_added"), n - 1)
                                    for k in range(4):
                                        last = pe.matmul(PS[:, 3 + n % 2, 128 * i:128 * i + 128], hid[:, n % 2, k, 128 * i:128 * i + 128], w_e2[:, e, k, :], start=(k == 0), stop=(k == 3))
                                last.then_inc(S("e_down"), 1)

                            up(0)
                            for n in range(len(jobs)):
                                if n + 1 < len(jobs):
                                    up(n + 1)
                                if n == 0:
                                    pe.wait_ge(S("gw"), 1)
                                    pe.transpose(PS[0:NT * E, 7, 0:128], gw[:].rearrange("p i e -> p (i e)"), ident[:]).then_inc(S("gw_turned"), 1)
                                    pe.wait_ge(S("gwT"), 1)
                                    for i in range(NT):
                                        last = pe.matmul(PS[:, 5 + i // 4, 128 * (i % 4):128 * (i % 4) + 128], gwT[:], b_e2[:, i, :], start=True, stop=True)
                                    last.then_inc(S("biased"), 1)
                                down(n)

                        @block.scalar
                        def _(act):
                            act.wait_ge(S("gate_less"), 1)
                            act.activation(gate[:], gate[:], ACT.Exp).then_inc(S("gate_exp"), 1)
                            for n, (e, j) in enumerate(jobs):
                                if n >= 2:
                                    act.wait_ge(S("e_down"), n - 1)
                                for k in range(4):
                                    act.wait_ge(S("e_up"), 4 * n + k + 1)
                                    act.activation(hid[:, n % 2, k, :], PS[:, (4 * n + k) % 3, :], ACT.Gelu, bias=b_e1[:, e, k:k + 1]).then_inc(S("e_gelu"), 1)

                        @block.vector
                        def _(dve):
                            link = chain(dve, S("moe_dve"))
                            shape = [128, NT, E, E]
                            dve.wait_ge(S("gates"), 1)
                            link(dve.tensor_tensor(gate[:], PS[:, 7, 0:NT * E].rearrange("p (i e) -> p i e", i=NT), b_gate[:].unsqueeze(1).to_broadcast([128, NT, E]), ALU.add))
                            mine, other = gate[:].unsqueeze(3).to_broadcast(shape), gate[:].unsqueeze(2).to_broadcast(shape)
                            dve.tensor_tensor(gt[:], other, mine, ALU.is_gt)
                            link(dve.tensor_tensor(eq[:], other, mine, ALU.is_equal))
                            link(dve.tensor_tensor(eq[:].rearrange("p i e f -> p i (e f)"), eq[:].rearrange("p i e f -> p i (e f)"),
                                                   tie[:].rearrange("p e f -> p (e f)").unsqueeze(1).to_broadcast([128, NT, E * E]), ALU.mult))
                            link(dve.tensor_tensor(gt[:], gt[:], eq[:], ALU.add))
                            dve.reduce_sum(rank[:], gt[:], AX.X)
                            link(dve.reduce_max(top[:], gate[:], AX.X))
                            dve.tensor_tensor(gate[:], gate[:], top[:].unsqueeze(2).to_broadcast([128, NT, E]), ALU.subtract).then_inc(S("gate_less"), 1)
                            link(dve.tensor_scalar(rank[:], rank[:], 2.0, None, ALU.is_lt))
                            dve.wait_ge(S("gate_exp"), 1)
                            link(dve.tensor_tensor(gw[:], gate[:], rank[:], ALU.mult))
                            link(dve.reduce_sum(top[:], gw[:], AX.X))
                            link(dve.reciprocal(top[:], top[:]))
                            dve.tensor_tensor(gw[:], gw[:], top[:].unsqueeze(2).to_broadcast([128, NT, E]), ALU.mult).then_inc(S("gw"), 1)
                            dve.wait_ge(S("gw_turned"), 1)
                            dve.tensor_copy(gwT[:], PS[0:NT * E, 7, 0:128]).then_inc(S("gwT"), 1)
                            dve.wait_ge(S("biased"), 1)
                            for j in range(2):
                                link(dve.tensor_tensor(x_tok[:, 4 * j:4 * j + 4, :], x_tok[:, 4 * j:4 * j + 4, :], PS[:, 5 + j, :].rearrange("p (i d) -> p i d", i=4), ALU.add))
                            for n, (e, j) in enumerate(jobs):
                                dve.wait_ge(S("e_down"), n + 1)
                                if n >= 2:
                                    dve.wait_ge(S("e_added"), n - 1)
                                for k in range(4):
                                    i = 4 * j + k
                                    last = dve.scalar_tensor_tensor(x_tok[:, i, :], PS[:, 3 + n % 2, 128 * k:128 * k + 128], gw[:, i, e:e + 1], x_tok[:, i, :], ALU.mult, ALU.add)
                                last.then_inc(S("e_added"), 1)

                        @block.sync
                        def _(sp):
                            sp.wait_ge(S("e_added"), len(jobs))
                            sp.dma_start(out_dram[b], x_tok[:]).then_inc(S("out"), 16)
                            sp.wait_ge(S("out"), 16)
                end_phase()


def lay_out(**i):
    import numpy as np
    n = {k: np.asarray(v) for k, v in i.items()}
    rot = (np.arange(D) // DH) * DH + (np.arange(D) % DH + DH // 2) % DH
    a = {"x": n["L0_attn_x"]}
    w = n["L0_attn_W_qkv"]
    q, k, v = w[:, :D], w[:, D:2 * D], w[:, 2 * D:]
    a["w_attn0"] = np.stack([q, q[:, rot], k, k[:, rot], v], axis=1)
    a["w_out0"] = n["L0_attn_W_o"]
    q, k, v = n["L1_attn_Wq"].T, n["L1_attn_Wk"].T, n["L1_attn_Wv"].T
    a["w_attn1"] = np.stack([q, q[:, rot], k, k[:, rot], v], axis=1)
    a["w_out1"] = n["L1_attn_Wo"].T
    a["w_qkv"] = n["L0_ffn_wqkv"].transpose(1, 0, 2)
    a["w_o"] = n["L0_ffn_wo"].reshape(DEPTH, 4, 128, D).transpose(2, 0, 1, 3)
    a["w_up"] = n["L0_ffn_w1"].transpose(1, 0, 2)
    pad = np.zeros((DEPTH, 384, D), n["L0_ffn_w2"].dtype)
    pad[:, :HID] = n["L0_ffn_w2"]
    a["w_down"] = pad.reshape(DEPTH, 3, 128, D).transpose(2, 0, 1, 3)
    pad = np.zeros((DEPTH, 2, 384), n["L0_ffn_b1"].dtype)
    pad[:, :, :HID] = n["L0_ffn_b1"].reshape(DEPTH, 2, HID)
    a["b_up"] = pad.reshape(DEPTH, 2, 3, 128).transpose(3, 0, 1, 2)
    a["b_down"] = n["L0_ffn_b2"]
    a["ln_gb"] = np.stack([n["L0_ffn_ln_g"].T, n["L0_ffn_ln_b"].T], axis=2)
    qs, ks = n["L0_ffn_q_scale"], n["L0_ffn_k_scale"]
    swap = (np.arange(LD) + LD // 2) % LD
    a["scales"] = np.stack([qs, qs[:, swap], ks, ks[:, swap]], axis=1)
    a["w_gate"] = n["L1_ffn_gate_w"].T
    a["b_gate"] = n["L1_ffn_gate_b"]
    a["w_e1"] = n["L1_ffn_w1"].transpose(1, 0, 2)
    a["b_e1"] = n["L1_ffn_b1"].reshape(E, 4, 128).transpose(2, 0, 1)
    a["w_e2"] = n["L1_ffn_w2"].reshape(E, 4, 128, D).transpose(2, 0, 1, 3)
    blk = np.zeros((NT, E, NT, D), n["L1_ffn_b2"].dtype)
    for t in range(NT):
        blk[t, :, t] = n["L1_ffn_b2"]
    a["b_e2"] = blk.reshape(NT * E, NT, D)
    return {k: np.ascontiguousarray(v) for k, v in a.items()}


def kernel(**inputs):
    import numpy as _np
    import concourse.bacc as _bacc
    from concourse import mybir as _mybir
    from concourse.bass_utils import run_bass_kernel_spmd as _run

    nc = _bacc.Bacc("TRN2", target_bir_lowering=False, num_devices=1)
    arrays = {}

    def feed(tag, group):
        aps = {}
        for name, v in group.items():
            arrays[f"{tag}_{name}"] = v
            aps[name] = nc.dram_tensor(f"{tag}_{name}", v.shape, _mybir.dt.from_np(v.dtype), kind="ExternalInput").ap()
        return aps

    a = feed("in", lay_out(**inputs))
    c = feed("const", constant_arrays())
    out = nc.dram_tensor("out_0", (B, T, D), _mybir.dt.float32, kind="ExternalOutput").ap()
    build(nc, a, c, out)
    r = _run(nc, [arrays], core_ids=[0])
    return r.results[0]["out_0"]
```

```python
import math
from contextlib import ExitStack

import numpy as np
import concourse.bass as bass
from concourse import mybir

F32 = mybir.dt.float32
BF16 = mybir.dt.bfloat16
U32 = mybir.dt.uint32
ALU = mybir.AluOpType
ACT = mybir.ActivationFunctionType
AX = mybir.AxisListType

B, T, D = 4, 1024, 128
NT = T // 128
H, DH = 16, 8
HG, GH = 4, 4
SLOT = 32
DEPTH, LH, LD = 2, 8, 64
INNER = LH * LD
WIN = 64
HID = int(D * 4 * 2 / 3)
HID_CHUNKS = [(0, 128), (128, 128), (256, HID - 256)]
E, EH = 8, 512
BIG = 1e30
M_ROW = 64
Q_PART = [0, 0, 1, 1, 0, 2]
K_PART = [0, 1, 0, 1, 2, 0]


def constant_arrays():
    c = {}
    c["ident"] = np.eye(128, dtype=np.float32)
    p, j = np.arange(128)[:, None], np.arange(128)[None, :]
    tri = np.stack([np.where(j > p, -BIG, 0.0), np.where(p > j, -BIG, 0.0)], axis=1)
    c["causal"] = tri.astype(np.float32)
    c["keep"] = (j >= p).astype(np.float32)
    q = p % WIN
    allowed = (q <= j - 0) & (j <= q + WIN)
    window = np.where(allowed, 0.0, -BIG)
    first = np.where(allowed & ~((p < WIN) & (j < WIN)), 0.0, -BIG)
    c["window"] = np.stack([first, window], axis=1).astype(np.float32)
    c["head_of"] = (p // DH == np.arange(H)[None, :]).astype(np.float32)
    half = DH // 2
    theta = (np.float32(1.0) / np.float32(10000.0) ** (np.arange(half, dtype=np.float32) / np.float32(half)))
    ang = np.arange(T, dtype=np.float32)[:, None] * theta.astype(np.float32)[None, :]
    cos, sin = np.cos(ang.astype(np.float64)), np.sin(ang.astype(np.float64))
    d = np.arange(D) % DH
    c["rope"] = np.stack([cos.T[d % half], sin.T[d % half] * np.where(d < half, -1.0, 1.0)[:, None]], axis=1).astype(np.float32)
    idx = np.arange(0, LD, 2, dtype=np.float32)
    inv = (np.float32(1.0) / np.float32(10000.0) ** (idx / np.float32(LD))).astype(np.float32)
    t = np.arange(T, dtype=np.float32)
    fr = (t[:, None] * inv[None, :]).astype(np.float32)
    fr = np.concatenate([fr, fr], -1).astype(np.float64)
    base = ((idx + np.float32(0.4 * LD)) / np.float32(1.4 * LD)).astype(np.float32)
    power = ((t - T // 2) / np.float32(WIN // 2)).astype(np.float32)
    sc = base[None, :].astype(np.float64) ** power[:, None].astype(np.float64)
    sc = np.concatenate([sc, sc], -1)
    sign = np.where(np.arange(LD) < LD // 2, -1.0, 1.0)[None, :]
    tabs = np.stack([np.cos(fr) * sc * 8.0, np.sin(fr) * sc * sign * 8.0,
                     np.cos(fr) / sc, np.sin(fr) / sc * sign], axis=0)
    c["xpos"] = tabs.reshape(4, NT, 128, LD).transpose(2, 0, 1, 3).astype(np.float32).copy()
    return c


def build(nc, a, c, out):
    ctx = ExitStack()
    with ctx:
        taken = {}

        def sb(name, shape, dt=F32, where=ctx):
            taken[name] = taken.get(name, 0) + 1
            return where.enter_context(nc.sbuf_tensor(name if taken[name] == 1 else f"{name}_{taken[name]}", shape, dt))

        sems = {}

        def S(name):
            if name not in sems:
                sems[name] = ctx.enter_context(nc.semaphore(name))
            return sems[name]

        late_weights_in = ctx.enter_context(nc.semaphore("late_weights_in"))
        PS = ctx.enter_context(nc.psum_tensor("PS", [128, 8, 512], F32))

        parts_dram = nc.dram_tensor("parts_dram", (2, H, len(Q_PART), DH, T), BF16, kind="Internal").ap()
        max_dram = nc.dram_tensor("max_dram", (HG, 2, 3, GH * 4, 128), BF16, kind="Internal").ap()

        w_attn0 = sb("w_attn0", [128, 5, D])
        w_out0 = sb("w_out0", [128, D])
        w_attn1 = sb("w_attn1", [128, 5, D])
        w_out1 = sb("w_out1", [128, D])
        w_qkv = sb("w_qkv", [128, DEPTH, 3 * INNER])
        w_o = sb("w_o", [128, DEPTH, 4, D])
        w_up = sb("w_up", [128, DEPTH, 2 * HID])
        w_down = sb("w_down", [128, DEPTH, 3, D])
        b_up = sb("b_up", [128, DEPTH, 2, 3])
        b_down = sb("b_down", [128, DEPTH, D])
        ln_gb = sb("ln_gb", [128, DEPTH, 2])
        w_gate = sb("w_gate", [128, E])
        b_gate = sb("b_gate", [128, E])
        b_e1 = sb("b_e1", [128, E, 4])
        b_e2 = sb("b_e2", [NT * E, NT, D])
        ident = sb("ident", [128, 128])
        identb = sb("identb", [128, 128], BF16)
        causalb = sb("causalb", [128, 2, 128], BF16)
        keep = sb("keep", [128, 128])
        windowb = sb("windowb", [128, 2, 4, 128], BF16)
        head_of = sb("head_of", [128, H])
        rope = sb("rope", [128, 2, T])
        xpos = sb("xpos", [128, DEPTH, 4, NT, LD])
        minus_half = sb("minus_half", [128, 2 * LH])
        tie = sb("tie", [128, E, E])
        zero = sb("zero", [128, 1])
        x_tok = sb("x_tok", [128, NT, D])
        xs_tok = sb("xs_tok", [128, NT, D])
        xT = sb("xT", [128, T])
        hT = sb("hT", [128, T])

        def chain(eng, sem):
            n = [0]

            def link(ins):
                n[0] += 1
                ins.then_inc(sem, 1)
                eng.wait_ge(sem, n[0])
            return link

        def end_phase():
            nc.all_engine_barrier()
            nums = sorted(s.num for s in sems.values())
            assert nums[-1] - nums[0] == len(nums) - 1
            nc.gpsimd.sem_clear(range(nums[0], nums[-1] + 1))
            nc.all_engine_barrier()

        with ExitStack() as tmp:
            windowf = sb("windowf", [128, 2, 128], F32, tmp)
            causalf = sb("causalf", [128, 2, 128], F32, tmp)
            xposf = sb("xposf", [128, 4, NT, LD], F32, tmp)
            scales = sb("scales", [128, DEPTH, 4, LD], F32, tmp)
            loads = [
                (w_attn0[:], a["w_attn0"]), (w_out0[:], a["w_out0"]), (w_attn1[:], a["w_attn1"]), (w_out1[:], a["w_out1"]),
                (b_up[:], a["b_up"]),
                (b_down[:], a["b_down"].partition_broadcast(128)), (ln_gb[:], a["ln_gb"]),
                (w_gate[:], a["w_gate"]), (b_gate[:], a["b_gate"].partition_broadcast(128)),
                (b_e1[:], a["b_e1"]), (b_e2[:], a["b_e2"]),
                (ident[:], c["ident"]), (causalf[:], c["causal"]), (keep[:], c["keep"]), (windowf[:], c["window"]),
                (head_of[:], c["head_of"]), (rope[:], c["rope"]), (xposf[:], c["xpos"]),
                (scales[:], a["scales"].partition_broadcast(128)),
            ]
            late_loads = [(w_qkv[:], a["w_qkv"]), (w_o[:], a["w_o"]), (w_up[:], a["w_up"]), (w_down[:], a["w_down"])]
            with nc.Block() as block:
                @block.sync
                def _(sp):
                    for dst, src in loads:
                        sp.dma_start(dst, src).then_inc(S("weights_in"), 16)
                    for dst, src in late_loads:
                        sp.dma_start(dst, src).then_inc(late_weights_in, 16)
                    sp.wait_ge(S("weights_in"), 16 * len(loads))

                @block.gpsimd
                def _(pool):
                    pool.memset(tie[:], 1.0).then_inc(S("tie"), 1)
                    pool.wait_ge(S("tie"), 1)
                    pool.affine_select(out=tie[:], in_=tie[:], compare_op=ALU.is_gt, fill=0.0,
                                       base=0, pattern=[[1, E], [-1, E]], channel_multiplier=0).then_inc(S("tie"), 1)
                    pool.wait_ge(S("tie"), 2)
                    pool.memset(minus_half[:], -0.5)
                    pool.memset(zero[:], 0.0)

                @block.vector
                def _(dve):
                    dve.wait_ge(S("weights_in"), 16 * len(loads))
                    dve.tensor_copy(identb[:], ident[:])
                    dve.tensor_copy(causalb[:], causalf[:])
                    for r in range(4):
                        dve.tensor_copy(windowb[:, :, r, :], windowf[:])
                    for l in range(DEPTH):
                        for k in range(4):
                            dve.tensor_tensor(xpos[:, l, k], xposf[:, k], scales[:, l, k].unsqueeze(1).to_broadcast([128, NT, LD]), ALU.mult)
        end_phase()

        def norm_stats(dve, link, x, tiles, tag):
            for i in tiles:
                last = dve.bn_stats(stats[:, i, :], x[:, i, :])
            link(last)
            for i in tiles:
                last = dve.bn_aggr(mean_var[:, i, :], stats[:, i, :])
            link(last)
            t = slice(tiles[0], tiles[-1] + 1)
            dve.tensor_scalar(var_eps[:, t], mean_var[:, t, 1], 1e-5, None, ALU.add).then_inc(S(tag + "_var"), 1)

        def norm_rstd(pool, tiles, tag):
            t = slice(tiles[0], tiles[-1] + 1)
            pool.wait_ge(S(tag + "_var"), 1)
            pool.tensor_tensor(rstd[:, t], var_eps[:, t], minus_half[:, 0:len(tiles)], ALU.pow).then_inc(S(tag + "_rstd"), 1)

        def norm_apply(dve, x, dst, tiles, tag):
            dve.wait_ge(S(tag + "_rstd"), 1)
            for i in tiles:
                dve.tensor_scalar(dst[:, i, :], x[:, i, :], mean_var[:, i, 0:1], rstd[:, i:i + 1],
                                  ALU.subtract, ALU.mult).then_inc(S(tag + "_normed"), 1)

        def layer_norm(block, x, dst, ready, tag):
            @block.vector
            def _(dve):
                link = chain(dve, S(tag + "_dve"))
                ready(dve)
                norm_stats(dve, link, x, range(NT), tag)
                norm_apply(dve, x, dst, range(NT), tag)

            @block.gpsimd
            def _(pool):
                norm_rstd(pool, range(NT), tag)

        stats = sb("stats", [128, NT, 6])
        mean_var = sb("mean_var", [128, NT, 2])
        var_eps = sb("var_eps", [128, NT])
        rstd = sb("rstd", [128, NT])

        def shifted_evac(eng, copy, bank, half, sem):
            t0 = 512 * half
            copy(hT[0:64, t0:t0 + 512], PS[0:64, bank, :])
            n = 512 if half == 0 else 511
            return copy(hT[64:128, t0 + 1:t0 + 1 + n], PS[64:128, bank, 0:n])

        def act_copy(act):
            return lambda o, i: act.activation(o, i, ACT.Copy)

        def write_part(eng, parts, n, k, t, sem):
            for g, part in enumerate((Q_PART, K_PART)[n]):
                if part == k:
                    eng.dma_start(parts_dram[n, :, g, :, t], parts[:, n, k, t]).then_inc(sem, 16)

        def restack(eng, dst, n, head0, heads, t0, tn, sem):
            src = parts_dram[n].rearrange("h g d t -> (g d) h t")[:, head0:head0 + heads, t0:t0 + tn]
            eng.dma_start(dst[0:DH * len(Q_PART)], src).then_inc(sem, 16)

        x_dram = a["x"].rearrange("b (i p) d -> b p i d", p=128)
        out_dram = out.rearrange("b (i p) d -> b p i d", p=128)

        with nc.Fori(0, B) as b:
            with nc.Block() as block:
                @block.sync
                def _(sp):
                    sp.dma_start(x_tok[:], x_dram[b]).then_inc(S("x_in"), 16)

                layer_norm(block, x_tok, xs_tok, lambda dve: dve.wait_ge(S("x_in"), 16), "ln0")

                @block.tensor
                def _(pe):
                    for i in range(NT):
                        pe.wait_ge(S("ln0_normed"), i + 1)
                        last = pe.transpose(PS[:, i // 4, 128 * (i % 4):128 * (i % 4) + 128], xs_tok[:, i, :], ident[:])
                        if i % 4 == 3:
                            last.then_inc(S("xT_bank"), 1)

                @block.scalar
                def _(act):
                    for j in range(2):
                        act.wait_ge(S("xT_bank"), j + 1)
                        act.activation(xT[:, 512 * j:512 * j + 512], PS[:, j, :], ACT.Copy)
            end_phase()

            with ExitStack() as tmp:
                Vst = sb("Vst", [128, NT, H, SLOT], F32, tmp)
                y_tok = sb("y_tok", [128, NT, D], F32, tmp)
                Qs = sb("Qs", [128, 3, GH, T], BF16, tmp)
                Ks = sb("Ks", [128, 3, GH, T], BF16, tmp)
                parts = sb("parts", [128, 2, 3, T], BF16, tmp)
                NP = 8
                P = sb("P", [128, NP, 512], F32, tmp)
                O = sb("O", [128, T], F32, tmp)
                yT = sb("yT", [128, T], F32, tmp)
                mx = sb("mx", [128, 2, GH, 4, 2], F32, tmp)
                mT = sb("mT", [GH * 4, 128], F32, tmp)
                mT2 = sb("mT2", [GH * 4, 128], F32, tmp)
                m_parts = sb("m_parts", [GH * 4, 3, 128], BF16, tmp)
                den = sb("den", [128, 4, GH], F32, tmp)

                ROTS = [(n, j) for j in range(2) for n in range(2)]
                STAGES = [(g, j) for g in range(HG) for j in range(2)]
                units1 = [(G, h, i, lo, min(lo + 512, 128 * (i + 1)))
                          for G, (g, j) in enumerate(STAGES) for i in range(4 * j, 4 * j + 4)
                          for lo in range(0, 128 * (i + 1), 512) for h in range(GH)]
                units2 = [(G, h, i, max(512 * j, 128 * i), 512 * (j + 1))
                          for G, (g, j) in enumerate(STAGES) for i in range(4 * j + 4) for h in range(GH)]
                N_UNITS = len(units1)
                assert N_UNITS == len(units2)
                end1 = [sum(u[0] <= G for u in units1) for G in range(len(STAGES))]
                end2 = [sum(u[0] <= G for u in units2) for G in range(len(STAGES))]
                LEAD = max(e - f for e, f in zip(end1, [0] + end2)) + 14
                order = [("rotate", 0), ("v", 0), ("rotate", 1), ("v", 1), ("rotate", 2), ("rotate", 3)]
                for m in range(N_UNITS + LEAD + 9):
                    n = m - LEAD
                    if m < N_UNITS:
                        order.append(("max", m))
                    if m - 2 in end1:
                        order.append(("turn_max", end1.index(m - 2)))
                    if 0 <= n < N_UNITS:
                        order.append(("key", n))
                    if GH <= n and n % GH == 0 and n <= N_UNITS:
                        order.append(("values", n // GH - 1))
                    if n - 6 in end2:
                        order.append(("turn_out", end2.index(n - 6)))
                    if n - 12 == end2[-2]:
                        order.append(("turn_y", 0))
                    if n - 16 == end2[-2]:
                        order.append(("project_y", 0))
                order += [("turn_y", 1), ("project_y", 1)]
                ALONE = N_UNITS - LEAD + 2
                key_bank = [3 + n % 2 if n < ALONE else (3 + ALONE % 2, 4 - ALONE % 2, 0, 1)[(n - ALONE) % 4] for n in range(N_UNITS)]
                Y_BANKS = ((2, 2), (0, 1))
                bank7 = [x for x in order if x[0] in ("turn_max", "turn_out")]
                with nc.Block() as block:
                    def stack(eng, G):
                        g, j = STAGES[G]
                        eng.wait_ge(S(f"parts_out{j}"), 16 * 2 * len(Q_PART))
                        if g < 3:
                            eng.wait_ge(S("q_zeroed"), g + 1)
                            eng.wait_ge(S("k_zeroed"), g + 1)
                        else:
                            eng.wait_ge(S("key_scores"), end2[1])
                        for n in range(2):
                            restack(eng, (Qs, Ks)[n][:, g % 3, :, 512 * j:512 * j + 512], n, GH * g, GH, 512 * j, 512, S(f"stacked{G}"))

                    @block.tensor
                    def _(pe):
                        def rotate(r):
                            n, j = ROTS[r]
                            if r >= 2:
                                pe.wait_ge(S("rotated"), r - 1)
                            for k in range(2):
                                last = pe.matmul(PS[:, 3 + 2 * (r % 2) + k, :], w_attn0[:, 2 * n + k, :], xT[:, 512 * j:512 * j + 512], start=True, stop=True)
                            last.then_inc(S("qk_made"), 1)

                        def v(j):
                            if j:
                                pe.wait_ge(S("v_out"), 1)
                            for k in range(4):
                                i = 4 * j + k
                                last = pe.matmul(PS[:, 7, 128 * k:128 * k + 128], xT[:, 128 * i:128 * i + 128], w_attn0[:, 4, :], start=True, stop=True)
                            last.then_inc(S("v_made"), 1)

                        def max_scores(m):
                            G, h, i, lo, hi = units1[m]
                            g, j = STAGES[G]
                            if m in [0] + end1:
                                pe.wait_ge(S(f"stacked{G}"), 16 * 2)
                                if j == 0 and g < 3:
                                    pe.wait_ge(S("k_ones"), g + 1)
                                elif j == 0:
                                    pe.wait_ge(S("max_rows_zero"), 1)
                            if m >= 3:
                                pe.wait_ge(S("max_read"), m - 2)
                            diag = hi == 128 * (i + 1)
                            last = pe.matmul(PS[:, m % 3, 0:hi - lo], Qs[:, g % 3, h, 128 * i:128 * i + 128], Ks[:, g % 3, h, lo:hi],
                                             start=True, stop=not diag)
                            if diag:
                                last = pe.matmul(PS[:, m % 3, hi - lo - 128:hi - lo], identb[:], causalb[:, 0, :], start=False, stop=True)
                            last.then_inc(S("max_scores"), 1)

                        def key_scores(n):
                            G, h, i, lo, hi = units2[n]
                            g, j = STAGES[G]
                            if n in [0] + end2:
                                pe.wait_ge(S(f"m_in{G}"), 16)
                            before = [k for k in range(n) if key_bank[k] == key_bank[n]]
                            if before:
                                pe.wait_ge(S("exp"), before[-1] + 1)
                            elif n < 2:
                                pe.wait_ge(S("rotated"), 4)
                            else:
                                pe.wait_ge(S("max_read"), N_UNITS)
                            diag = lo == 128 * i
                            last = pe.matmul(PS[:, key_bank[n], 0:hi - lo], Ks[:, g % 3, h, 128 * i:128 * i + 128], Qs[:, g % 3, h, lo:hi],
                                             start=True, stop=not diag)
                            if diag:
                                last = pe.matmul(PS[:, key_bank[n], 0:128], identb[:], causalb[:, 1, :], start=False, stop=True)
                            last.then_inc(S("key_scores"), 1)

                        def values(v):
                            G, _, i, lo, hi = units2[GH * v]
                            g, j = STAGES[G]
                            if v == 0:
                                pe.wait_ge(S("v_ready"), 2)
                            pe.wait_ge(S("exp"), GH * (v + 1))
                            if i == 0 and g:
                                pe.wait_ge(S("O_copied"), G - 1)
                            for h in range(GH):
                                last = pe.matmul(PS[SLOT * h:SLOT * h + SLOT, 5 + j, lo - 512 * j:hi - 512 * j],
                                                 Vst[:, i, GH * g + h, :], P[:, (GH * v + h) % NP, 0:hi - lo],
                                                 start=(i == 0), stop=(i == 4 * j + 3))
                            last.then_inc(S("values"), 1)

                        def wait_bank7(step, k):
                            n = bank7.index((step, k))
                            if n:
                                pe.wait_ge(S("bank7_read"), n)
                            else:
                                pe.wait_ge(S("v_out"), 2)

                        def turn_max(G):
                            g, j = STAGES[G]
                            pe.wait_ge(S("max_read"), end1[G])
                            if j:
                                pe.wait_ge(S("joined"), g + 1)
                            wait_bank7("turn_max", G)
                            pe.transpose(PS[0:GH * 4, 7, 0:128], mx[:, G % 2, :, :, 0], ident[:]).then_inc(S("m_turned"), 1)

                        def turn_out(G):
                            pe.wait_ge(S("O_copied"), G + 1)
                            wait_bank7("turn_out", G)
                            for k in range(4):
                                i = 4 * STAGES[G][1] + k
                                last = pe.transpose(PS[:, 7, 128 * k:128 * k + 128], O[:, 128 * i:128 * i + 128], ident[:])
                            last.then_inc(S("O_turned"), 1)

                        def turn_y(j):
                            if j:
                                pe.wait_ge(S("exp"), N_UNITS)
                            else:
                                pe.wait_ge(S("max_read"), N_UNITS)
                            pe.wait_ge(S("bank7_read"), bank7.index(("turn_out", 2 * HG - 2 + j)) + 1)
                            for k in range(4):
                                last = pe.transpose(PS[:, Y_BANKS[j][0], 128 * k:128 * k + 128], y_tok[:, 4 * j + k, :], ident[:])
                            last.then_inc(S("y_turned"), 1)

                        def project_y(j):
                            pe.wait_ge(S("yT"), j + 1)
                            for k in range(4):
                                i = 4 * j + k
                                last = pe.matmul(PS[:, Y_BANKS[j][1], 128 * k:128 * k + 128], yT[:, 128 * i:128 * i + 128], w_out0[:], start=True, stop=True)
                            last.then_inc(S("y_projected"), 1)

                        steps = {"rotate": rotate, "v": v, "max": max_scores, "key": key_scores, "values": values,
                                 "turn_max": turn_max, "turn_out": turn_out, "turn_y": turn_y, "project_y": project_y}
                        for step, k in order:
                            steps[step](k)

                    @block.vector
                    def _(dve):
                        link = chain(dve, S("attn_dve"))

                        def rotate(r):
                            n, j = ROTS[r]
                            t = slice(512 * j, 512 * j + 512)
                            dve.wait_ge(S("qk_made"), r + 1)
                            dve.tensor_tensor(P[:, 0], PS[:, 3 + 2 * (r % 2), :], rope[:, 0, t], ALU.mult)
                            link(dve.tensor_tensor(P[:, 1], PS[:, 4 + 2 * (r % 2), :], rope[:, 1, t], ALU.mult))
                            dve.tensor_tensor(P[:, 2], P[:, 0], P[:, 1], ALU.add).then_inc(S("rotated"), 1)
                            dve.wait_ge(S("rotated"), r + 1)
                            for k, (whole, rest) in enumerate(((2, 0), (0, 1), (1, None))):
                                dve.tensor_copy(parts[:, n, k, t], P[:, whole]).then_inc(S("parts"), 1)
                                dve.wait_ge(S("parts"), 3 * r + k + 1)
                                if k < 2:
                                    link(dve.tensor_tensor(P[:, rest], P[:, whole], parts[:, n, k, t], ALU.subtract))

                        def maxima(m):
                            G, h, i, lo, hi = units1[m]
                            if m in end1 and G >= 2:
                                dve.wait_ge(S("m_turned"), G - 1)
                            dve.wait_ge(S("max_scores"), m + 1)
                            dve.reduce_max(mx[:, G % 2, h, i % 4, lo // 512:lo // 512 + 1], PS[:, m % 3, 0:hi - lo], AX.X).then_inc(S("max_read"), 1)
                            if m + 1 in end1:
                                dve.wait_ge(S("max_read"), m + 1)
                                if STAGES[G][1]:
                                    dve.tensor_tensor(mx[:, G % 2, :, :, 0], mx[:, G % 2, :, :, 0], mx[:, G % 2, :, :, 1], ALU.max).then_inc(S("joined"), 1)

                        def split(G):
                            dve.wait_ge(S("m_turned"), G + 1)
                            if G:
                                dve.wait_ge(S("m_out"), 16 * G)
                            n = bank7.index(("turn_max", G))
                            dve.tensor_scalar(mT[:], PS[0:GH * 4, 7, 0:128], -1.0, None, ALU.mult).then_inc(S("bank7_read"), 1)
                            dve.wait_ge(S("bank7_read"), n + 1)
                            link(dve.tensor_copy(m_parts[:, 0], mT[:]))
                            link(dve.tensor_tensor(mT2[:], mT[:], m_parts[:, 0], ALU.subtract))
                            link(dve.tensor_copy(m_parts[:, 1], mT2[:]))
                            link(dve.tensor_tensor(mT[:], mT2[:], m_parts[:, 1], ALU.subtract))
                            dve.tensor_copy(m_parts[:, 2], mT[:]).then_inc(S("m_parts"), 1)
                            dve.wait_ge(S("m_parts"), G + 1)

                        def normalise(G):
                            g, j = STAGES[G]
                            dve.wait_ge(S("O_turned"), G + 1)
                            o = PS[:, 7, :].rearrange("p (i h s) -> p i h s", i=4, h=GH)
                            link(dve.reciprocal(den[:], o[:, :, :, DH]))
                            dve.tensor_tensor(y_tok[:, 4 * j:4 * j + 4, 32 * g:32 * g + 32].rearrange("p i (h d) -> p i h d", h=GH),
                                              o[:, :, :, 0:DH], den[:].unsqueeze(3).to_broadcast([128, 4, GH, DH]), ALU.mult).then_inc(S("bank7_read"), 1)
                            dve.wait_ge(S("bank7_read"), bank7.index(("turn_out", G)) + 1)

                        def add_y(j):
                            dve.wait_ge(S("y_projected"), j + 1)
                            dve.tensor_tensor(x_tok[:, 4 * j:4 * j + 4, :], x_tok[:, 4 * j:4 * j + 4, :],
                                              PS[:, Y_BANKS[j][1], :].rearrange("p (i d) -> p i d", i=4), ALU.add)

                        steps = {"rotate": rotate, "max": maxima, "turn_max": split, "turn_out": normalise, "project_y": add_y}
                        for step, k in order:
                            if step in steps:
                                steps[step](k)

                    @block.scalar
                    def _(act):
                        for g in range(3):
                            act.activation(Ks[:, g].rearrange("p h t -> p (h t)").bitcast(F32), zero[:].to_broadcast([128, GH * T // 2]), ACT.Copy).then_inc(S("k_zeroed"), 1)
                            if g < 2:
                                act.wait_ge(S("v_made"), g + 1)
                                act.activation(Vst[:, 4 * g:4 * g + 4, :, 0:DH],
                                               PS[:, 7, :].rearrange("p (i h d) -> p i h d", i=4, h=H), ACT.Copy).then_inc(S("v_out"), 1)
                        for G in (2, 3, 4, 5):
                            stack(act, G)
                        act.activation(hT[0:64, :], xT[0:64, :], ACT.Copy)
                        act.activation(hT[64:128, 1:T], xT[64:128, 0:T - 1], ACT.Copy)
                        act.activation(hT[64:128, 0:1], zero[64:128, :], ACT.Copy)

                        def exp(n):
                            G, h, i, lo, hi = units2[n]
                            if n == 0:
                                act.wait_ge(S("parts"), 12)
                            act.wait_ge(S("key_scores"), n + 1)
                            if n >= NP:
                                act.wait_ge(S("values"), (n - NP) // GH + 1)
                            act.activation(P[:, n % NP, 0:hi - lo], PS[:, key_bank[n], 0:hi - lo], ACT.Exp,
                                           scale=1.0 / math.sqrt(DH)).then_inc(S("exp"), 1)

                        def copy_out(G):
                            j = STAGES[G][1]
                            act.wait_ge(S("values"), end2[G] // GH)
                            if G >= 2:
                                act.wait_ge(S("O_turned"), G - 1)
                            act.activation(O[:, 512 * j:512 * j + 512], PS[:, 5 + j, :], ACT.Copy).then_inc(S("O_copied"), 1)

                        for step, k in order:
                            if step == "key":
                                if k - 2 in end2:
                                    copy_out(end2.index(k - 2))
                                exp(k)
                            elif step == "turn_out" and k == len(STAGES) - 1:
                                copy_out(k)
                            elif step == "turn_y":
                                act.wait_ge(S("y_turned"), k + 1)
                                act.activation(yT[:, 512 * k:512 * k + 512], PS[:, Y_BANKS[k][0], :], ACT.Copy).then_inc(S("yT"), 1)

                    @block.gpsimd
                    def _(pool):
                        for g in range(3):
                            pool.memset(Qs[:, g].bitcast(U32), 0).then_inc(S("q_zeroed"), 1)
                            pool.wait_ge(S("q_zeroed"), g + 1)
                            pool.wait_ge(S("k_zeroed"), g + 1)
                            pool.memset(Ks[M_ROW:M_ROW + 3, g], 1.0).then_inc(S("k_ones"), 1)
                            pool.wait_ge(S("k_ones"), g + 1)
                        pool.memset(Vst[:, :, :, DH:SLOT], 0.0).then_inc(S("v_ready"), 1)
                        pool.wait_ge(S("v_ready"), 1)
                        pool.memset(Vst[:, :, :, DH:DH + 1], 1.0).then_inc(S("v_ready"), 1)
                        pool.wait_ge(S("key_scores"), end2[1])
                        pool.memset(Qs[M_ROW:M_ROW + 3, 0].bitcast(U32), 0).then_inc(S("max_rows_zero"), 1)

                    @block.sync
                    def _(sp):
                        for j in range(2):
                            for r in (2 * j, 2 * j + 1):
                                for k in range(3):
                                    sp.wait_ge(S("parts"), 3 * r + k + 1)
                                    write_part(sp, parts, ROTS[r][0], k, slice(512 * j, 512 * j + 512), S(f"parts_out{j}"))
                            stack(sp, j)
                        for G, (g, j) in enumerate(STAGES):
                            sp.wait_ge(S("m_parts"), G + 1)
                            sp.dma_start(max_dram[g, j].rearrange("k r t -> r k t"), m_parts[:]).then_inc(S("m_out"), 16)
                            sp.wait_ge(S("m_out"), 16 * (G + 1))
                            sp.dma_start(Qs[M_ROW:M_ROW + 3, g % 3, :, 512 * j:512 * j + 512], max_dram[g, j].rearrange("k (h i) t -> k h (i t)", h=GH)).then_inc(S(f"m_in{G}"), 16)
                            if G == 3:
                                stack(sp, 6)
                                stack(sp, 7)
                end_phase()

            layers = ExitStack()
            hs = sb("hs", [128, NT, D], F32, layers)
            HALF_A, HALF_B = range(NT // 2), range(NT // 2, NT)
            for l in range(DEPTH):
                with ExitStack() as tmp:
                    NV = 4
                    raw = sb("raw", [128, 2, 3, INNER], F32, tmp)
                    sq = sb("sq", [128, 2, INNER], F32, tmp)
                    ra = sb("ra", [128, 2, INNER], F32, tmp)
                    rb = sb("rb", [128, 2, INNER], F32, tmp)
                    ss = sb("ss", [128, 2, LH], F32, tmp)
                    nrm = sb("nrm", [128, 2, LH], F32, tmp)
                    qk = sb("qk", [128, 2, INNER], F32, tmp)
                    qT = sb("qT", [128, 2, 4, 128], F32, tmp)
                    kT = sb("kT", [128, 4, WIN + T], F32, tmp)
                    V_A = sb("V_A", [128, NV, LH, LD + 1], F32, tmp)
                    V_B = sb("V_B", [128, NV, LH, LD + 1], F32, tmp)
                    sm = sb("sm", [128, 2, LH, 128], F32, tmp)
                    PT = sb("PT", [128, LH, 128], F32, tmp)
                    mxl = sb("mxl", [128, LH], F32, tmp)
                    rd = sb("rd", [128, LH], F32, tmp)
                    o_tok = sb("o_tok", [128, INNER], F32, tmp)
                    oT = sb("oT", [128, 4, 128], F32, tmp)
                    with nc.Block() as block:
                        OUT_BANK = {0: 7, 1: 2}

                        def low_uses(i):
                            return (i - 1) // NV + 1 if i % NV else i // NV

                        @block.tensor
                        def _(pe):
                            for i in range(NT if l else 0):
                                pe.transpose(PS[:, i // 4, 128 * (i % 4):128 * (i % 4) + 128], xs_tok[:, i, :], ident[:]).then_inc(S("h_turned"), 1)

                            def project_qk(i):
                                if i == 0:
                                    if l == 0:
                                        pe.wait_ge(late_weights_in, 16 * len(late_loads))
                                    pe.wait_ge(S("set"), 1)
                                    if l:
                                        pe.wait_ge(S("hT"), 2)
                                else:
                                    pe.wait_ge(S("raw_qk"), i)
                                for n in range(2):
                                    last = pe.matmul(PS[:, n, :], hT[:, 128 * i:128 * i + 128], w_qkv[:, l, INNER * n:INNER * n + INNER], start=True, stop=True)
                                last.then_inc(S("qk_made"), 1)

                            def project_v(i):
                                if i:
                                    pe.wait_ge(S("raw_v"), i)
                                if i >= 4:
                                    pe.wait_ge(S("o"), i - 3)
                                pe.matmul(PS[:, 2, :], hT[:, 128 * i:128 * i + 128], w_qkv[:, l, 2 * INNER:3 * INNER], start=True, stop=True).then_inc(S("v_made"), 1)

                            def turn_o(i):
                                pe.wait_ge(S("o"), i + 1)
                                for k in range(4):
                                    last = pe.transpose(PS[:, 3, 128 * k:128 * k + 128], o_tok[:, 128 * k:128 * k + 128], ident[:])
                                last.then_inc(S("o_turned"), 1)

                            def turn_p(g, i):
                                if g == 1:
                                    pe.wait_ge(S("p"), i + 1)
                                elif i >= 1:
                                    pe.wait_ge(S("o_features"), i)
                                for k in range(4):
                                    last = pe.transpose(PS[:, 3 + g, 128 * k:128 * k + 128], sm[:, i % 2, 4 * g + k, :], ident[:])
                                last.then_inc(S(f"turned_p{g}"), 1)

                            def turn_qk(n, i):
                                if n == 1:
                                    pe.wait_ge(S("qk"), i + 1)
                                if i >= 2:
                                    pe.wait_ge(S(f"p_features{n}"), i - 1)
                                for k in range(4):
                                    last = pe.transpose(PS[:, 3 + n, 128 * k:128 * k + 128], qk[:, n, 128 * k:128 * k + 128], ident[:])
                                last.then_inc(S(f"turned_qk{n}"), 1)

                            def back(i):
                                pe.wait_ge(S("o_features"), i + 1)
                                if i:
                                    pe.wait_ge(S("xs"), i)
                                for k in range(4):
                                    last = pe.matmul(PS[:, 7, 512 - D:512], oT[:, k, :], w_o[:, l, k, :], start=(k == 0), stop=(k == 3))
                                last.then_inc(S("back"), 1)

                            def scores(i):
                                for n in range(2):
                                    pe.wait_ge(S(f"qk_features{n}"), i + 1)
                                if i:
                                    pe.wait_ge(S("less_max"), i)
                                for g in range(2):
                                    pe.matmul(PS[:, 5 + g, :], identb[:], windowb[:, min(i, 1)].rearrange("p r j -> p (r j)"), start=True, stop=False, skip_group_check=True)
                                for k in range(4):
                                    for w in range(2):
                                        for g in range(2):
                                            last = pe.matmul(PS[64 * w:64 * w + 64, 5 + g, 128 * k:128 * k + 128],
                                                             qT[LD * g:LD * g + LD, i % 2, k, 64 * w:64 * w + 64],
                                                             kT[LD * g:LD * g + LD, k, 128 * i + 64 * w:128 * i + 64 * w + 128],
                                                             start=False, stop=(k == 3), skip_group_check=True)
                                            if k == 3 and w == 1:
                                                last.then_inc(S("scores"), 1)

                            def values(g, i):
                                if g == 1:
                                    pe.wait_ge(S(f"v_in{i % NV}"), 32 * (i // NV + 1))
                                    if i:
                                        pe.wait_ge(S(f"v_low{i % NV}"), 16 * low_uses(i))
                                    pe.wait_ge(S("raw_v"), min(i + 4, NT))
                                elif i:
                                    pe.wait_ge(S("o"), i)
                                pe.wait_ge(S(f"p_features{g}"), i + 1)
                                for k in range(4):
                                    for w, V in ((0, V_B), (1, V_A)):
                                        last = pe.matmul(PS[64 * w:64 * w + 64, OUT_BANK[g], (LD + 1) * k:(LD + 1) * (k + 1)],
                                                         PT[:, 4 * g + k, 64 * w:64 * w + 64], V[:, i % NV, 2 * k + g, :], start=True, stop=True)
                                last.then_inc(S("pv"), 1)

                            for i in range(2):
                                project_qk(i)
                                project_v(i)
                            turn_qk(1, 0)
                            turn_qk(0, 0)
                            for s in range(NT + 2):
                                if s + 2 < NT:
                                    project_qk(s + 2)
                                if s < NT:
                                    scores(s)
                                if 1 <= s <= NT:
                                    turn_p(1, s - 1)
                                if s >= 2:
                                    turn_o(s - 2)
                                if s + 2 < NT:
                                    project_v(s + 2)
                                if 1 <= s <= NT:
                                    turn_p(0, s - 1)
                                if s + 1 < NT:
                                    turn_qk(1, s + 1)
                                if s >= 2:
                                    back(s - 2)
                                if 1 <= s <= NT:
                                    values(1, s - 1)
                                if s + 1 < NT:
                                    turn_qk(0, s + 1)
                                if 1 <= s <= NT:
                                    values(0, s - 1)

                        @block.scalar
                        def _(act):
                            for j in range(2 if l else 0):
                                act.wait_ge(S("h_turned"), 4 * (j + 1))
                                shifted_evac(act, act_copy(act), j, j, None).then_inc(S("hT"), 1)

                            def raw_qk(i):
                                act.wait_ge(S("qk_made"), i + 1)
                                if i >= 2:
                                    act.wait_ge(S("rot"), 2 * (i - 1))
                                act.activation(raw[:, i % 2, 0:2].rearrange("p n d -> p (n d)"), PS[:, 0:2, :].rearrange("p n d -> p (n d)"), ACT.Copy).then_inc(S("raw_qk"), 1)
                                act.wait_ge(S("raw_qk"), i + 1)
                                if i:
                                    act.wait_ge(S("ss"), i)
                                act.activation(sq[:], raw[:, i % 2, 0:2], ACT.Square).then_inc(S("sq"), 1)

                            def raw_v(i):
                                act.wait_ge(S("v_made"), i + 1)
                                if i >= 2:
                                    act.wait_ge(S(f"v_in{(i - 2) % NV}"), 32 * ((i - 2) // NV + 1))
                                    act.wait_ge(S(f"v_low{(i - 1) % NV}"), 16 * low_uses(i - 1))
                                act.activation(raw[:, i % 2, 2], PS[:, 2, :], ACT.Copy).then_inc(S("raw_v"), 1)

                            def weights_out(g, i):
                                act.wait_ge(S(f"turned_p{g}"), i + 1)
                                act.activation(PT[:, 4 * g:4 * g + 4].rearrange("p k t -> p (k t)"), PS[:, 3 + g, :], ACT.Copy).then_inc(S(f"p_features{g}"), 1)

                            def q_out(i):
                                act.wait_ge(S("turned_qk0"), i + 1)
                                act.activation(qT[:, i % 2].rearrange("p k t -> p (k t)"), PS[:, 3, :], ACT.Copy).then_inc(S("qk_features0"), 1)

                            def k_out(i):
                                act.wait_ge(S("turned_qk1"), i + 1)
                                act.activation(kT[:, :, WIN + 128 * i:WIN + 128 * i + 128], PS[:, 4, :].rearrange("p (k t) -> p k t", k=4), ACT.Copy).then_inc(S("qk_features1"), 1)

                            for i in range(2):
                                raw_qk(i)
                                raw_v(i)
                            k_out(0)
                            q_out(0)
                            for s in range(NT + 2):
                                if s + 2 < NT:
                                    raw_qk(s + 2)
                                if 1 <= s <= NT:
                                    weights_out(1, s - 1)
                                if s >= 2:
                                    act.wait_ge(S("o_turned"), s - 1)
                                    act.activation(oT[:].rearrange("p k t -> p (k t)"), PS[:, 3, :], ACT.Copy).then_inc(S("o_features"), 1)
                                if s + 2 < NT:
                                    raw_v(s + 2)
                                if 1 <= s <= NT:
                                    weights_out(0, s - 1)
                                if s + 1 < NT:
                                    k_out(s + 1)
                                if s < NT:
                                    act.wait_ge(S("less_max"), s + 1)
                                    act.activation(sm[:, s % 2], sm[:, s % 2], ACT.Exp).then_inc(S("p"), 1)
                                if s + 1 < NT:
                                    q_out(s + 1)

                        @block.vector
                        def _(dve):
                            link = chain(dve, S("local_dve"))
                            dve.memset(kT[:, :, 0:WIN], 0.0)
                            dve.memset(V_B[0:64, 0, :, 0:LD], 0.0)
                            if l:
                                dve.memset(hT[64:128, 0:1], 0.0)
                            for V in (V_A, V_B):
                                last = dve.memset(V[:, :, :, LD:LD + 1], 1.0)
                            last.then_inc(S("set"), 1)

                            def rotate(i):
                                dve.wait_ge(S("sq"), i + 1)
                                dve.reduce_sum(ss[:], sq[:].rearrange("p n (h d) -> p n h d", h=LH), AX.X).then_inc(S("ss"), 1)
                                if i:
                                    dve.wait_ge(S("qk"), i)
                                for n in range(2):
                                    x = raw[:, i % 2, n].rearrange("p (h a d) -> p h a d", h=LH, a=2)
                                    cos = xpos[:, l, 2 * n, i].unsqueeze(1).to_broadcast([128, LH, LD])
                                    sin = xpos[:, l, 2 * n + 1, i].rearrange("p (a d) -> p a d", a=2).unsqueeze(1).to_broadcast([128, LH, 2, LD // 2])
                                    dve.tensor_tensor(ra[:, n].rearrange("p (h d) -> p h d", h=LH), raw[:, i % 2, n].rearrange("p (h d) -> p h d", h=LH), cos, ALU.mult)
                                    dve.tensor_tensor(rb[:, n].rearrange("p (h a d) -> p h a d", h=LH, a=2), x[:, :, ::-1, :], sin, ALU.mult).then_inc(S("rot"), 1)
                                dve.wait_ge(S("rot"), 2 * (i + 1))
                                link(dve.tensor_tensor(ra[:], ra[:], rb[:], ALU.add))
                                dve.wait_ge(S("nrm"), i + 1)
                                if i:
                                    dve.wait_ge(S("turned_qk0"), i)
                                dve.tensor_tensor(qk[:].rearrange("p n (h d) -> p (n h) d", h=LH), ra[:].rearrange("p n (h d) -> p (n h) d", h=LH),
                                                  nrm[:].rearrange("p n h -> p (n h)").unsqueeze(2).to_broadcast([128, 2 * LH, LD]), ALU.mult).then_inc(S("qk"), 1)

                            def less_max(i):
                                if i >= 2:
                                    dve.wait_ge(S("turned_p0"), i - 1)
                                for g in range(2):
                                    dve.wait_ge(S("scores"), 2 * i + 2)
                                    s = PS[:, 5 + g, :].rearrange("p (k j) -> p k j", k=4)
                                    link(dve.reduce_max(mxl[:, 4 * g:4 * g + 4], s, AX.X))
                                    last = dve.tensor_tensor(sm[:, i % 2, 4 * g:4 * g + 4, :], s, mxl[:, 4 * g:4 * g + 4].unsqueeze(2).to_broadcast([128, 4, 128]), ALU.subtract)
                                last.then_inc(S("less_max"), 1)

                            def over_sum(i):
                                if i:
                                    dve.wait_ge(S("o_turned"), i)
                                for g in (1, 0):
                                    dve.wait_ge(S("pv"), 2 * i + 2 - g)
                                    o = PS[:, OUT_BANK[g], 0:4 * (LD + 1)].rearrange("p (k s) -> p k s", k=4)
                                    link(dve.reciprocal(rd[:, 4 * g:4 * g + 4], o[:, :, LD]))
                                    last = dve.tensor_tensor(o_tok[:].rearrange("p (k g d) -> p k g d", k=4, g=2)[:, :, g, :], o[:, :, 0:LD],
                                                             rd[:, 4 * g:4 * g + 4].unsqueeze(2).to_broadcast([128, 4, LD]), ALU.mult)
                                last.then_inc(S("o"), 1)

                            rotate(0)
                            rotate(1)
                            for s in range(NT + 2):
                                if s < NT:
                                    less_max(s)
                                if s + 2 < NT:
                                    rotate(s + 2)
                                if 1 <= s <= NT:
                                    over_sum(s - 1)
                                if s >= 2:
                                    dve.wait_ge(S("back"), s - 1)
                                    dve.tensor_tensor(xs_tok[:, s - 2, :], xs_tok[:, s - 2, :], PS[:, 7, 512 - D:512], ALU.add).then_inc(S("xs"), 1)
                                if s == 6:
                                    dve.wait_ge(S("xs"), 4)
                                    link(dve.tensor_copy(hs[:, 0:4, 0:64], xs_tok[:, 0:4, 0:64]))
                                elif s == 7:
                                    dve.wait_ge(S("shift"), 32)
                                    dve.wait_ge(S("first"), 1)
                                    norm_stats(dve, link, hs, HALF_A, "lnf")
                                elif s == 8:
                                    norm_apply(dve, hs, hs, HALF_A, "lnf")

                        @block.gpsimd
                        def _(pool):
                            pool.memset(hs[0:1, 0, 64:], 0.0).then_inc(S("first"), 1)
                            for i in range(NT):
                                pool.wait_ge(S("ss"), i + 1)
                                if i:
                                    pool.wait_ge(S("qk"), i)
                                pool.tensor_scalar(nrm[:], ss[:], 1e-24, None, ALU.max).then_inc(S("norm2"), 1)
                                pool.wait_ge(S("norm2"), i + 1)
                                pool.tensor_tensor(nrm[:].rearrange("p n h -> p (n h)"), nrm[:].rearrange("p n h -> p (n h)"), minus_half[:, 0:2 * LH], ALU.pow).then_inc(S("nrm"), 1)
                            norm_rstd(pool, HALF_A, "lnf")

                        @block.sync
                        def _(sp):
                            sp.wait_ge(S("set"), 1)
                            for i in range(NT):
                                sp.wait_ge(S("raw_v"), i + 1)
                                v = raw[:, i % 2, 2].rearrange("p (h d) -> p h d", h=LH)
                                if i >= NV:
                                    sp.wait_ge(S("pv"), 2 * (i - NV + 1))
                                sp.dma_start(V_A[:, i % NV, :, 0:LD], v).then_inc(S(f"v_in{i % NV}"), 16)
                                sp.dma_start(V_B[64:128, i % NV, :, 0:LD], v[0:64]).then_inc(S(f"v_in{i % NV}"), 16)
                                if i + 1 < NT:
                                    if i + 1 >= NV:
                                        sp.wait_ge(S("pv"), 2 * (i + 2 - NV))
                                    sp.dma_start(V_B[0:64, (i + 1) % NV, :, 0:LD], v[64:128]).then_inc(S(f"v_low{(i + 1) % NV}"), 16)
                            sp.wait_ge(S("xs"), 4)
                            sp.dma_start(hs[1:128, 0:4, 64:], xs_tok[0:127, 0:4, 64:]).then_inc(S("shift"), 16)
                            sp.dma_start(hs[0:1, 1:4, 64:], xs_tok[127:128, 0:3, 64:]).then_inc(S("shift"), 16)
                    end_phase()

                with ExitStack() as tmp:
                    hn = sb("hn", [128, T], F32, tmp)
                    gl = sb("gl", [128, 2, 512], F32, tmp)
                    hid = sb("hid", [128, 3, T], F32, tmp)
                    with nc.Block() as block:
                        @block.sync
                        def _(sp):
                            sp.dma_start(hs[1:128, 4:NT, 64:], xs_tok[0:127, 4:NT, 64:]).then_inc(S("shift"), 16)
                            sp.dma_start(hs[0:1, 4:NT, 64:], xs_tok[127:128, 3:NT - 1, 64:]).then_inc(S("shift"), 16)

                        @block.gpsimd
                        def _(pool):
                            norm_rstd(pool, HALF_B, "lnf")

                        @block.tensor
                        def _(pe):
                            def turn(j):
                                if j:
                                    pe.wait_ge(S("lnf_normed"), 4)
                                for k in range(4):
                                    last = pe.transpose(PS[:, j, 128 * k:128 * k + 128], hs[:, 4 * j + k, :], ident[:])
                                last.then_inc(S("hn_turned"), 1)

                            def up(n):
                                j, (c0, cw) = n // 3, HID_CHUNKS[n % 3]
                                pe.wait_ge(S("hn"), j + 1)
                                if n >= 2:
                                    pe.wait_ge(S("hid"), n - 1)
                                for k in range(2):
                                    last = pe.matmul(PS[0:cw, 2 + 2 * (n % 2) + k, :], w_up[:, l, HID * k + c0:HID * k + c0 + cw], hn[:, 512 * j:512 * j + 512], start=True, stop=True)
                                last.then_inc(S("up"), 1)

                            def down(j):
                                pe.wait_ge(S("hid"), 3 * (j + 1))
                                for k in range(4):
                                    i = 4 * j + k
                                    for n, (c0, cw) in enumerate(HID_CHUNKS):
                                        last = pe.matmul(PS[:, 6 + j, 128 * k:128 * k + 128], hid[0:cw, n, 128 * i:128 * i + 128], w_down[0:cw, l, n, :], start=(n == 0), stop=(n == 2))
                                last.then_inc(S("down"), 1)

                            turn(0)
                            for n in range(3):
                                up(n)
                            turn(1)
                            up(3)
                            down(0)
                            up(4)
                            up(5)
                            down(1)

                        @block.scalar
                        def _(act):
                            for n in range(6):
                                cw = HID_CHUNKS[n % 3][1]
                                act.wait_ge(S("up"), n + 1)
                                if n >= 2:
                                    act.wait_ge(S("hid"), n - 1)
                                act.activation(gl[0:cw, n % 2, :], PS[0:cw, 3 + 2 * (n % 2), :], ACT.Gelu, bias=b_up[0:cw, l, 1, n % 3:n % 3 + 1]).then_inc(S("gelu"), 1)

                        @block.vector
                        def _(dve):
                            link = chain(dve, S("ffn_dve"))

                            def features(j):
                                dve.wait_ge(S("hn_turned"), j + 1)
                                dve.tensor_scalar(hn[:, 512 * j:512 * j + 512], PS[:, j, :], ln_gb[:, l, 0:1], ln_gb[:, l, 1:2], ALU.mult, ALU.add).then_inc(S("hn"), 1)

                            def gated(n):
                                j, cw = n // 3, HID_CHUNKS[n % 3][1]
                                dve.wait_ge(S("gelu"), n + 1)
                                dve.scalar_tensor_tensor(hid[0:cw, n % 3, 512 * j:512 * j + 512], PS[0:cw, 2 + 2 * (n % 2), :], b_up[0:cw, l, 0, n % 3:n % 3 + 1],
                                                         gl[0:cw, n % 2, :], ALU.add, ALU.mult).then_inc(S("hid"), 1)

                            features(0)
                            link(dve.tensor_copy(hs[:, 4:NT, 0:64], xs_tok[:, 4:NT, 0:64]))
                            dve.wait_ge(S("shift"), 32)
                            norm_stats(dve, link, hs, HALF_B, "lnf")
                            gated(0)
                            norm_apply(dve, hs, hs, HALF_B, "lnf")
                            gated(1)
                            features(1)
                            gated(2)
                            dve.tensor_tensor(xs_tok[:], xs_tok[:], b_down[:, l].unsqueeze(1).to_broadcast([128, NT, D]), ALU.add).then_inc(S("xb"), 1)
                            for n in range(3, 6):
                                gated(n)
                            dve.wait_ge(S("xb"), 1)
                            for j in range(2):
                                dve.wait_ge(S("down"), j + 1)
                                dve.tensor_tensor(xs_tok[:, 4 * j:4 * j + 4, :], xs_tok[:, 4 * j:4 * j + 4, :], PS[:, 6 + j, :].rearrange("p (i d) -> p i d", i=4), ALU.add)
                    end_phase()

            layers.close()

            with nc.Block() as block:
                def both(dve):
                    link = chain(dve, S("both"))
                    link(dve.tensor_tensor(x_tok[:], x_tok[:], xs_tok[:], ALU.add))

                layer_norm(block, x_tok, xs_tok, both, "ln1")

                @block.tensor
                def _(pe):
                    for i in range(NT):
                        pe.wait_ge(S("ln1_normed"), i + 1)
                        last = pe.transpose(PS[:, i // 4, 128 * (i % 4):128 * (i % 4) + 128], xs_tok[:, i, :], ident[:])
                        if i % 4 == 3:
                            last.then_inc(S("xT_bank"), 1)

                @block.scalar
                def _(act):
                    for j in range(2):
                        act.wait_ge(S("xT_bank"), j + 1)
                        act.activation(xT[:, 512 * j:512 * j + 512], PS[:, j, :], ACT.Copy)
            end_phase()

            with ExitStack() as tmp:
                w_e1 = sb("w_e1", [128, E, EH], F32, tmp)
                w_e2 = sb("w_e2", [128, E, 4, D], F32, tmp)
                NH = 4
                hid = sb("hid_e", [128, NH, 512], F32, tmp)
                gate = sb("gate", [128, NT, E], F32, tmp)
                gt = sb("gt", [128, NT, E, E], F32, tmp)
                eq = sb("eq", [128, NT, E, E], F32, tmp)
                rank = sb("rank", [128, NT, E], F32, tmp)
                top = sb("top", [128, NT], F32, tmp)
                gw = sb("gw", [128, NT, E], F32, tmp)
                gwT = sb("gwT", [NT * E, 128], F32, tmp)
                Vst = sb("Vst1", [128, NT, H, SLOT], F32, tmp)
                r_q = sb("r_q", [128, T], F32, tmp)
                r_k = sb("r_k", [128, T], F32, tmp)
                QT = 256
                Qs = sb("Qs1", [128, 2, H, QT], BF16, tmp)
                Ks = sb("Ks1", [128, 2, H, QT], BF16, tmp)
                scr = sb("scr1", [128, 2, T], F32, tmp)
                parts = sb("parts1", [128, 2, 3, T], BF16, tmp)
                O = sb("O1", [128, HG, 128], F32, tmp)
                y_tok = sb("y_tok1", [128, 2, D], F32, tmp)
                den = sb("den1", [128, HG, GH], F32, tmp)
                yT = sb("yT1", [128, 128], F32, tmp)
                A = scr[:].rearrange("p n (m k t) -> p (n m) k t", m=2, k=GH)
                turned = xs_tok[:].rearrange("p (a i) d -> p a (i d)", a=2)
                k_tok = xs_tok
                KV = hT[:].rearrange("p (a h s) -> p a h s", a=2, h=H)

                jobs = [(e, j) for e in range(E) for j in range(2)]
                UNITS = 4 * len(jobs)
                DOWN_BANK = (2, 4)
                ROTS = [(n, j) for j in range(2) for n in range(2)]
                EXPERT_LOADS = ((0, 1), (1, 4), (4, E))

                places = [(-9, "gates", 0), (-8, "rotate", 0), (-7, "v", 0), (-6, "rotate", 1), (-5, "v", 1), (-4, "rotate", 2),
                          (-3, "rotate", 3), (1.5, "weigh", 0), (1.6, "bias", 0), (1.7, "bias", 1), (1.8, "phi", 0), (1.9, "phi", 1),
                          (2.5, "phi", 2), (2.6, "phi", 3), (7, "turn_k", 0), (9, "turn_k", 1)]
                for u in range(UNITS):
                    places += [(u, "up", u), (u + 2.1, "down", u)]
                START, STRIDE = 10.2, 1.45
                for m in range(HG * NT):
                    at = START + STRIDE * m
                    places += [(at, "scores", m), (at + 1.2, "out", m)]
                    if m % HG == HG - 1:
                        i = m // HG
                        if i + 1 < NT:
                            places.append((at + 1.21, "state", i))
                        places += [(at + 2.7, "turn_out", i), (at + 4.2, "turn_y", i), (at + 5.7, "project_y", i)]
                order = [(step, k) for _, step, k in sorted(places)]
                x_adds = {}
                for step, k in order:
                    if step in ("bias", "project_y") or step == "down" and k % 4 == 3:
                        x_adds[step, k] = len(x_adds) + 1

                with nc.Block() as block:
                    @block.tensor
                    def _(pe):
                        def gates():
                            for i in range(NT):
                                last = pe.matmul(PS[:, 7, E * i:E * i + E], xT[:, 128 * i:128 * i + 128], w_gate[:], start=True, stop=True)
                            last.then_inc(S("gates"), 1)

                        def rotate(r):
                            n, j = ROTS[r]
                            if r >= 2:
                                pe.wait_ge(S("rotated"), r - 1)
                            for k in range(2):
                                last = pe.matmul(PS[:, 3 + 2 * (r % 2) + k, :], w_attn1[:, 2 * n + k, :], xT[:, 512 * j:512 * j + 512], start=True, stop=True)
                            last.then_inc(S("qk_made"), 1)

                        def v(j):
                            if j == 0:
                                pe.wait_ge(S("gates_read"), 1)
                            else:
                                pe.wait_ge(S("v_out"), 1)
                            for k in range(4):
                                i = 4 * j + k
                                last = pe.matmul(PS[:, 7, 128 * k:128 * k + 128], xT[:, 128 * i:128 * i + 128], w_attn1[:, 4, :], start=True, stop=True)
                            last.then_inc(S("v_made"), 1)

                        def turn_gates():
                            pe.wait_ge(S("gw"), 1)
                            pe.wait_ge(S("v_out"), 2)
                            pe.transpose(PS[0:NT * E, 7, 0:128], gw[:].rearrange("p i e -> p (i e)"), ident[:]).then_inc(S("gw_turned"), 1)

                        def bias(j):
                            pe.wait_ge(S("gwT"), 1)
                            pe.wait_ge(S("rotated"), 4)
                            for k in range(4):
                                last = pe.matmul(PS[:, DOWN_BANK[j], 128 * k:128 * k + 128], gwT[:], b_e2[:, 4 * j + k, :], start=True, stop=True)
                            last.then_inc(S("biased"), 1)

                        def turn_k(j):
                            pe.wait_ge(S("phi"), 2 * j + 2)
                            for k in range(4):
                                i = 4 * j + k
                                last = pe.transpose(PS[:, 5 + j, 128 * k:128 * k + 128], r_k[:, 128 * i:128 * i + 128], ident[:])
                            last.then_inc(S("k_turned"), 1)

                        def up(u):
                            n, k = divmod(u, 4)
                            e, j = jobs[n]
                            for c, (e0, _) in enumerate(EXPERT_LOADS):
                                if (e, j, k) == (e0, 0, 0):
                                    pe.wait_ge(S(f"experts_in{c}"), 32)
                            if u >= 2:
                                pe.wait_ge(S("e_gelu"), u - 1)
                            pe.matmul(PS[:, u % 2, :], w_e1[:, e, 128 * k:128 * k + 128], xT[:, 512 * j:512 * j + 512], start=True, stop=True).then_inc(S("e_up"), 1)

                        def down(u):
                            n, k = divmod(u, 4)
                            e, j = jobs[n]
                            if k == 0:
                                pe.wait_ge(S("x_added"), x_adds[("down", u - 5) if n >= 2 else ("bias", n)])
                            pe.wait_ge(S("e_gelu"), u + 1)
                            for i in range(4):
                                last = pe.matmul(PS[:, DOWN_BANK[n % 2], 128 * i:128 * i + 128], hid[:, u % NH, 128 * i:128 * i + 128], w_e2[:, e, k, :],
                                                 start=(k == 0 and i == 0), stop=(k == 3), skip_group_check=True)
                            last.then_inc(S("e_down"), 1)

                        def scores(m):
                            i, g = divmod(m, HG)
                            c, t0 = divmod(128 * i, QT)
                            if g == 0 and t0 == 0:
                                pe.wait_ge(S(f"q_in{c}"), 16)
                                pe.wait_ge(S(f"k_in{c}"), 16)
                            if m:
                                pe.wait_ge(S("kept"), m)
                            for k in range(GH):
                                last = pe.matmul(PS[:, 3, 128 * k:128 * k + 128], Ks[:, c % 2, GH * g + k, t0:t0 + 128],
                                                 Qs[:, c % 2, GH * g + k, t0:t0 + 128], start=True, stop=True)
                            last.then_inc(S("a_scores"), 1)

                        def chunk_out(m):
                            i, g = divmod(m, HG)
                            if m == 0:
                                pe.wait_ge(S("k_tok"), 1)
                                pe.wait_ge(S("zeroed"), 5)
                            if g == 0 and i:
                                pe.wait_ge(S("O_copied"), i)
                                pe.wait_ge(S("state"), i)
                            if i:
                                pe.matmul(PS[:, 5, 128 * g:128 * g + 128], KV[:, i % 2, GH * g:GH * g + GH, :].rearrange("p h s -> p (h s)"),
                                          r_q[:, 128 * i:128 * i + 128], start=True, stop=False, skip_group_check=True)
                            pe.wait_ge(S("kept"), m + 1)
                            for k in range(GH):
                                last = pe.matmul(PS[SLOT * k:SLOT * k + SLOT, 5, 128 * g:128 * g + 128], Vst[:, i, GH * g + k, :], A[:, m % 4, k, :],
                                                 start=(i == 0), stop=True, skip_group_check=True)
                            last.then_inc(S("a_out"), 1)

                        def state(i):
                            if i == 0:
                                pe.wait_ge(S("k_tok"), 2)
                            else:
                                pe.wait_ge(S("state"), i)
                            pe.matmul(PS[:, 6, :], k_tok[:, i, :], Vst[:, i].rearrange("p h s -> p (h s)"), start=(i == 0), stop=True, skip_group_check=True).then_inc(S("summed"), 1)

                        def turn_out(i):
                            pe.wait_ge(S("O_copied"), i + 1)
                            if i:
                                pe.wait_ge(S("x_added"), x_adds["project_y", i - 1])
                            for g in range(HG):
                                last = pe.transpose(PS[:, 7, 128 * g:128 * g + 128], O[:, g, :], ident[:])
                            last.then_inc(S("O_turned"), 1)

                        def turn_y(i):
                            pe.wait_ge(S("y"), i + 1)
                            pe.transpose(PS[:, 7, 0:128], y_tok[:, i % 2, :], ident[:]).then_inc(S("y_turned"), 1)

                        def project_y(i):
                            pe.wait_ge(S("yT"), i + 1)
                            pe.matmul(PS[:, 7, 0:D], yT[:], w_out1[:], start=True, stop=True).then_inc(S("y_projected"), 1)

                        for step, k in order:
                            if step == "gates":
                                gates()
                            elif step == "rotate":
                                rotate(k)
                            elif step == "v":
                                v(k)
                            elif step == "weigh":
                                turn_gates()
                            elif step == "bias":
                                bias(k)
                            elif step == "turn_k":
                                turn_k(k)
                            elif step == "up":
                                up(k)
                            elif step == "down":
                                down(k)
                            elif step == "scores":
                                scores(k)
                            elif step == "out":
                                chunk_out(k)
                            elif step == "state":
                                state(k)
                            elif step == "turn_out":
                                turn_out(k)
                            elif step == "turn_y":
                                turn_y(k)
                            elif step == "project_y":
                                project_y(k)

                    @block.scalar
                    def _(act):
                        for c, (e0, e1) in enumerate(EXPERT_LOADS):
                            act.dma_start(w_e1[:, e0:e1], a["w_e1"][:, e0:e1]).then_inc(S(f"experts_in{c}"), 16)
                            act.dma_start(w_e2[:, e0:e1], a["w_e2"][:, e0:e1]).then_inc(S(f"experts_in{c}"), 16)
                        for step, k in order:
                            if step == "gates":
                                act.wait_ge(S("gate_less"), 1)
                                act.activation(gate[:], gate[:], ACT.Exp).then_inc(S("gate_exp"), 1)
                            elif step == "rotate":
                                n, j = ROTS[k]
                                act.wait_ge(S("phi_in"), k + 1)
                                x = scr[:, n, 512 * j:512 * j + 512]
                                act.activation(x, x, ACT.Exp).then_inc(S("phi_out"), 1)
                            elif step == "v":
                                act.wait_ge(S("v_made"), k + 1)
                                act.activation(Vst[:, 4 * k:4 * k + 4, :, 0:DH],
                                               PS[:, 7, :].rearrange("p (i h d) -> p i h d", i=4, h=H), ACT.Copy).then_inc(S("v_out"), 1)
                            elif step == "up":
                                act.wait_ge(S("e_up"), k + 1)
                                if k >= NH:
                                    act.wait_ge(S("e_down"), k - NH + 1)
                                act.activation(hid[:, k % NH, :], PS[:, k % 2, :], ACT.Gelu, bias=b_e1[:, jobs[k // 4][0], k % 4:k % 4 + 1]).then_inc(S("e_gelu"), 1)
                            elif step == "out" and k % HG == HG - 1:
                                i = k // HG
                                act.wait_ge(S("a_out"), k + 1)
                                if i:
                                    act.wait_ge(S("O_turned"), i)
                                act.activation(O[:].rearrange("p g t -> p (g t)"), PS[:, 5, :], ACT.Copy).then_inc(S("O_copied"), 1)
                            elif step == "turn_y":
                                act.wait_ge(S("y_turned"), k + 1)
                                if k:
                                    act.wait_ge(S("y_projected"), k)
                                act.activation(yT[:], PS[:, 7, 0:128], ACT.Copy).then_inc(S("yT"), 1)

                    @block.vector
                    def _(dve):
                        link = chain(dve, S("second_dve"))

                        def gates():
                            shape = [128, NT, E, E]
                            dve.wait_ge(S("gates"), 1)
                            dve.tensor_tensor(gate[:], PS[:, 7, 0:NT * E].rearrange("p (i e) -> p i e", i=NT), b_gate[:].unsqueeze(1).to_broadcast([128, NT, E]), ALU.add).then_inc(S("gates_read"), 1)
                            dve.wait_ge(S("gates_read"), 1)
                            mine, other = gate[:].unsqueeze(3).to_broadcast(shape), gate[:].unsqueeze(2).to_broadcast(shape)
                            link(dve.reduce_max(top[:], gate[:], AX.X))
                            dve.tensor_tensor(gt[:], other, mine, ALU.is_gt)
                            link(dve.tensor_tensor(eq[:], other, mine, ALU.is_equal))
                            dve.tensor_tensor(gate[:], gate[:], top[:].unsqueeze(2).to_broadcast([128, NT, E]), ALU.subtract).then_inc(S("gate_less"), 1)
                            link(dve.tensor_tensor(eq[:].rearrange("p i e f -> p i (e f)"), eq[:].rearrange("p i e f -> p i (e f)"),
                                                   tie[:].rearrange("p e f -> p (e f)").unsqueeze(1).to_broadcast([128, NT, E * E]), ALU.mult))
                            link(dve.tensor_tensor(gt[:], gt[:], eq[:], ALU.add))
                            link(dve.reduce_sum(rank[:], gt[:], AX.X))
                            link(dve.tensor_scalar(rank[:], rank[:], 2.0, None, ALU.is_lt))

                        def weigh():
                            dve.wait_ge(S("gate_exp"), 1)
                            link(dve.tensor_tensor(gw[:], gate[:], rank[:], ALU.mult))
                            link(dve.reduce_sum(top[:], gw[:], AX.X))
                            link(dve.reciprocal(top[:], top[:]))
                            dve.tensor_tensor(gw[:], gw[:], top[:].unsqueeze(2).to_broadcast([128, NT, E]), ALU.mult).then_inc(S("gw"), 1)
                            dve.wait_ge(S("gw_turned"), 1)
                            dve.tensor_copy(gwT[:], PS[0:NT * E, 7, 0:128]).then_inc(S("gwT"), 1)

                        def rotate(r):
                            n, j = ROTS[r]
                            q = (r_q, r_k)[n][:, 512 * j:512 * j + 512]
                            dve.wait_ge(S("qk_made"), r + 1)
                            dve.tensor_tensor(turned[:, 0], PS[:, 3 + 2 * (r % 2), :], rope[:, 0, 512 * j:512 * j + 512], ALU.mult)
                            link(dve.tensor_tensor(turned[:, 1], PS[:, 4 + 2 * (r % 2), :], rope[:, 1, 512 * j:512 * j + 512], ALU.mult))
                            dve.tensor_tensor(q, turned[:, 0], turned[:, 1], ALU.add).then_inc(S("rotated"), 1)
                            dve.wait_ge(S("rotated"), r + 1)
                            dve.tensor_scalar(scr[:, n, 512 * j:512 * j + 512], q, 0.0, None, ALU.min).then_inc(S("phi_in"), 1)

                        def phi(r):
                            n, j = ROTS[r]
                            q, s = (r_q, r_k)[n][:, 512 * j:512 * j + 512], scr[:, n, 512 * j:512 * j + 512]
                            p = [parts[:, n, k, 512 * j:512 * j + 512] for k in range(3)]
                            dve.wait_ge(S("phi_out"), r + 1)
                            dve.scalar_tensor_tensor(q, q, 0.0, s, ALU.max, ALU.add).then_inc(S("phi"), 1)
                            dve.wait_ge(S("phi"), r + 1)
                            for k in range(3):
                                whole = s if k else q
                                dve.tensor_copy(p[k], whole).then_inc(S("parts"), 1)
                                dve.wait_ge(S("parts"), 3 * r + k + 1)
                                if k < 2:
                                    link(dve.tensor_tensor(s, whole, p[k], ALU.subtract))

                        def before_adding(step, k):
                            if x_adds[step, k] > 1:
                                dve.wait_ge(S("x_added"), x_adds[step, k] - 1)

                        def add_four(j, bank):
                            return dve.tensor_tensor(x_tok[:, 4 * j:4 * j + 4, :], x_tok[:, 4 * j:4 * j + 4, :], PS[:, bank, :].rearrange("p (i d) -> p i d", i=4), ALU.add)

                        def add_expert(u):
                            n = u // 4
                            e, j = jobs[n]
                            dve.wait_ge(S("e_down"), u + 1)
                            before_adding("down", u)
                            for k in range(4):
                                i = 4 * j + k
                                last = dve.scalar_tensor_tensor(x_tok[:, i, :], PS[:, DOWN_BANK[n % 2], 128 * k:128 * k + 128], gw[:, i, e:e + 1], x_tok[:, i, :], ALU.mult, ALU.add)
                            last.then_inc(S("x_added"), 1)

                        def masked(m):
                            dve.wait_ge(S("a_scores"), m + 1)
                            if m >= 4:
                                dve.wait_ge(S("a_out"), m - 3)
                            dve.tensor_tensor(A[:, m % 4], PS[:, 3, :].rearrange("p (k t) -> p k t", k=GH),
                                              keep[:].unsqueeze(1).to_broadcast([128, GH, 128]), ALU.mult).then_inc(S("kept"), 1)

                        def state(i):
                            dve.wait_ge(S("summed"), i + 1)
                            if i:
                                dve.wait_ge(S("a_out"), HG * i)
                            dve.tensor_tensor(KV[:, (i + 1) % 2], PS[:, 6, :].rearrange("p (h s) -> p h s", h=H),
                                              head_of[:].unsqueeze(2).to_broadcast([128, H, SLOT]), ALU.mult).then_inc(S("state"), 1)

                        def normalise(i):
                            dve.wait_ge(S("O_turned"), i + 1)
                            if i:
                                dve.wait_ge(S("y"), i)
                            if i >= 2:
                                dve.wait_ge(S("y_turned"), i - 1)
                            o = PS[:, 7, :].rearrange("p (g h s) -> p g h s", g=HG, h=GH)
                            link(dve.tensor_scalar(den[:], o[:, :, :, DH], 1e-6, None, ALU.max))
                            link(dve.reciprocal(den[:], den[:]))
                            dve.tensor_tensor(y_tok[:, i % 2, :].rearrange("p (g h d) -> p g h d", g=HG, h=GH), o[:, :, :, 0:DH],
                                              den[:].unsqueeze(3).to_broadcast([128, HG, GH, DH]), ALU.mult).then_inc(S("y"), 1)

                        for step, k in order:
                            if step == "gates":
                                gates()
                            elif step == "rotate":
                                rotate(k)
                            elif step == "weigh":
                                weigh()
                            elif step == "bias":
                                dve.wait_ge(S("biased"), k + 1)
                                add_four(k, DOWN_BANK[k]).then_inc(S("x_added"), 1)
                            elif step == "phi":
                                phi(k)
                            elif step == "turn_k":
                                dve.wait_ge(S("k_turned"), k + 1)
                                dve.tensor_copy(k_tok[:, 4 * k:4 * k + 4, :], PS[:, 5 + k, :].rearrange("p (i d) -> p i d", i=4)).then_inc(S("k_tok"), 1)
                            elif step == "down" and k % 4 == 3:
                                add_expert(k)
                            elif step == "scores":
                                masked(k)
                            elif step == "state":
                                state(k)
                            elif step == "turn_out":
                                normalise(k)
                            elif step == "project_y":
                                dve.wait_ge(S("y_projected"), k + 1)
                                before_adding(step, k)
                                dve.tensor_tensor(x_tok[:, k, :], x_tok[:, k, :], PS[:, 7, 0:D], ALU.add).then_inc(S("x_added"), 1)

                    @block.gpsimd
                    def _(pool):
                        pool.memset(Qs[:].bitcast(U32), 0).then_inc(S("zeroed"), 1)
                        pool.memset(Ks[:].bitcast(U32), 0).then_inc(S("zeroed"), 1)
                        pool.memset(Vst[:, :, :, DH:SLOT], 0.0).then_inc(S("zeroed"), 1)
                        pool.wait_ge(S("zeroed"), 3)
                        pool.memset(Vst[:, :, :, DH:DH + 1], 1.0).then_inc(S("zeroed"), 2)

                    @block.sync
                    def _(sp):
                        def parts_out(r):
                            n, j = ROTS[r]
                            for k in range(3):
                                sp.wait_ge(S("parts"), 3 * r + k + 1)
                                write_part(sp, parts, n, k, slice(512 * j, 512 * j + 512), S(f"parts_out{j}"))

                        for r in range(2):
                            parts_out(r)
                        sp.wait_ge(S("zeroed"), 2)
                        for c in range(T // QT):
                            j = QT * c // 512
                            if c == 1:
                                for r in (2, 3):
                                    parts_out(r)
                            sp.wait_ge(S(f"parts_out{j}"), 16 * 2 * len(Q_PART))
                            if c >= 2:
                                sp.wait_ge(S("a_scores"), HG * QT // 128 * (c - 1))
                            restack(sp, Qs[:, c % 2], 0, 0, H, QT * c, QT, S(f"q_in{c}"))
                            restack(sp, Ks[:, c % 2], 1, 0, H, QT * c, QT, S(f"k_in{c}"))
                        sp.wait_ge(S("x_added"), len(x_adds))
                        sp.dma_start(out_dram[b], x_tok[:]).then_inc(S("out"), 16)
                        sp.wait_ge(S("out"), 16)
            end_phase()


def lay_out(**i):
    import numpy as np
    n = {k: np.asarray(v) for k, v in i.items()}
    rot = (np.arange(D) // DH) * DH + (np.arange(D) % DH + DH // 2) % DH
    a = {"x": n["L0_attn_x"]}
    w = n["L0_attn_W_qkv"]
    q, k, v = w[:, :D], w[:, D:2 * D], w[:, 2 * D:]
    a["w_attn0"] = np.stack([q, q[:, rot], k, k[:, rot], v], axis=1)
    a["w_out0"] = n["L0_attn_W_o"]
    q, k, v = n["L1_attn_Wq"].T, n["L1_attn_Wk"].T, n["L1_attn_Wv"].T
    a["w_attn1"] = np.stack([q, q[:, rot], k, k[:, rot], v], axis=1)
    a["w_out1"] = n["L1_attn_Wo"].T
    a["w_qkv"] = n["L0_ffn_wqkv"].transpose(1, 0, 2)
    a["w_o"] = n["L0_ffn_wo"].reshape(DEPTH, 4, 128, D).transpose(2, 0, 1, 3)
    a["w_up"] = n["L0_ffn_w1"].transpose(1, 0, 2)
    pad = np.zeros((DEPTH, 384, D), n["L0_ffn_w2"].dtype)
    pad[:, :HID] = n["L0_ffn_w2"]
    a["w_down"] = pad.reshape(DEPTH, 3, 128, D).transpose(2, 0, 1, 3)
    pad = np.zeros((DEPTH, 2, 384), n["L0_ffn_b1"].dtype)
    pad[:, :, :HID] = n["L0_ffn_b1"].reshape(DEPTH, 2, HID)
    a["b_up"] = pad.reshape(DEPTH, 2, 3, 128).transpose(3, 0, 1, 2)
    a["b_down"] = n["L0_ffn_b2"]
    a["ln_gb"] = np.stack([n["L0_ffn_ln_g"].T, n["L0_ffn_ln_b"].T], axis=2)
    qs, ks = n["L0_ffn_q_scale"], n["L0_ffn_k_scale"]
    swap = (np.arange(LD) + LD // 2) % LD
    a["scales"] = np.stack([qs, qs[:, swap], ks, ks[:, swap]], axis=1)
    a["w_gate"] = n["L1_ffn_gate_w"].T
    a["b_gate"] = n["L1_ffn_gate_b"]
    a["w_e1"] = n["L1_ffn_w1"].transpose(1, 0, 2)
    a["b_e1"] = n["L1_ffn_b1"].reshape(E, 4, 128).transpose(2, 0, 1)
    a["w_e2"] = n["L1_ffn_w2"].reshape(E, 4, 128, D).transpose(2, 0, 1, 3)
    blk = np.zeros((NT, E, NT, D), n["L1_ffn_b2"].dtype)
    for t in range(NT):
        blk[t, :, t] = n["L1_ffn_b2"]
    a["b_e2"] = blk.reshape(NT * E, NT, D)
    return {k: np.ascontiguousarray(v) for k, v in a.items()}


def kernel(**inputs):
    import numpy as _np
    import concourse.bacc as _bacc
    from concourse import mybir as _mybir
    from concourse.bass_utils import run_bass_kernel_spmd as _run

    nc = _bacc.Bacc("TRN2", target_bir_lowering=False, num_devices=1)
    arrays = {}

    def feed(tag, group):
        aps = {}
        for name, v in group.items():
            arrays[f"{tag}_{name}"] = v
            aps[name] = nc.dram_tensor(f"{tag}_{name}", v.shape, _mybir.dt.from_np(v.dtype), kind="ExternalInput").ap()
        return aps

    a = feed("in", lay_out(**inputs))
    c = feed("const", constant_arrays())
    out = nc.dram_tensor("out_0", (B, T, D), _mybir.dt.float32, kind="ExternalOutput").ap()
    build(nc, a, c, out)
    r = _run(nc, [arrays], core_ids=[0])
    return r.results[0]["out_0"]
```
